# Optimizing a Trainium2 kernel written in Bass

```python
import numpy as np
import jax
import jax.numpy as jnp

def _softmax(x, axis=-1):
    return jax.nn.softmax(x, axis=axis)

def _gelu(x):
    return jax.nn.gelu(x, approximate=True)

def _silu(x):
    return jax.nn.silu(x)

def _sigmoid(x):
    return jax.nn.sigmoid(x)

def _layernorm(x, axis=-1, eps=1e-05):
    m = jnp.mean(x, axis=axis, keepdims=True)
    v = jnp.var(x, axis=axis, keepdims=True)
    return (x - m) / jnp.sqrt(v + eps)

def _scatter_add(tgt, idx, src, axis=0):
    return tgt.at[idx].add(src)

def _segment_sum(src, seg, n):
    return jax.ops.segment_sum(src, seg, n)
kernel_name = 'mk_perceiver_d2_seqx_r4_19147d'

def setup_inputs(seed: int=0):
    np.random.seed(seed)
    _w = jnp.asarray

    def _rec_inputs():
        import jax
        import jax.numpy as jnp
        _rk = jax.random.key(seed)
        x = 0.0003765 + 1 * jax.random.normal(jax.random.fold_in(_rk, 1), (4, 256, 256), jnp.float32)
        _lenS = 256 - jax.random.randint(jax.random.fold_in(_rk, 7), (4,), 0, max(1, 256 // 4) + 1, jnp.int32)
        _lenS2 = 4096 - jax.random.randint(jax.random.fold_in(_rk, 8), (4,), 0, max(1, 4096 // 4) + 1, jnp.int32)
        _ctx_1024P = jax.random.normal(jax.random.fold_in(_rk, 11), (4, 16, 256), jnp.float32)
        _ctx_1024c = jax.random.dirichlet(jax.random.fold_in(_rk, 511), 0.3 * jnp.ones((16,), jnp.float32), (4, 4096))
        _ctx_1024t = jnp.einsum('bsk,bkd->bsd', _ctx_1024c, _ctx_1024P)
        _ctx_1024t = _ctx_1024t * jax.lax.rsqrt(jnp.mean(jnp.square(_ctx_1024t)) + 1e-12) * 0.953939
        ctx_1024 = -0.000292821 + 1.00034 * (_ctx_1024t + 0.3 * jax.random.normal(jax.random.fold_in(_rk, 611), (4, 4096, 256), jnp.float32))
        _validS = jnp.arange(256)[None, :] < _lenS[:, None]
        _validS2 = jnp.arange(4096)[None, :] < _lenS2[:, None]
        _causal = jnp.tril(jnp.ones((256, 256), dtype=bool))
        mask_Bx1xSxS2_if1 = jnp.where(jnp.ones((4, 1, 256, 4096), dtype=bool), 1, 0).astype(jnp.int32)
        return (x, ctx_1024, mask_Bx1xSxS2_if1)
    x, ctx_1024, mask_Bx1xSxS2_if1 = _rec_inputs()

    def _L0_xattn_setup():
        import jax, jax.numpy as jnp
        import numpy as np
        HEADS = 16
        key = jax.random.key(seed)
        ks = jax.random.split(key, 8)
        N, S, E = (2, 512, 256)
        D = E // HEADS
        return {'values': jax.random.normal(ks[0], (N, S, E), jnp.float32), 'keys': jax.random.normal(ks[1], (N, S, E), jnp.float32), 'queries': jax.random.normal(ks[2], (N, S, E), jnp.float32), 'mask': jnp.ones((N, 1, S, S), jnp.int32), 'Wv': jax.random.normal(ks[3], (D, D), jnp.float32) * D ** (-0.5), 'Wk': jax.random.normal(ks[4], (D, D), jnp.float32) * D ** (-0.5), 'Wq': jax.random.normal(ks[5], (D, D), jnp.float32) * D ** (-0.5), 'Wo': jax.random.normal(ks[6], (E, E), jnp.float32) * E ** (-0.5), 'bo': jnp.zeros((E,), jnp.float32)}
    _L0_xattn_all = _L0_xattn_setup()
    _L0_xattn_in = {k: v for k, v in _L0_xattn_all.items() if k in ('Wv', 'Wk', 'Wq', 'Wo', 'bo')}
    del _L0_xattn_all

    def _L0_attn_setup():
        import jax, jax.numpy as jnp
        import numpy as np
        NUM_HEADS = 16
        TOP_K = 64
        key = jax.random.key(seed)
        ks = jax.random.split(key, 9)
        B, S, E = (2, 256, 256)
        x = jax.random.normal(ks[0], (B, S, E), jnp.float32)
        init = lambda k: jax.random.normal(k, (E, E), jnp.float32) * 0.02
        return {'x': x, 'Wq': init(ks[1]), 'bq': jnp.zeros((E,), jnp.float32), 'Wk': init(ks[2]), 'bk': jnp.zeros((E,), jnp.float32), 'Wv': init(ks[3]), 'bv': jnp.zeros((E,), jnp.float32), 'Wo': init(ks[4]), 'bo': jnp.zeros((E,), jnp.float32)}
    _L0_attn_all = _L0_attn_setup()
    _L0_attn_in = {k: v for k, v in _L0_attn_all.items() if k in ('Wq', 'bq', 'Wk', 'bk', 'Wv', 'bv', 'Wo', 'bo')}
    del _L0_attn_all

    def _L0_ffn_setup():
        import jax, jax.numpy as jnp
        import numpy as np
        B, S, D = (4, 512, 256)
        E = 8
        CF = 1
        key = jax.random.key(seed)
        k_x, k_g, k_w, k_b = jax.random.split(key, 4)
        x = jax.random.normal(k_x, (B, S, D), dtype=jnp.float32)
        Wg = jax.random.normal(k_g, (D, E), dtype=jnp.float32) * (1.0 / np.sqrt(D))
        We = jax.random.normal(k_w, (D, D), dtype=jnp.float32) * (1.0 / np.sqrt(D))
        be = jax.random.normal(k_b, (D,), dtype=jnp.float32) * 0.01
        return {'x': x, 'Wg': Wg, 'We': We, 'be': be}
    _L0_ffn_all = _L0_ffn_setup()
    _L0_ffn_in = {k: v for k, v in _L0_ffn_all.items() if k in ('Wg', 'We', 'be')}
    del _L0_ffn_all

    def _L1_xattn_setup():
        import jax, jax.numpy as jnp
        import numpy as np
        INPUT_DIM = 256
        OUTPUT_DIM = 256
        B, LQ, LKV = (4, 512, 512)
        SCALE = float(np.sqrt(INPUT_DIM))
        key = jax.random.key(seed)
        k1, k2, k3, k4, k5 = jax.random.split(key, 5)
        s = 1.0 / np.sqrt(INPUT_DIM)
        return {'x1': jax.random.normal(k1, (B, LQ, INPUT_DIM), dtype=jnp.float32), 'x2': jax.random.normal(k2, (B, LKV, INPUT_DIM), dtype=jnp.float32), 'w_q': jax.random.normal(k3, (OUTPUT_DIM, INPUT_DIM), dtype=jnp.float32) * s, 'w_k': jax.random.normal(k4, (OUTPUT_DIM, INPUT_DIM), dtype=jnp.float32) * s, 'w_v': jax.random.normal(k5, (OUTPUT_DIM, INPUT_DIM), dtype=jnp.float32) * s}
    _L1_xattn_all = _L1_xattn_setup()
    _L1_xattn_in = {k: v for k, v in _L1_xattn_all.items() if k in ('w_q', 'w_k', 'w_v')}
    del _L1_xattn_all

    def _L1_attn_setup():
        import jax, jax.numpy as jnp
        import numpy as np
        D_MODEL = 256
        D_STATE = 16
        D_CONV = 4
        EXPAND = 2
        D_HALF = D_MODEL // 2
        D_INNER = EXPAND * D_HALF
        DT_RANK = (D_HALF + 15) // 16
        EPS = 1e-05

        def _silu(x):
            return x * jax.nn.sigmoid(x)

        def _mamba(x, in_proj_w, conv_w, conv_b, x_proj_w, dt_proj_w, dt_proj_b, A_log, D, out_proj_w):
            B, L, _ = x.shape
            xz = x @ in_proj_w.T
            xc, z = jnp.split(xz, 2, axis=-1)
            xt = jnp.moveaxis(xc, 1, 2)
            xt = jnp.pad(xt, ((0, 0), (0, 0), (D_CONV - 1, 0)))
            xt = jax.lax.conv_general_dilated(xt, conv_w, (1,), 'VALID', dimension_numbers=('NCH', 'OIH', 'NCH'), feature_group_count=D_INNER)
            xc = _silu(jnp.moveaxis(xt, 1, 2) + conv_b)
            x_dbl = xc @ x_proj_w.T
            dt = jax.nn.softplus(x_dbl[..., :DT_RANK] @ dt_proj_w.T + dt_proj_b)
            Bm = x_dbl[..., DT_RANK:DT_RANK + D_STATE]
            Cm = x_dbl[..., DT_RANK + D_STATE:]
            A = -jnp.exp(A_log)

            def step(h, ins):
                dt_t, B_t, C_t, u_t = ins
                dA = jnp.exp(dt_t[..., None] * A)
                h = h * dA + (dt_t * u_t)[..., None] * B_t[:, None, :]
                y = jnp.einsum('bdn,bn->bd', h, C_t)
                return (h, y)
            h0 = jnp.zeros((B, D_INNER, D_STATE), xc.dtype)
            ins = (jnp.moveaxis(dt, 1, 0), jnp.moveaxis(Bm, 1, 0), jnp.moveaxis(Cm, 1, 0), jnp.moveaxis(xc, 1, 0))
            _, ys = jax.lax.scan(step, h0, ins)
            y = jnp.moveaxis(ys, 0, 1) + D * xc
            y = y * _silu(z)
            return y @ out_proj_w.T
        key = jax.random.key(seed)
        ks = iter(jax.random.split(key, 64))

        def rn(shape, s=0.02):
            return jax.random.normal(next(ks), shape, dtype=jnp.float32) * s
        inp = {'x': jax.random.normal(next(ks), (2, 1024, D_MODEL), dtype=jnp.float32), 'norm_w': jnp.ones((D_MODEL,), jnp.float32), 'norm_b': jnp.zeros((D_MODEL,), jnp.float32)}
        for pre in ('fwd', 'bwd'):
            inp[pre + '_in_proj_w'] = rn((2 * D_INNER, D_HALF))
            inp[pre + '_conv_w'] = rn((D_INNER, 1, D_CONV), 0.1)
            inp[pre + '_conv_b'] = jnp.zeros((D_INNER,), jnp.float32)
            inp[pre + '_x_proj_w'] = rn((DT_RANK + 2 * D_STATE, D_INNER))
            inp[pre + '_dt_proj_w'] = rn((D_INNER, DT_RANK), 0.1)
            inp[pre + '_dt_proj_b'] = rn((D_INNER,), 0.1)
            inp[pre + '_A_log'] = jnp.log(jnp.broadcast_to(jnp.arange(1, D_STATE + 1, dtype=jnp.float32), (D_INNER, D_STATE)))
            inp[pre + '_D'] = jnp.ones((D_INNER,), jnp.float32)
            inp[pre + '_out_proj_w'] = rn((D_HALF, D_INNER))
        return inp
    _L1_attn_all = _L1_attn_setup()
    _L1_attn_in = {k: v for k, v in _L1_attn_all.items() if k in ('norm_w', 'norm_b', 'fwd_in_proj_w', 'fwd_conv_w', 'fwd_conv_b', 'fwd_x_proj_w', 'fwd_dt_proj_w', 'fwd_dt_proj_b', 'fwd_A_log', 'fwd_D', 'fwd_out_proj_w', 'bwd_in_proj_w', 'bwd_conv_w', 'bwd_conv_b', 'bwd_x_proj_w', 'bwd_dt_proj_w', 'bwd_dt_proj_b', 'bwd_A_log', 'bwd_D', 'bwd_out_proj_w')}
    del _L1_attn_all

    def _L1_ffn_setup():
        import jax, jax.numpy as jnp
        import numpy as np
        B, S, D, T = (4, 1024, 256, 8)
        key = jax.random.key(seed)
        k1, k2, k3, k4 = jax.random.split(key, 4)
        x = jax.random.normal(k1, (B, S, D), dtype=jnp.float32)
        tile_sigs = jax.random.normal(k2, (T, D), dtype=jnp.float32)
        bound = 1.0 / np.sqrt(D)
        W = jax.random.uniform(k3, (T, D, D), minval=-bound, maxval=bound, dtype=jnp.float32)
        b = jax.random.uniform(k4, (T, D), minval=-bound, maxval=bound, dtype=jnp.float32)
        return {'x': x, 'tile_sigs': tile_sigs, 'W': W, 'b': b}
    _L1_ffn_all = _L1_ffn_setup()
    _L1_ffn_in = {k: v for k, v in _L1_ffn_all.items() if k in ('tile_sigs', 'W', 'b')}
    del _L1_ffn_all
    return {'x': x, 'ctx_1024': ctx_1024, 'mask_Bx1xSxS2_if1': mask_Bx1xSxS2_if1, 'L0_xattn_Wv': _L0_xattn_in['Wv'], 'L0_xattn_Wk': _L0_xattn_in['Wk'], 'L0_xattn_Wq': _L0_xattn_in['Wq'], 'L0_xattn_Wo': _L0_xattn_in['Wo'], 'L0_xattn_bo': _L0_xattn_in['bo'], 'L0_attn_Wq': _L0_attn_in['Wq'], 'L0_attn_bq': _L0_attn_in['bq'], 'L0_attn_Wk': _L0_attn_in['Wk'], 'L0_attn_bk': _L0_attn_in['bk'], 'L0_attn_Wv': _L0_attn_in['Wv'], 'L0_attn_bv': _L0_attn_in['bv'], 'L0_attn_Wo': _L0_attn_in['Wo'], 'L0_attn_bo': _L0_attn_in['bo'], 'L0_ffn_Wg': _L0_ffn_in['Wg'], 'L0_ffn_We': _L0_ffn_in['We'], 'L0_ffn_be': _L0_ffn_in['be'], 'L1_xattn_w_q': _L1_xattn_in['w_q'], 'L1_xattn_w_k': _L1_xattn_in['w_k'], 'L1_xattn_w_v': _L1_xattn_in['w_v'], 'L1_attn_norm_w': _L1_attn_in['norm_w'], 'L1_attn_norm_b': _L1_attn_in['norm_b'], 'L1_attn_fwd_in_proj_w': _L1_attn_in['fwd_in_proj_w'], 'L1_attn_fwd_conv_w': _L1_attn_in['fwd_conv_w'], 'L1_attn_fwd_conv_b': _L1_attn_in['fwd_conv_b'], 'L1_attn_fwd_x_proj_w': _L1_attn_in['fwd_x_proj_w'], 'L1_attn_fwd_dt_proj_w': _L1_attn_in['fwd_dt_proj_w'], 'L1_attn_fwd_dt_proj_b': _L1_attn_in['fwd_dt_proj_b'], 'L1_attn_fwd_A_log': _L1_attn_in['fwd_A_log'], 'L1_attn_fwd_D': _L1_attn_in['fwd_D'], 'L1_attn_fwd_out_proj_w': _L1_attn_in['fwd_out_proj_w'], 'L1_attn_bwd_in_proj_w': _L1_attn_in['bwd_in_proj_w'], 'L1_attn_bwd_conv_w': _L1_attn_in['bwd_conv_w'], 'L1_attn_bwd_conv_b': _L1_attn_in['bwd_conv_b'], 'L1_attn_bwd_x_proj_w': _L1_attn_in['bwd_x_proj_w'], 'L1_attn_bwd_dt_proj_w': _L1_attn_in['bwd_dt_proj_w'], 'L1_attn_bwd_dt_proj_b': _L1_attn_in['bwd_dt_proj_b'], 'L1_attn_bwd_A_log': _L1_attn_in['bwd_A_log'], 'L1_attn_bwd_D': _L1_attn_in['bwd_D'], 'L1_attn_bwd_out_proj_w': _L1_attn_in['bwd_out_proj_w'], 'L1_ffn_tile_sigs': _L1_ffn_in['tile_sigs'], 'L1_ffn_W': _L1_ffn_in['W'], 'L1_ffn_b': _L1_ffn_in['b']}

def reference(x, ctx_1024, mask_Bx1xSxS2_if1, L0_xattn_Wv, L0_xattn_Wk, L0_xattn_Wq, L0_xattn_Wo, L0_xattn_bo, L0_attn_Wq, L0_attn_bq, L0_attn_Wk, L0_attn_bk, L0_attn_Wv, L0_attn_bv, L0_attn_Wo, L0_attn_bo, L0_ffn_Wg, L0_ffn_We, L0_ffn_be, L1_xattn_w_q, L1_xattn_w_k, L1_xattn_w_v, L1_attn_norm_w, L1_attn_norm_b, L1_attn_fwd_in_proj_w, L1_attn_fwd_conv_w, L1_attn_fwd_conv_b, L1_attn_fwd_x_proj_w, L1_attn_fwd_dt_proj_w, L1_attn_fwd_dt_proj_b, L1_attn_fwd_A_log, L1_attn_fwd_D, L1_attn_fwd_out_proj_w, L1_attn_bwd_in_proj_w, L1_attn_bwd_conv_w, L1_attn_bwd_conv_b, L1_attn_bwd_x_proj_w, L1_attn_bwd_dt_proj_w, L1_attn_bwd_dt_proj_b, L1_attn_bwd_A_log, L1_attn_bwd_D, L1_attn_bwd_out_proj_w, L1_ffn_tile_sigs, L1_ffn_W, L1_ffn_b):
    import jax
    import jax.numpy as jnp

    def _L0_xattn_ref(values, keys, queries, mask, Wv, Wk, Wq, Wo, bo):
        import jax, jax.numpy as jnp
        import numpy as np
        HEADS = 16
        N, Sq, E = queries.shape
        H = HEADS
        D = E // H
        v = values.reshape(N, -1, H, D)
        k = keys.reshape(N, -1, H, D)
        q = queries.reshape(N, Sq, H, D)
        v = jnp.einsum('nlhd,od->nlho', v, Wv)
        k = jnp.einsum('nlhd,od->nlho', k, Wk)
        q = jnp.einsum('nqhd,od->nqho', q, Wq)
        energy = jnp.einsum('nqhd,nkhd->nhqk', q, k)
        energy = jnp.where(mask == 0, jnp.float32(-1e+20), energy)
        attn = jax.nn.softmax(energy * (1.0 / E ** 0.5), axis=3)
        out = jnp.einsum('nhqk,nkhd->nqhd', attn, v).reshape(N, Sq, E)
        return out @ Wo.T + bo

    def _L0_attn_ref(x, Wq, bq, Wk, bk, Wv, bv, Wo, bo):
        import jax, jax.numpy as jnp
        import numpy as np
        NUM_HEADS = 16
        TOP_K = 64
        B, S, E = x.shape
        H = NUM_HEADS
        hd = E // H
        scale = jnp.sqrt(jnp.float32(hd))

        def proj(W, b):
            return (x @ W.T + b).reshape(B, S, H, hd).transpose(0, 2, 1, 3)
        q = proj(Wq, bq)
        k = proj(Wk, bk)
        v = proj(Wv, bv)
        scores = jnp.einsum('bhqd,bhkd->bhqk', q, k) / scale
        top_scores, top_idx = jax.lax.top_k(scores, TOP_K)
        vg = jnp.take_along_axis(v[:, :, None, :, :], top_idx[..., None], axis=3)
        w = jax.nn.softmax(top_scores, axis=-1)
        out = jnp.einsum('bhqk,bhqkd->bhqd', w, vg)
        out = out.transpose(0, 2, 1, 3).reshape(B, S, E)
        return out @ Wo.T + bo

    def _L0_ffn_ref(x, Wg, We, be):
        import jax, jax.numpy as jnp
        import numpy as np
        B, S, D = (4, 512, 256)
        E = 8
        CF = 1
        b, s, d = x.shape
        n = b * s
        cap = n // E * CF
        h = x.reshape(n, d)
        router_logits = h @ Wg
        probs = jax.nn.softmax(router_logits, axis=1)
        best = jnp.argmax(probs, axis=1)
        mask = jax.nn.one_hot(best, E, dtype=probs.dtype)
        gate = jnp.sum(probs * mask, axis=1)
        locations = jnp.cumsum(mask, axis=0) - 1.0
        mask = mask * (locations < cap).astype(mask.dtype)
        loc_idx = jnp.sum(locations * mask, axis=1).astype(jnp.int32)
        new_gate = gate[:, None] * mask
        loc_oh = jax.nn.one_hot(loc_idx, cap, dtype=new_gate.dtype)
        combine = new_gate[:, :, None] * loc_oh[:, None, :]
        dispatch = (combine != 0).astype(h.dtype)
        dispatched = jnp.einsum('nec,nd->ecd', dispatch, h).reshape(E * cap, d)
        expert_out = dispatched @ We + be
        out = combine.reshape(n, E * cap) @ expert_out
        return out.reshape(b, s, d)

    def _L1_xattn_ref(x1, x2, w_q, w_k, w_v):
        import jax, jax.numpy as jnp
        import numpy as np
        INPUT_DIM = 256
        OUTPUT_DIM = 256
        B, LQ, LKV = (4, 512, 512)
        SCALE = float(np.sqrt(INPUT_DIM))
        q = jnp.einsum('bsi,oi->bso', x1, w_q)
        k = jnp.einsum('bti,oi->bto', x2, w_k)
        v = jnp.einsum('bti,oi->bto', x2, w_v)
        scores = jnp.einsum('bsd,btd->bst', q, k) / SCALE
        attn = jax.nn.softmax(scores, axis=-1)
        out = jnp.einsum('bst,btd->bsd', attn, v)
        return out

    def _L1_attn_ref(x, norm_w, norm_b, fwd_in_proj_w, fwd_conv_w, fwd_conv_b, fwd_x_proj_w, fwd_dt_proj_w, fwd_dt_proj_b, fwd_A_log, fwd_D, fwd_out_proj_w, bwd_in_proj_w, bwd_conv_w, bwd_conv_b, bwd_x_proj_w, bwd_dt_proj_w, bwd_dt_proj_b, bwd_A_log, bwd_D, bwd_out_proj_w):
        import jax, jax.numpy as jnp
        import numpy as np
        D_MODEL = 256
        D_STATE = 16
        D_CONV = 4
        EXPAND = 2
        D_HALF = D_MODEL // 2
        D_INNER = EXPAND * D_HALF
        DT_RANK = (D_HALF + 15) // 16
        EPS = 1e-05

        def _silu(x):
            return x * jax.nn.sigmoid(x)

        def _mamba(x, in_proj_w, conv_w, conv_b, x_proj_w, dt_proj_w, dt_proj_b, A_log, D, out_proj_w):
            B, L, _ = x.shape
            xz = x @ in_proj_w.T
            xc, z = jnp.split(xz, 2, axis=-1)
            xt = jnp.moveaxis(xc, 1, 2)
            xt = jnp.pad(xt, ((0, 0), (0, 0), (D_CONV - 1, 0)))
            xt = jax.lax.conv_general_dilated(xt, conv_w, (1,), 'VALID', dimension_numbers=('NCH', 'OIH', 'NCH'), feature_group_count=D_INNER)
            xc = _silu(jnp.moveaxis(xt, 1, 2) + conv_b)
            x_dbl = xc @ x_proj_w.T
            dt = jax.nn.softplus(x_dbl[..., :DT_RANK] @ dt_proj_w.T + dt_proj_b)
            Bm = x_dbl[..., DT_RANK:DT_RANK + D_STATE]
            Cm = x_dbl[..., DT_RANK + D_STATE:]
            A = -jnp.exp(A_log)

            def step(h, ins):
                dt_t, B_t, C_t, u_t = ins
                dA = jnp.exp(dt_t[..., None] * A)
                h = h * dA + (dt_t * u_t)[..., None] * B_t[:, None, :]
                y = jnp.einsum('bdn,bn->bd', h, C_t)
                return (h, y)
            h0 = jnp.zeros((B, D_INNER, D_STATE), xc.dtype)
            ins = (jnp.moveaxis(dt, 1, 0), jnp.moveaxis(Bm, 1, 0), jnp.moveaxis(Cm, 1, 0), jnp.moveaxis(xc, 1, 0))
            _, ys = jax.lax.scan(step, h0, ins)
            y = jnp.moveaxis(ys, 0, 1) + D * xc
            y = y * _silu(z)
            return y @ out_proj_w.T
        residual = x
        mu = x.mean(-1, keepdims=True)
        var = ((x - mu) ** 2).mean(-1, keepdims=True)
        xn = (x - mu) * jax.lax.rsqrt(var + EPS) * norm_w + norm_b
        x_fwd, x_bwd = jnp.split(xn, 2, axis=-1)
        out_fwd = _mamba(x_fwd, fwd_in_proj_w, fwd_conv_w, fwd_conv_b, fwd_x_proj_w, fwd_dt_proj_w, fwd_dt_proj_b, fwd_A_log, fwd_D, fwd_out_proj_w)
        out_bwd = _mamba(x_bwd[:, ::-1, :], bwd_in_proj_w, bwd_conv_w, bwd_conv_b, bwd_x_proj_w, bwd_dt_proj_w, bwd_dt_proj_b, bwd_A_log, bwd_D, bwd_out_proj_w)[:, ::-1, :]
        return jnp.concatenate([out_fwd, out_bwd], axis=-1) + residual

    def _L1_ffn_ref(x, tile_sigs, W, b):
        import jax, jax.numpy as jnp
        import numpy as np
        B, S, D, T = (4, 1024, 256, 8)
        scores = jnp.einsum('bsd,td->bst', x, jnp.sign(tile_sigs))
        idx = jnp.argmax(scores, axis=-1)
        all_out = jnp.einsum('bsd,tde->bste', x, W) + b[None, None]
        out = jnp.take_along_axis(all_out, idx[:, :, None, None], axis=2)
        return out[:, :, 0, :]
    x = x + _L0_xattn_ref(ctx_1024, ctx_1024, _layernorm(x, axis=-1), mask_Bx1xSxS2_if1, L0_xattn_Wv, L0_xattn_Wk, L0_xattn_Wq, L0_xattn_Wo, L0_xattn_bo)
    x = x + _L0_attn_ref(_layernorm(x, axis=-1), L0_attn_Wq, L0_attn_bq, L0_attn_Wk, L0_attn_bk, L0_attn_Wv, L0_attn_bv, L0_attn_Wo, L0_attn_bo)
    x = x + _L0_ffn_ref(_layernorm(x, axis=-1), L0_ffn_Wg, L0_ffn_We, L0_ffn_be)
    x = x + _L1_xattn_ref(_layernorm(x, axis=-1), ctx_1024, L1_xattn_w_q, L1_xattn_w_k, L1_xattn_w_v)
    x = x + _L1_attn_ref(_layernorm(x, axis=-1), L1_attn_norm_w, L1_attn_norm_b, L1_attn_fwd_in_proj_w, L1_attn_fwd_conv_w, L1_attn_fwd_conv_b, L1_attn_fwd_x_proj_w, L1_attn_fwd_dt_proj_w, L1_attn_fwd_dt_proj_b, L1_attn_fwd_A_log, L1_attn_fwd_D, L1_attn_fwd_out_proj_w, L1_attn_bwd_in_proj_w, L1_attn_bwd_conv_w, L1_attn_bwd_conv_b, L1_attn_bwd_x_proj_w, L1_attn_bwd_dt_proj_w, L1_attn_bwd_dt_proj_b, L1_attn_bwd_A_log, L1_attn_bwd_D, L1_attn_bwd_out_proj_w)
    x = x + _L1_ffn_ref(_layernorm(x, axis=-1), L1_ffn_tile_sigs, L1_ffn_W, L1_ffn_b)
    return x

_drawn_inputs = setup_inputs


def setup_inputs(seed=0):
    import zlib

    import numpy as np

    out = dict(_drawn_inputs(seed))
    spreads = {'L0_xattn_bo': (0.0, 0.1),
     'L0_attn_bq': (0.0, 0.1),
     'L0_attn_bk': (0.0, 0.1),
     'L0_attn_bv': (0.0, 0.1),
     'L0_attn_bo': (0.0, 0.1),
     'L1_attn_norm_w': (1.0, 0.2),
     'L1_attn_norm_b': (0.0, 0.1),
     'L1_attn_fwd_conv_b': (0.0, 0.1),
     'L1_attn_fwd_D': (1.0, 0.2),
     'L1_attn_bwd_conv_b': (0.0, 0.1),
     'L1_attn_bwd_D': (1.0, 0.2)}
    factors = {}
    for name, (base, spread) in spreads.items():
        noise = np.random.default_rng([zlib.crc32(name.encode()), seed]).standard_normal(out[name].shape)
        drawn = base * np.exp(spread * noise) if base else spread * noise
        out[name] = jnp.asarray(drawn.astype(out[name].dtype))
    for name, factor in factors.items():
        out[name] = (out[name] * factor).astype(out[name].dtype)
    return out
```

```python
from contextlib import ExitStack

import concourse.bass as bass
from concourse import mybir

ALU = mybir.AluOpType
ACT = mybir.ActivationFunctionType
AX = mybir.AxisListType
F32 = mybir.dt.float32
BF16 = mybir.dt.bfloat16
I32 = mybir.dt.int32
U32 = mybir.dt.uint32

P = 128
B, S, E, SK = 4, 256, 256, 4096
H, D = 16, 16
T = S // P
ROWS = B * T
C = E // P
KT = SK // P
HG = 4
GC = H // HG // C
RING = 3
PARTS = [0, 0, 0, 1, 1, 2]
QPARTS = [0, 1, 2, 0, 1, 0]
NB = len(PARTS)
KR = NB * D
NEG = -1.0e20
LOW = -3.0e38
EPS = 1e-5
TOPK = 64
EX = 8
CAP = 4 * 256 // EX
VP = D + 1


class Chain:

    def __init__(self, eng, sem):
        self.eng, self.sem, self.n = eng, sem, 0

    def hold(self):
        self.n += 1
        self.eng.sem_inc(self.sem, 1)

    def restart(self):
        self.hold()
        self.eng.sem_clear(self.sem)
        self.n = 0

    def __call__(self, ins):
        self.n += 1
        ins.then_inc(self.sem, 1)
        self.eng.wait_ge(self.sem, self.n)


def row_tile(X, t):
    return X[:, bass.ds(t, 1), :].rearrange("p a d -> p (a d)")


def scope(nc, stage):
    ctx = ExitStack()
    sems = []

    def clear():
        nc.clear_and_free_semaphores(sems)
        nc.all_engine_barrier()

    ctx.callback(clear)
    sb = lambda name, shape, dt=F32: ctx.enter_context(nc.sbuf_tensor(f"{stage}_{name}", shape, dt))

    def sem(name):
        sems.append(nc.alloc_semaphore(f"{stage}_{name}"))
        return sems[-1]

    return ctx, sb, sem


def prepare(nc, a, X, ps, ident, identb, W2, qscratch):
    ctx, sb, sem = scope(nc, "prepare")
    with ctx:
        w16 = sb("w16", [D, 2, D])
        m16 = sb("m16", [D, D])
        Mbd = sb("Mbd", [P, P])
        Vbd = sb("Vbd", [P, P])
        woT = sb("woT", [P, C, E])
        bo = sb("bo", [P, E])
        stats = sb("stats", [P, 6])
        mv = sb("mv", [P, 2])
        ve = sb("ve", [P, 1])
        rstd = sb("rstd", [P, 1])
        mhalf = sb("mhalf", [P, 1])
        xn = sb("xn", [P, E])
        xnT = sb("xnT", [P, C, P])
        qrest = sb("qrest", [P, C, P])
        qparts = sb("qparts", [P, 3, C, ROWS, P], BF16)

        x_loaded, w_loaded, zeroed = sem("x_loaded"), sem("w_loaded"), sem("zeroed")
        m_made, m_copied, m_placed = sem("m_made"), sem("m_copied"), sem("m_placed")
        v_placed, w2_made, ident_ready = sem("v_placed"), sem("w2_made"), sem("ident_ready")
        var_ready, rstd_ready, xn_ready = sem("var_ready"), sem("rstd_ready"), sem("xn_ready")
        xn_turned, xnT_ready, q_ready, q_split = sem("xn_turned"), sem("xnT_ready"), sem("q_ready"), sem("q_split")
        q_stored, dve_step, pool_step = sem("q_stored"), sem("dve_step"), sem("pool_step")
        w2_copied, bo_added = sem("w2_copied"), sem("bo_added")

        block = ctx.enter_context(nc.Block())

        @block.sync
        def _(sp):
            sp.dma_start(X[:], a["x"].rearrange("b s d -> (b s) d").rearrange("(r p) d -> p r d", p=P)).then_inc(x_loaded, 16)
            sp.dma_start(w16[:, 0, :], a["wq0"]).then_inc(w_loaded, 16)
            sp.dma_start(w16[:, 1, :], a["wk0"]).then_inc(w_loaded, 16)
            sp.dma_start(woT[:], a["wo0T"].rearrange("(c p) n -> p c n", p=P)).then_inc(w_loaded, 16)
            sp.dma_start(bo[:], a["bo0"].partition_broadcast(P)).then_inc(w_loaded, 16)
            sp.wait_ge(zeroed, 2)
            for h in range(P // D):
                sp.dma_start(Vbd[h * D:(h + 1) * D, h * D:(h + 1) * D], a["wv0"]).then_inc(v_placed, 16)
            sp.wait_ge(m_copied, 1)
            for h in range(P // D):
                sp.dma_start(Mbd[h * D:(h + 1) * D, h * D:(h + 1) * D], m16[:]).then_inc(m_placed, 16)
            sp.wait_ge(q_split, ROWS)
            for n, part in enumerate(QPARTS):
                for c in range(C):
                    sp.dma_start(qscratch[n, :, c].rearrange("b p q -> p b q"),
                                 qparts[:, part, c].rearrange("p (b t) q -> p b (t q)", t=T)).then_inc(q_stored, 16)
            sp.wait_ge(q_stored, 16 * NB * C)

        @block.gpsimd
        def _(pool):
            pool.memset(Mbd[:], 0.0).then_inc(zeroed, 1)
            pool.memset(Vbd[:], 0.0).then_inc(zeroed, 1)
            pool.memset(ident[:], 0.0).then_inc(pool_step, 1)
            pool.memset(identb[:], 0.0).then_inc(pool_step, 1)
            pool.memset(mhalf[:], -0.5).then_inc(pool_step, 1)
            pool.wait_ge(pool_step, 3)
            for t in (ident, identb):
                pool.affine_select(out=t[:], in_=t[:], compare_op=ALU.not_equal, fill=1.0, base=0,
                                   pattern=[[-1, P]], channel_multiplier=1).then_inc(ident_ready, 1)
            with pool.Fori(0, ROWS) as t:
                pool.wait_ge(var_ready, t + 1)
                pool.tensor_tensor(rstd[:], ve[:], mhalf[:], ALU.pow).then_inc(rstd_ready, 1)

        @block.scalar
        def _(act):
            with act.Fori(0, ROWS) as t:
                act.wait_ge(xn_turned, t + 1)
                act.copy(xnT[:], ps[:, 0, 0:C * P].rearrange("p (c q) -> p c q", c=C)).then_inc(xnT_ready, 1)

        @block.tensor
        def _(pe):
            pe.wait_ge(w_loaded, 64)
            pe.matmul(ps[0:D, 2, 0:D], w16[:, 0, :], w16[:, 1, :], start=True, stop=True).then_inc(m_made, 1)
            pe.wait_ge(v_placed, 16 * (P // D))
            for c in range(C):
                pe.matmul(ps[:, 3, c * E:(c + 1) * E], Vbd[:], woT[:, c, :], start=True, stop=True).then_inc(w2_made, 1)
            pe.wait_ge(ident_ready, 2)
            pe.wait_ge(m_placed, 16 * (P // D))
            with pe.Fori(0, ROWS) as t:
                pe.wait_ge(xn_ready, t + 1)
                for c in range(C):
                    mm = pe.transpose(ps[:, 0, c * P:(c + 1) * P], xn[:, c * P:(c + 1) * P], ident[:])
                mm.then_inc(xn_turned, 1)
                pe.wait_ge(xnT_ready, t + 1)
                for c in range(C):
                    mm = pe.matmul(ps[:, 1, c * P:(c + 1) * P], Mbd[:], xnT[:, c, :], start=True, stop=True)
                mm.then_inc(q_ready, 1)

        @block.vector
        def _(dve):
            step = Chain(dve, dve_step)
            dve.wait_ge(m_made, 1)
            dve.tensor_copy(m16[:], ps[0:D, 2, 0:D]).then_inc(m_copied, 1)
            dve.wait_ge(w2_made, C)
            dve.tensor_copy(W2[:], ps[:, 3, :].rearrange("p (c n) -> p c n", c=C)).then_inc(w2_copied, 1)
            dve.wait_ge(x_loaded, 16)
            with dve.Fori(0, ROWS) as t:
                step.restart()
                x_t = row_tile(X, t)
                step(dve.bn_stats(stats[:], x_t))
                step(dve.bn_aggr(mv[:], stats[:]))
                dve.tensor_scalar(ve[:], mv[:, 1:2], EPS, None, ALU.add).then_inc(var_ready, 1)
                dve.wait_ge(rstd_ready, t + 1)
                dve.tensor_scalar(xn[:], x_t, mv[:, 0:1], rstd[:], ALU.subtract, ALU.mult).then_inc(xn_ready, 1)
                dve.wait_ge(q_ready, t + 1)
                q = ps[:, 1, 0:C * P].rearrange("p (c q) -> p c q", c=C)
                part = lambda i: qparts[:, i, :, bass.ds(t, 1), :].rearrange("p c a q -> p c (a q)")
                step(dve.tensor_copy(part(0), q))
                step(dve.tensor_tensor(qrest[:], q, part(0), ALU.subtract))
                step(dve.tensor_copy(part(1), qrest[:]))
                dve.tensor_tensor(part(2), qrest[:], part(1), ALU.subtract).then_inc(q_split, 1)
            step.restart()
            for t in range(ROWS):
                dve.tensor_tensor(X[:, t, :], X[:, t, :], bo[:], ALU.add).then_inc(bo_added, 1)
            dve.wait_ge(bo_added, ROWS)
            dve.wait_ge(w2_copied, 1)


def cross_attention(nc, a, X, ps, ident, identb, W2, qscratch):
    ctx, sb, sem = scope(nc, "cross")
    with ctx:
        stage = sb("stage", [P, SK])
        kparts = sb("kparts", [P, 3, SK], BF16)
        kstack = [sb(f"kstack{i}", [P, HG, SK], BF16) for i in range(2)]
        qstack = [sb(f"qstack{i}", [P, HG, S], BF16) for i in range(2)]
        maskb = sb("maskb", [P, T, SK], BF16)
        vstage = sb("vstage", [P, KT, HG, D])
        values = [sb(f"values{i}", [P, KT, HG * VP + 32 - VP]) for i in range(2)]
        probs = [sb(f"probs{i}", [P, HG, S]) for i in range(RING)]
        maxima = sb("maxima", [P, HG * T, 4])
        shift = sb("shift", [P, HG * T])
        rest = sb("rest", [P, 2, HG * T])
        shiftp = sb("shiftp", [P, HG * T, 3], BF16)
        accT = sb("accT", [P, S])
        recip = sb("recip", [P, T, HG])
        heads = sb("heads", [P, T, P])
        headsT = sb("headsT", [P, S])

        stage_loaded, stage_free = sem("stage_loaded"), sem("stage_free")
        kparts_ready, kparts_free = sem("kparts_ready"), sem("kparts_free")
        stack_loaded, stack_free = [sem(f"stack_loaded{g}") for g in range(GC)], sem("stack_free")
        v_loaded, v_free, values_ready = sem("v_loaded"), sem("v_free"), sem("values_ready")
        natural_ready, natural_reduced = sem("natural_ready"), sem("natural_reduced")
        shift_ready, shift_turned, shift_placed = sem("shift_ready"), sem("shift_turned"), sem("shift_placed")
        scores_ready, exp_done, pv_done = sem("scores_ready"), sem("exp_done"), sem("pv_done")
        acc_copied, acc_turned, heads_ready = sem("acc_copied"), sem("acc_turned"), sem("heads_ready")
        heads_turned, headsT_ready, proj_ready, x_added = (
            sem("heads_turned"), sem("headsT_ready"), sem("proj_ready"), sem("x_added"))
        passed = sem("passed")
        dve_step, mask_ready, ones_ready = sem("dve_step"), sem("mask_ready"), sem("ones_ready")

        slot = lambda i: ps[:, 2 * (i % RING):2 * (i % RING) + 2, :]
        acc = lambda g: ps[:, 6, g * S:(g + 1) * S]
        PER = HG * NB + NB
        NAT = HG * T * 4

        block = ctx.enter_context(nc.Block())

        @block.sync
        def _(sp):
            with sp.Fori(0, B) as b:
                for t in range(T):
                    sp.wait_ge(stage_free, b * 4 + t + 1)
                    sp.dma_start(stage[:].bitcast(I32), a["mask"][bass.ds(b, 1), t * P:(t + 1) * P, :]
                                 .rearrange("a p k -> p (a k)")).then_inc(stage_loaded, 16)
                with sp.Fori(0, C) as c:
                    i = b * C + c
                    sp.wait_ge(stage_free, b * 4 + c + 3)
                    sp.dma_start(stage[:], a["ctxT"][bass.ds(i, 1)].rearrange("a p k -> p (a k)")).then_inc(stage_loaded, 16)
                    sp.wait_ge(kparts_ready, i + 1)
                    for g in range(GC):
                        sp.wait_ge(stack_free, i * GC + g + 1)
                        for j in range(HG):
                            r = (g * HG + j) * D
                            for n, part in enumerate(PARTS):
                                sp.dma_start(kstack[g][n * D:(n + 1) * D, j, :], kparts[r:r + D, part, :]).then_inc(stack_loaded[g], 16)
                        for n in range(NB):
                            src = qscratch[n, bass.ds(b, 1), bass.ds(c, 1), g * HG * D:(g + 1) * HG * D, :]
                            sp.dma_start(qstack[g][n * D:(n + 1) * D, :, :],
                                         src.rearrange("a c (j d) q -> (a c j) d q", d=D).rearrange("j d q -> d j q")).then_inc(stack_loaded[g], 16)

        @block.gpsimd
        def _(pool):
            with pool.Fori(0, B * C) as i:
                for g in range(GC):
                    n = i * GC + g
                    pool.wait_ge(v_free, n + 1)
                    pool.dma_start(vstage[:], a["ctxV"][bass.ds(n, 1)].rearrange("a p (k j d) -> p (a k) j d", j=HG, d=D)).then_inc(v_loaded, 16)

        @block.scalar
        def _(act):
            act.sem_inc(exp_done, RING)
            with act.Fori(0, B * C) as i:
                for g in range(GC):
                    n = i * GC + g
                    act.wait_ge(shift_turned, n + 1)
                    act.copy(qstack[g][KR:KR + 3, :, :], ps[:].bitcast(BF16)[KR:KR + 3, 7, :]
                             .rearrange("p (j q) -> p j q", j=HG)).then_inc(shift_placed, 1)
                    for k in range(KT):
                        act.wait_ge(scores_ready, n * KT + k + 1)
                        act.wait_ge(pv_done, n * KT + max(k + 1, RING))
                        act.activation(probs[k % RING][:], slot(k).rearrange("p a (h q) -> p (a h) q", h=2), ACT.Exp,
                                       scale=1.0 / 16.0).then_inc(exp_done, 1)
                    if g == GC - 1:
                        act.wait_ge(heads_turned, i + 1)
                        act.copy(headsT[:], ps[:, 7, 0:S]).then_inc(headsT_ready, 1)

        @block.tensor
        def _(pe):
            pe.sem_inc(pv_done, RING)
            pe.sem_inc(kparts_free, 1)
            pe.sem_inc(stack_free, 2)
            pe.wait_ge(ones_ready, 2)
            with pe.Fori(0, B) as b:
                pe.wait_ge(mask_ready, T * b + T)
                pe.sem_inc(passed, 1)
                with pe.Fori(0, C) as c:
                    i = b * C + c
                    for g in range(GC):
                        n = i * GC + g
                        ks, qs = kstack[g], qstack[g]
                        pe.wait_ge(stack_loaded[g], (i + 1) * (16 * PER))
                        if g == GC - 1:
                            pe.sem_inc(kparts_free, 1)
                        for u in range(NAT):
                            j, t, part = u // (4 * T), u // 4 % T, u % 4
                            if u < RING:
                                pe.wait_ge(exp_done, n * KT + [RING - 1, RING, RING - 2][u])
                            else:
                                pe.wait_ge(natural_reduced, n * NAT + u - RING + 1)
                            for w in range(2):
                                k0 = part * 1024 + w * 512
                                out = slot(u)[:, w, :]
                                pe.matmul(out, qs[0:KR, j, t * P:(t + 1) * P], ks[0:KR, j, k0:k0 + 512], start=True, stop=False)
                                mm = pe.matmul(out, identb[:], maskb[:, t, k0:k0 + 512], start=False, stop=True)
                            mm.then_inc(natural_ready, 1)
                        pe.wait_ge(shift_ready, n + 1)
                        pe.wait_ge(heads_ready, n + 1)
                        pe.wait_ge(x_added, i + 1)
                        for u in range(HG * T):
                            mm = pe.transpose(ps[:].bitcast(BF16)[KR:KR + 3, 7, u * P:(u + 1) * P], shiftp[:, u, :], identb[:])
                        mm.then_inc(shift_turned, 1)
                        pe.wait_ge(shift_placed, n + 1)
                        pe.wait_ge(natural_reduced, (n + 1) * NAT)
                        for k in range(KT + 2):
                            if k < KT:
                                if k >= RING:
                                    pe.wait_ge(exp_done, n * KT + k + 1)
                                for j in range(HG):
                                    pe.matmul(slot(k)[:, j // 2, (j % 2) * S:(j % 2 + 1) * S], ks[0:KR + 3, j, k * P:(k + 1) * P],
                                              qs[0:KR + 3, j, :], start=(j % 2 == 0), stop=False, skip_group_check=True)
                                for w in range(2):
                                    for t in range(T):
                                        mm = pe.matmul(slot(k)[:, w, :].rearrange("p (h t q) -> p h t q", h=2, t=T)[:, :, t, :],
                                                       maskb[:, t, k * P:(k + 1) * P],
                                                       identb[:].unsqueeze(1).to_broadcast([P, 2, P]), start=False,
                                                       stop=(t == T - 1), skip_group_check=True)
                                mm.then_inc(scores_ready, 1)
                            if k >= 2:
                                kk = k - 2
                                if kk == 0:
                                    pe.wait_ge(values_ready, n + 1)
                                pe.wait_ge(exp_done, n * KT + RING + kk + 1)
                                for j in range(HG):
                                    mm = pe.matmul(acc(g)[32 * j:32 * j + 32, :], values[g][:, kk, j * VP:j * VP + 32], probs[kk % RING][:, j, :],
                                                   start=(kk == 0), stop=(kk == KT - 1), skip_group_check=True)
                                mm.then_inc(pv_done, 1)
                        pe.wait_ge(acc_copied, n + 1)
                        pe.sem_inc(stack_free, 1)
                        for t in range(T):
                            mm = pe.transpose(ps[:, 7, t * P:(t + 1) * P], accT[:, t * P:(t + 1) * P], ident[:])
                        mm.then_inc(acc_turned, 1)
                    pe.wait_ge(heads_ready, i * GC + GC + 1)
                    for t in range(T):
                        mm = pe.transpose(ps[:, 7, t * P:(t + 1) * P], heads[:, t, :], ident[:])
                    mm.then_inc(heads_turned, 1)
                    pe.wait_ge(headsT_ready, i + 1)
                    for t in range(T):
                        mm = pe.matmul(ps[:, 7, t * E:(t + 1) * E], headsT[:, t * P:(t + 1) * P],
                                       W2[:, bass.ds(c, 1), :].rearrange("p a n -> p (a n)"), start=True, stop=True)
                    mm.then_inc(proj_ready, 1)

        @block.vector
        def _(dve):
            step = Chain(dve, dve_step)
            for i in range(2):
                dve.memset(values[i][:], 1.0).then_inc(dve_step, 1)
                dve.memset(kstack[i][96:128, :, :], 1.0).then_inc(ones_ready, 1)
            dve.wait_ge(dve_step, 2)
            dve.sem_inc(stage_free, 1)
            dve.sem_inc(v_free, 1)
            dve.sem_inc(heads_ready, 1)
            dve.sem_inc(x_added, 1)
            with dve.Fori(0, B) as b:
                for t in range(T):
                    dve.wait_ge(stage_loaded, b * 64 + (t + 1) * 16)
                    dve.tensor_scalar(maskb[:, t, :], stage[:].bitcast(I32), 0.0, NEG, ALU.is_equal, ALU.mult).then_inc(mask_ready, 1)
                    dve.wait_ge(mask_ready, T * b + t + 1)
                    dve.sem_inc(stage_free, 1)
                with dve.Fori(0, C) as c:
                    i = b * C + c
                    step.restart()
                    dve.wait_ge(stage_loaded, b * 64 + c * 16 + 48)
                    dve.wait_ge(kparts_free, i + 1)
                    step(dve.tensor_copy(kparts[:, 0, :], stage[:]))
                    step(dve.tensor_tensor(stage[:], stage[:], kparts[:, 0, :], ALU.subtract))
                    step(dve.tensor_copy(kparts[:, 1, :], stage[:]))
                    step(dve.tensor_tensor(kparts[:, 2, :], stage[:], kparts[:, 1, :], ALU.subtract))
                    dve.sem_inc(kparts_ready, 1)
                    dve.sem_inc(stage_free, 1)
                    for g in range(GC):
                        n = i * GC + g
                        dve.wait_ge(v_loaded, (n + 1) * 16)
                        step(dve.tensor_copy(values[g][:, :, 0:HG * VP].rearrange("p k (j v) -> p k j v", v=VP)[:, :, :, 0:D], vstage[:]))
                        dve.sem_inc(v_free, 1)
                        dve.sem_inc(values_ready, 1)
                        for u in range(NAT):
                            dve.wait_ge(natural_ready, n * NAT + u + 1)
                            dve.reduce_max(maxima[:, u // 4, u % 4:u % 4 + 1], slot(u), AX.XY).then_inc(natural_reduced, 1)
                        dve.wait_ge(natural_reduced, (n + 1) * NAT)
                        step(dve.reduce_max(shift[:], maxima[:], AX.X))
                        step(dve.tensor_scalar(rest[:, 0, :], shift[:], -1.0, None, ALU.mult))
                        step(dve.tensor_copy(shiftp[:, :, 0], rest[:, 0, :]))
                        step(dve.tensor_tensor(rest[:, 1, :], rest[:, 0, :], shiftp[:, :, 0], ALU.subtract))
                        step(dve.tensor_copy(shiftp[:, :, 1], rest[:, 1, :]))
                        dve.tensor_tensor(shiftp[:, :, 2], rest[:, 1, :], shiftp[:, :, 1], ALU.subtract).then_inc(shift_ready, 1)
                        dve.wait_ge(pv_done, (n + 1) * KT + RING)
                        dve.tensor_copy(accT[:], acc(g)).then_inc(acc_copied, 1)
                        dve.wait_ge(acc_turned, n + 1)
                        turned = ps[:, 7, 0:S].rearrange("p (t j v) -> p t j v", t=T, j=HG)
                        step(dve.reciprocal(recip[:], turned[:, :, :, D]))
                        dve.tensor_tensor(heads[:, :, g * HG * D:(g + 1) * HG * D].rearrange("p t (j d) -> p t j d", d=D), turned[:, :, :, 0:D],
                                          recip[:].unsqueeze(3).to_broadcast([P, T, HG, D]), ALU.mult).then_inc(heads_ready, 1)
                    dve.wait_ge(proj_ready, i + 1)
                    for t in range(T):
                        x_t = row_tile(X, b * T + t)
                        ins = dve.tensor_tensor(x_t, x_t, ps[:, 7, t * E:(t + 1) * E], ALU.add)
                        if t < T - 1:
                            step(ins)
                    ins.then_inc(x_added, 1)
            dve.wait_ge(x_added, B * C + 1)


def self_attention(nc, a, X, ps, ident):
    ctx, sb, sem = scope(nc, "self")
    with ctx:
        wqT = sb("wqT", [P, C, HG, HG, 32])
        wkT = sb("wkT", [P, C, HG, HG, 32])
        wvT = sb("wvT", [P, C, E])
        woT = sb("woT", [P, C, E])
        bq = sb("bq", [P, HG])
        bk = sb("bk", [P, HG])
        bv = sb("bv", [P, E])
        bo = sb("bo", [P, E])
        stats = sb("stats", [P, T, 6])
        mv = sb("mv", [P, T, 2])
        ve = sb("ve", [P, T])
        rstd = sb("rstd", [P, T])
        mhalf = sb("mhalf", [P, T])
        xn = sb("xn", [P, T, E])
        xnT = sb("xnT", [P, C, S])
        qT = sb("qT", [P, HG, S])
        kT = sb("kT", [P, HG, S])
        v = sb("v", [P, T, H, VP])
        qg = sb("qg", [P, S])
        kg = sb("kg", [P, HG, S])
        s = sb("s", [P, 2, 2, S])
        top = sb("top", [P, 2, TOPK // 8, 8])
        work = sb("work", [P, 2, S])
        nmax = sb("nmax", [P, 2])
        e = sb("e", [P, 2, S])
        pm = sb("pm", [P, 2, S])
        pT = sb("pT", [P, 2, T, P])
        recip = sb("recip", [P, T, HG])
        ao = sb("ao", [P, T, E])
        aoT = sb("aoT", [P, C, S])

        w_loaded, w_zeroed, mhalf_ready = sem("w_loaded"), sem("w_zeroed"), sem("mhalf_ready")
        var_ready, rstd_ready, xn_ready = sem("var_ready"), sem("rstd_ready"), sem("xn_ready")
        xn_turned, xnT_ready = sem("xn_turned"), sem("xnT_ready")
        qk_made, qk_copied, v_made, v_ready = sem("qk_made"), sem("qk_copied"), sem("v_made"), sem("v_ready")
        kg_ready, scores_made, first_max, scores_read = sem("kg_ready"), sem("scores_made"), sem("first_max"), sem("scores_read")
        scores_copied = sem("scores_copied")
        nmax_ready, e_ready, pm_ready, pm_turned = sem("nmax_ready"), sem("e_ready"), sem("pm_ready"), sem("pm_turned")
        pT_ready, pv_done, heads_ready = sem("pT_ready"), sem("pv_done"), sem("heads_ready")
        ao_turned, aoT_ready, proj_ready, x_added = sem("ao_turned"), sem("aoT_ready"), sem("proj_ready"), sem("x_added")
        dve_step, pool_step = sem("dve_step"), sem("pool_step")
        passed, passed2 = sem("passed"), sem("passed2")

        NG = H // HG
        UNITS = HG * T
        pair, turn, wide = ps[:, 0, :], ps[:, 1, :], ps[:, 2, :]
        sums = wide[:, 0:T * HG * VP].rearrange("p (t j v) -> p t j v", t=T, j=HG)
        unit = lambda u: (2 * (u // 4) + u % 2, u // 2 % 2)

        block = ctx.enter_context(nc.Block())

        @block.sync
        def _(sp):
            sp.wait_ge(w_zeroed, 4)
            for w, name in ((wqT, "wq1T"), (wkT, "wk1T")):
                for c in range(C):
                    sp.dma_start(w[:, c, :, :, 0:D].rearrange("p g j d -> p (g j) d"),
                                 a[name][c * P:(c + 1) * P, :].rearrange("p (h d) -> p h d", d=D)).then_inc(w_loaded, 16)
            for w, name in ((wvT, "wv1T"), (woT, "wo1T")):
                sp.dma_start(w[:], a[name].rearrange("(c p) n -> p c n", p=P)).then_inc(w_loaded, 16)
            for w, name in ((bv, "bv1"), (bo, "bo1")):
                sp.dma_start(w[:], a[name].partition_broadcast(P)).then_inc(w_loaded, 16)
            for w, name in ((bq, "bq1"), (bk, "bk1")):
                for j in range(HG):
                    sp.dma_start(w[32 * j:32 * j + D, :], a[name][j]).then_inc(w_loaded, 16)

        @block.gpsimd
        def _(pool):
            pool.memset(mhalf[:], -0.5).then_inc(mhalf_ready, 1)
            for w in (wqT, wkT, bq, bk):
                pool.memset(w[:], 0.0).then_inc(w_zeroed, 1)
            pool.memset(kg[:], 0.0).then_inc(mhalf_ready, 1)
            step = Chain(pool, pool_step)
            pool.wait_ge(mhalf_ready, 2)
            with pool.Fori(0, B) as b:
                pool.wait_ge(var_ready, b + 1)
                pool.tensor_tensor(rstd[:], ve[:], mhalf[:], ALU.pow).then_inc(rstd_ready, 1)
                pool.wait_ge(qk_copied, 2 * NG * (b + 1))
                pool.sem_inc(passed2, 1)
                with pool.Fori(0, NG) as g:
                    n = b * NG + g
                    pool.wait_ge(scores_made, n * HG + 1)
                    step.restart()
                    step(pool.tensor_copy(qg[:], row_tile(qT, g)))
                    for j in range(HG):
                        rows = slice(32 * j, 32 * j + 32)
                        step(pool.tensor_copy(kg[rows, j, :], kT[rows, bass.ds(g, 1), :].rearrange("p a q -> p (a q)")))
                    pool.sem_inc(kg_ready, 1)

        @block.scalar
        def _(act):
            act.sem_inc(e_ready, 3)
            act.sem_inc(pT_ready, 2)
            act.sem_inc(scores_copied, 1)
            act.wait_ge(w_loaded, 256)
            with act.Fori(0, B) as b:
                act.wait_ge(xn_turned, b + 1)
                act.copy(xnT[:], turn.rearrange("p (c s) -> p c s", c=C)).then_inc(xnT_ready, 1)
                for g in range(NG):
                    act.wait_ge(qk_made, b * NG + g + 1)
                    act.activation(qT[:, g, :], pair[:, 0:S], ACT.Identity, bias=bq[:, g:g + 1]).then_inc(qk_copied, 1)
                    act.activation(kT[:, g, :], pair[:, S:2 * S], ACT.Identity, bias=bk[:, g:g + 1]).then_inc(qk_copied, 1)
                with act.Fori(0, NG) as g:
                    n = (b * NG + g) * UNITS

                    def turned(u):
                        act.wait_ge(pm_turned, n + u + 3)
                        act.wait_ge(pv_done, n + u + 1)
                        act.copy(pT[:, u % 2].rearrange("p t q -> p (t q)"), turn[:, 0:S]).then_inc(pT_ready, 1)

                    def copied(p):
                        act.wait_ge(scores_made, (b * NG + g) * HG + p + 2)
                        act.wait_ge(scores_read, n + 2 * p + 1)
                        act.copy(s[:, p % 2].rearrange("p j k -> p (j k)"), pair).then_inc(scores_copied, 1)

                    copied(0)
                    copied(1)
                    for u in range(UNITS):
                        act.wait_ge(first_max, n + u + 1)
                        act.mul(nmax[:, u % 2:u % 2 + 1], top[:, u % 2, 0, 0:1], -0.25).then_inc(nmax_ready, 1)
                        act.wait_ge(nmax_ready, n + u + 1)
                        act.wait_ge(pm_ready, n + u + 1)
                        act.activation(e[:, u % 2], s[:, u // 2 % 2, u % 2], ACT.Exp, scale=0.25,
                                       bias=nmax[:, u % 2:u % 2 + 1]).then_inc(e_ready, 1)
                        if u >= 1:
                            turned(u - 1)
                        if u % 2 == 1 and u // 2 + 2 < HG:
                            copied(u // 2 + 2)
                    turned(UNITS - 1)
                act.wait_ge(ao_turned, b + 1)
                act.copy(aoT[:], turn.rearrange("p (c s) -> p c s", c=C)).then_inc(aoT_ready, 1)

        @block.tensor
        def _(pe):
            pe.sem_inc(pm_turned, 2)
            pe.sem_inc(pv_done, 2)
            pe.sem_inc(scores_made, 1)
            pe.wait_ge(w_loaded, 256)
            with pe.Fori(0, B) as b:
                pe.wait_ge(xn_ready, b + 1)
                for c in range(C):
                    for t in range(T):
                        mm = pe.transpose(turn[:, c * S + t * P:c * S + (t + 1) * P], xn[:, t, c * P:(c + 1) * P], ident[:])
                mm.then_inc(xn_turned, 1)
                pe.wait_ge(xnT_ready, b + 1)
                for g in range(NG):
                    if g >= 1:
                        pe.wait_ge(qk_copied, 2 * NG * b + 2 * g)
                    for i, w in enumerate((wqT, wkT)):
                        for c in range(C):
                            mm = pe.matmul(pair[:, i * S:(i + 1) * S], w[:, c, g].rearrange("p j d -> p (j d)"), xnT[:, c, :],
                                           start=(c == 0), stop=(c == C - 1))
                    mm.then_inc(qk_made, 1)
                for t in range(T):
                    for c in range(C):
                        mm = pe.matmul(wide[:, t * E:(t + 1) * E], xnT[:, c, t * P:(t + 1) * P], wvT[:, c, :],
                                       start=(c == 0), stop=(c == C - 1))
                mm.then_inc(v_made, 1)
                pe.wait_ge(qk_copied, 2 * NG * (b + 1))
                pe.wait_ge(v_ready, b + 1)
                pe.sem_inc(passed, 1)
                with pe.Fori(0, NG) as g:
                    q = b * NG + g
                    n = q * UNITS
                    pe.wait_ge(kg_ready, q + 1)
                    pe.wait_ge(heads_ready, q + 1)

                    def scores(p):
                        pe.wait_ge(scores_copied, q * HG + p + 1)
                        j, t = unit(2 * p)
                        pe.matmul(pair, qg[:, t * P:(t + 1) * P], kg[:, j:j + 2, :].rearrange("p j k -> p (j k)"),
                                  start=True, stop=True).then_inc(scores_made, 1)

                    def product(u):
                        j, t = unit(u)
                        pe.wait_ge(pT_ready, n + u + 3)
                        for k in range(T):
                            mm = pe.matmul(sums[:, t, j, :], pT[:, u % 2, k, :],
                                           v[:, k, bass.ds(g * HG + j, 1), :].rearrange("p a v -> p (a v)"), start=(k == 0), stop=(k == T - 1))
                        mm.then_inc(pv_done, 1)

                    scores(0)
                    scores(1)
                    for u in range(UNITS):
                        pe.wait_ge(pm_ready, n + u + 3)
                        pe.wait_ge(pT_ready, n + u + 2)
                        for k in range(T):
                            mm = pe.transpose(turn[:, k * P:(k + 1) * P], pm[:, u % 2, k * P:(k + 1) * P], ident[:])
                        mm.then_inc(pm_turned, 1)
                        if u % 2 == 1 and u // 2 + 2 < HG:
                            scores(u // 2 + 2)
                        if u >= 1:
                            product(u - 1)
                    product(UNITS - 1)
                pe.wait_ge(heads_ready, (b + 1) * NG + 1)
                for c in range(C):
                    for t in range(T):
                        mm = pe.transpose(turn[:, c * S + t * P:c * S + (t + 1) * P], ao[:, t, c * P:(c + 1) * P], ident[:])
                mm.then_inc(ao_turned, 1)
                pe.wait_ge(aoT_ready, b + 1)
                for t in range(T):
                    for c in range(C):
                        mm = pe.matmul(wide[:, t * E:(t + 1) * E], aoT[:, c, t * P:(t + 1) * P], woT[:, c, :],
                                       start=(c == 0), stop=(c == C - 1))
                mm.then_inc(proj_ready, 1)

        @block.vector
        def _(dve):
            step = Chain(dve, dve_step)
            dve.memset(v[:], 1.0).then_inc(dve_step, 1)
            dve.wait_ge(dve_step, 1)
            dve.sem_inc(scores_read, 3)
            dve.sem_inc(pm_ready, 2)
            dve.sem_inc(heads_ready, 1)
            dve.wait_ge(w_loaded, 256)
            with dve.Fori(0, B) as b:
                step.restart()
                for t in range(T):
                    step(dve.bn_stats(stats[:, t], row_tile(X, b * T + t)))
                    step(dve.bn_aggr(mv[:, t], stats[:, t]))
                dve.tensor_scalar(ve[:], mv[:, :, 1], EPS, None, ALU.add).then_inc(var_ready, 1)
                dve.wait_ge(rstd_ready, b + 1)
                for t in range(T):
                    step(dve.tensor_scalar(xn[:, t], row_tile(X, b * T + t), mv[:, t, 0:1], rstd[:, t:t + 1], ALU.subtract, ALU.mult))
                dve.sem_inc(xn_ready, 1)
                for t in range(T):
                    step(dve.tensor_tensor(row_tile(X, b * T + t), row_tile(X, b * T + t), bo[:], ALU.add))
                dve.wait_ge(v_made, b + 1)
                for t in range(T):
                    step(dve.tensor_tensor(v[:, t, :, 0:D], wide[:, t * E:(t + 1) * E].rearrange("p (h d) -> p h d", d=D),
                                           bv[:].rearrange("p (h d) -> p h d", d=D), ALU.add))
                dve.sem_inc(v_ready, 1)
                with dve.Fori(0, NG) as g:
                    q = b * NG + g
                    n = q * UNITS
                    step.restart()
                    for u in range(UNITS):
                        w = work[:, u % 2]
                        dve.wait_ge(scores_copied, q * HG + u // 2 + 2)
                        for r in range(TOPK // 8):
                            if r == 0:
                                step.hold()
                            best, src = top[:, u % 2, r], (s[:, u // 2 % 2, u % 2] if r == 0 else w)
                            step(dve.max(best, src))
                            if r == 0:
                                dve.sem_inc(first_max, 1)
                            step(dve.match_replace(w, best, src, LOW))
                            if r == 0:
                                dve.sem_inc(scores_read, 1)
                        dve.wait_ge(e_ready, n + u + 4)
                        dve.wait_ge(pm_turned, n + u + 1)
                        dve.scalar_tensor_tensor(out=pm[:, u % 2], in0=w, scalar=LOW, in1=e[:, u % 2], op0=ALU.is_equal, op1=ALU.mult).then_inc(pm_ready, 1)
                    dve.wait_ge(pv_done, n + UNITS + 2)
                    step(dve.reciprocal(recip[:], sums[:, :, :, D]))
                    dve.tensor_tensor(ao[:, :, bass.ds(g * (HG * D), HG * D)].rearrange("p t (j d) -> p t j d", d=D), sums[:, :, :, 0:D],
                                      recip[:].unsqueeze(3).to_broadcast([P, T, HG, D]), ALU.mult).then_inc(heads_ready, 1)
                dve.wait_ge(proj_ready, b + 1)
                step.restart()
                for t in range(T):
                    x_t = row_tile(X, b * T + t)
                    step(dve.tensor_tensor(x_t, x_t, wide[:, t * E:(t + 1) * E], ALU.add))
                dve.sem_inc(x_added, 1)


class Norm:

    def __init__(self, sb, sem, bank):
        self.stats, self.mv = sb("stats", [P, T, 6]), sb("mv", [P, T, 2])
        self.ve, self.rstd, self.mhalf = sb("ve", [P, T]), sb("rstd", [P, T]), sb("mhalf", [P, T])
        self.xn, self.xnT, self.bank = sb("xn", [P, T, E]), sb("xnT", [P, C, S]), bank
        self.var_ready, self.rstd_ready, self.xn_ready = sem("var_ready"), sem("rstd_ready"), sem("xn_ready")
        self.xn_turned, self.xnT_ready = sem("xn_turned"), sem("xnT_ready")

    def vector(self, dve, step, tile, b):
        for t in range(T):
            step(dve.bn_stats(self.stats[:, t], tile(t)))
            step(dve.bn_aggr(self.mv[:, t], self.stats[:, t]))
        dve.tensor_scalar(self.ve[:], self.mv[:, :, 1], EPS, None, ALU.add).then_inc(self.var_ready, 1)
        dve.wait_ge(self.rstd_ready, b + 1)
        for t in range(T):
            step(dve.tensor_scalar(self.xn[:, t], tile(t), self.mv[:, t, 0:1], self.rstd[:, t:t + 1], ALU.subtract, ALU.mult))
        dve.sem_inc(self.xn_ready, 1)

    def gpsimd(self, pool, b):
        pool.wait_ge(self.var_ready, b + 1)
        pool.tensor_tensor(self.rstd[:], self.ve[:], self.mhalf[:], ALU.pow).then_inc(self.rstd_ready, 1)

    def tensor(self, pe, b, ident):
        pe.wait_ge(self.xn_ready, b + 1)
        for c in range(C):
            for t in range(T):
                mm = pe.transpose(self.bank[:, c * S + t * P:c * S + (t + 1) * P], self.xn[:, t, c * P:(c + 1) * P], ident[:])
        mm.then_inc(self.xn_turned, 1)

    def scalar(self, act, b):
        act.wait_ge(self.xn_turned, b + 1)
        act.copy(self.xnT[:], self.bank.rearrange("p (c s) -> p c s", c=C)).then_inc(self.xnT_ready, 1)


def argmax_row(dve, step, lg, best, idx, idxf, oh, count):
    for t in range(T):
        step(dve.max(best[:, t], lg[:, t]))
        step(dve.max_index(idx[:, t], best[:, t], lg[:, t]))
    step(dve.tensor_copy(idxf[:], idx[:, :, 0]))
    for t in range(T):
        step(dve.tensor_scalar(oh[:, t], count[:], idxf[:, t:t + 1], None, ALU.is_equal))


def experts(nc, a, X, ps, ident):
    ctx, sb, sem = scope(nc, "moe")
    with ctx:
        norm = Norm(sb, sem, ps[:, 0, :])
        wg = sb("wg", [P, C, EX])
        we = sb("we", [P, C, E])
        be = sb("be", [P, E])
        count = sb("count", [P, EX])
        upto = sb("upto", [P, P])
        ones = sb("ones", [P, P])
        lg = sb("lg", [P, T, EX])
        best = sb("best", [P, T, 8])
        idx = sb("idx", [P, T, 8], U32)
        idxf = sb("idxf", [P, T])
        oh = sb("oh", [P, T, EX])
        seen = sb("seen", [P, EX])
        nmax = sb("nmax", [P, T])
        ex = sb("ex", [P, T, EX])
        den = sb("den", [P, T])
        gate = sb("gate", [P, T])
        place = sb("place", [P, T, EX])
        rank = sb("rank", [P, T])
        keep = sb("keep", [P, T])
        hb = sb("hb", [P, T, E])

        loaded, consts, consts2 = sem("loaded"), sem("consts"), sem("consts2")
        lg_made, h_made, nmax_ready, den_ready = sem("lg_made"), sem("h_made"), sem("nmax_ready"), sem("den_ready")
        oh_ready, place_made, x_added, dve_step = sem("oh_ready"), sem("place_made"), sem("x_added"), sem("dve_step")
        lgp = ps[:, 1, 0:T * EX].rearrange("p (t e) -> p t e", t=T)
        hp = ps[:, 2, :].rearrange("p (t n) -> p t n", t=T)
        pp = ps[:, 3, 0:T * EX].rearrange("p (t e) -> p t e", t=T)

        block = ctx.enter_context(nc.Block())

        @block.sync
        def _(sp):
            sp.dma_start(wg[:], a["wg"].rearrange("(c p) n -> p c n", p=P)).then_inc(loaded, 16)
            sp.dma_start(we[:], a["we"].rearrange("(c p) n -> p c n", p=P)).then_inc(loaded, 16)
            sp.dma_start(be[:], a["be"].partition_broadcast(P)).then_inc(loaded, 16)

        @block.gpsimd
        def _(pool):
            pool.memset(norm.mhalf[:], -0.5).then_inc(consts, 1)
            pool.memset(ones[:], 1.0).then_inc(consts, 1)
            pool.memset(upto[:], 1.0).then_inc(consts, 1)
            pool.memset(seen[:], 0.0).then_inc(consts, 1)
            pool.iota(count[:], pattern=[[1, EX]], base=0, channel_multiplier=0, allow_small_or_imprecise_dtypes=True).then_inc(consts, 1)
            pool.wait_ge(consts, 5)
            pool.affine_select(out=upto[:], in_=upto[:], compare_op=ALU.is_ge, fill=0.0, base=0,
                               pattern=[[1, P]], channel_multiplier=-1).then_inc(consts2, 1)
            with pool.Fori(0, B) as b:
                norm.gpsimd(pool, b)

        @block.scalar
        def _(act):
            with act.Fori(0, B) as b:
                norm.scalar(act, b)
                act.wait_ge(nmax_ready, b + 1)
                for t in range(T):
                    act.activation(ex[:, t], lg[:, t], ACT.Exp, bias=nmax[:, t:t + 1], accum_out=den[:, t:t + 1]).then_inc(den_ready, 1)

        @block.tensor
        def _(pe):
            pe.wait_ge(loaded, 48)
            pe.wait_ge(consts2, 1)
            with pe.Fori(0, B) as b:
                norm.tensor(pe, b, ident)
                pe.wait_ge(norm.xnT_ready, b + 1)
                for t in range(T):
                    for c in range(C):
                        mm = pe.matmul(lgp[:, t], norm.xnT[:, c, t * P:(t + 1) * P], wg[:, c, :], start=(c == 0), stop=(c == C - 1))
                mm.then_inc(lg_made, 1)
                for t in range(T):
                    for c in range(C):
                        mm = pe.matmul(hp[:, t], norm.xnT[:, c, t * P:(t + 1) * P], we[:, c, :], start=(c == 0), stop=(c == C - 1))
                mm.then_inc(h_made, 1)
                pe.wait_ge(oh_ready, b + 1)
                for t in range(T):
                    pe.matmul(pp[:, t], ones[:], seen[:], start=True, stop=False)
                    for before in range(t):
                        pe.matmul(pp[:, t], ones[:], oh[:, before], start=False, stop=False)
                    mm = pe.matmul(pp[:, t], upto[:], oh[:, t], start=False, stop=True)
                mm.then_inc(place_made, 1)

        @block.vector
        def _(dve):
            step = Chain(dve, dve_step)
            dve.wait_ge(loaded, 48)
            dve.wait_ge(consts, 5)
            with dve.Fori(0, B) as b:
                step.restart()
                tile = lambda t: row_tile(X, b * T + t)
                norm.vector(dve, step, tile, b)
                dve.wait_ge(lg_made, b + 1)
                step(dve.tensor_copy(lg[:], lgp))
                argmax_row(dve, step, lg, best, idx, idxf, oh, count)
                dve.sem_inc(oh_ready, 1)
                dve.tensor_scalar(nmax[:], best[:, :, 0], -1.0, None, ALU.mult).then_inc(nmax_ready, 1)
                dve.wait_ge(h_made, b + 1)
                step(dve.tensor_tensor(hb[:], hp, be[:].unsqueeze(1).to_broadcast([P, T, E]), ALU.add))
                dve.wait_ge(den_ready, T * (b + 1))
                step(dve.reciprocal(gate[:], den[:]))
                dve.wait_ge(place_made, b + 1)
                step(dve.tensor_tensor(place[:], pp, oh[:], ALU.mult))
                for t in range(T):
                    step(dve.tensor_tensor(seen[:], seen[:], oh[:, t], ALU.add))
                step(dve.reduce_sum(rank[:], place[:], AX.X))
                step(dve.tensor_scalar(keep[:], rank[:], float(CAP), None, ALU.is_le))
                step(dve.tensor_tensor(keep[:], keep[:], gate[:], ALU.mult))
                for t in range(T):
                    ins = dve.scalar_tensor_tensor(out=tile(t), in0=hb[:, t], scalar=keep[:, t:t + 1], in1=tile(t), op0=ALU.mult, op1=ALU.add)
                    ins.then_inc(x_added, 1)
                dve.wait_ge(x_added, T * b + T)


def context_attention(nc, a, X, ps, ident):
    ctx, sb, sem = scope(nc, "ctx")
    with ctx:
        norm = Norm(sb, sem, ps[:, 7, :])
        M, MW = 4, SK // 4
        W = 8
        wq = sb("wq", [P, C, E])
        wk = sb("wk", [P, C, E])
        wvT = sb("wvT", [P, C, E])
        G = sb("G", [P, C, E])
        qT = sb("qT", [P, C, S])
        kx = sb("kx", [P, M, C, MW])
        vx = sb("vx", [P, KT, E])
        sc = sb("sc", [P, T, SK])
        mx = sb("mx", [P, T, M])
        nmax = sb("nmax", [P, T])
        den = sb("den", [P, T, M])
        recip = sb("recip", [P, T])
        pT = sb("pT", [P, 2, 4 * P])
        o = sb("o", [P, T, E])
        oT = sb("oT", [P, C, S])

        loaded, g_made, g_copied, consts = sem("loaded"), sem("g_made"), sem("g_copied"), sem("consts")
        k_loaded = [sem(f"k_loaded{m}") for m in range(M)]
        v_loaded = [sem(f"v_loaded{m}") for m in range(M)]
        q_made, qT_ready, scores_made, scores_copied = sem("q_made"), sem("qT_ready"), sem("scores_made"), sem("scores_copied")
        mx_ready, nmax_ready, exp_ready = sem("mx_ready"), sem("nmax_ready"), sem("exp_ready")
        turned, pT_ready, pv_done, o_ready = sem("turned"), sem("pT_ready"), sem("pv_done"), sem("o_ready")
        o_turned, oT_ready, proj_ready, dve_step = sem("o_turned"), sem("oT_ready"), sem("proj_ready"), sem("dve_step")
        x_added = sem("x_added")
        MC, WC = T * M, T * W

        slot = lambda m: ps[:, 2 * (m % 2):2 * (m % 2) + 2, :]
        turn = lambda w: ps[:, 4 + w % 2, :]
        acc, wide = ps[:, 6, 0:E], ps[:, 7, :]

        block = ctx.enter_context(nc.Block())

        @block.sync
        def _(sp):
            for w, name in ((wq, "wq2"), (wk, "wk2"), (wvT, "wv2T")):
                sp.dma_start(w[:], a[name].rearrange("(c p) n -> p c n", p=P)).then_inc(loaded, 16)
            with sp.Fori(0, B) as b:
                for m in range(M):
                    sp.wait_ge(scores_made, MC * b + M + m + 1)
                    for c in range(C):
                        sp.dma_start(kx[:, m, c, :], a["ctxT"][bass.ds(b * C + c, 1), :, m * MW:(m + 1) * MW].rearrange("a p k -> p (a k)")).then_inc(k_loaded[m], 16)
                for m in range(M):
                    sp.wait_ge(pv_done, WC * b + W + 2 * m + 2)
                    sp.dma_start(vx[:, m * 8:(m + 1) * 8, :], a["ctx"][bass.ds(b, 1), m * MW:(m + 1) * MW, :]
                                 .rearrange("a (k p) d -> p (a k) d", p=P)).then_inc(v_loaded[m], 16)

        @block.gpsimd
        def _(pool):
            pool.memset(norm.mhalf[:], -0.5).then_inc(consts, 1)
            pool.wait_ge(consts, 1)
            with pool.Fori(0, B) as b:
                norm.gpsimd(pool, b)

        @block.scalar
        def _(act):
            act.sem_inc(scores_copied, 2)
            act.wait_ge(g_made, 1)
            act.copy(G[:].rearrange("p c n -> p (c n)"), wide).then_inc(g_copied, 1)
            with act.Fori(0, B) as b:
                norm.scalar(act, b)
                act.wait_ge(q_made, b + 1)
                act.copy(qT[:].rearrange("p c s -> p (c s)"), wide).then_inc(qT_ready, 1)
                for t in range(T):
                    for m in range(M):
                        n = (b * T + t) * M + m
                        act.wait_ge(scores_made, MC + n + 1)
                        act.copy(sc[:, t, m * MW:(m + 1) * MW], slot(m).rearrange("p a k -> p (a k)")).then_inc(scores_copied, 1)
                for t in range(T):
                    act.wait_ge(nmax_ready, b * T + t + 1)
                    for m in range(M):
                        part = sc[:, t, m * MW:(m + 1) * MW]
                        act.activation(part, part, ACT.Exp, scale=1.0 / 16.0, bias=nmax[:, t:t + 1], accum_out=den[:, t, m:m + 1]).then_inc(exp_ready, 1)
                act.wait_ge(o_turned, b + 1)
                act.copy(oT[:].rearrange("p c s -> p (c s)"), wide).then_inc(oT_ready, 1)

        @block.tensor
        def _(pe):
            pe.sem_inc(scores_made, MC)
            pe.sem_inc(pv_done, WC)
            pe.wait_ge(loaded, 48)
            for i in range(C):
                for c in range(C):
                    mm = pe.matmul(wide[:, i * E:(i + 1) * E], wq[:, c, i * P:(i + 1) * P], wk[:, c, :], start=(c == 0), stop=(c == C - 1))
            mm.then_inc(g_made, 1)
            pe.wait_ge(g_copied, 1)
            with pe.Fori(0, B) as b:
                norm.tensor(pe, b, ident)
                pe.wait_ge(norm.xnT_ready, b + 1)
                for j in range(C):
                    for c in range(C):
                        mm = pe.matmul(wide[:, j * S:(j + 1) * S], G[:, c, j * P:(j + 1) * P], norm.xnT[:, c, :], start=(c == 0), stop=(c == C - 1))
                mm.then_inc(q_made, 1)
                pe.wait_ge(qT_ready, b + 1)
                for t in range(T):
                    for m in range(M):
                        n = (b * T + t) * M + m
                        if t == 0:
                            pe.wait_ge(k_loaded[m], 16 * C * (b + 1))
                        pe.wait_ge(scores_copied, n + 1)
                        for w in range(2):
                            for c in range(C):
                                mm = pe.matmul(slot(m)[:, w, :], qT[:, c, t * P:(t + 1) * P], kx[:, m, c, w * 512:(w + 1) * 512], start=(c == 0), stop=(c == C - 1))
                        mm.then_inc(scores_made, 1)
                for t in range(T):
                    n = (b * T + t) * W

                    def product(w):
                        if t == 0 and w % 2 == 0:
                            pe.wait_ge(v_loaded[w // 2], 16 * (b + 1))
                        if w == 0:
                            pe.wait_ge(o_ready, b * T + t + 1)
                        pe.wait_ge(pT_ready, n + w + 3)
                        for i in range(4):
                            mm = pe.matmul(acc, pT[:, w % 2, i * P:(i + 1) * P], vx[:, 4 * w + i, :], start=(w == 0 and i == 0), stop=(w == W - 1 and i == 3))
                        mm.then_inc(pv_done, 1)

                    for w in range(W):
                        pe.wait_ge(exp_ready, (b * T + t) * M + w // 2 + 1)
                        pe.wait_ge(pT_ready, n + w + 1)
                        for i in range(4):
                            k = 4 * w + i
                            mm = pe.transpose(turn(w)[:, i * P:(i + 1) * P], sc[:, t, k * P:(k + 1) * P], ident[:])
                        mm.then_inc(turned, 1)
                        if w >= 1:
                            product(w - 1)
                    product(W - 1)
                pe.wait_ge(o_ready, b * T + T + 1)
                for c in range(C):
                    for t in range(T):
                        mm = pe.transpose(wide[:, c * S + t * P:c * S + (t + 1) * P], o[:, t, c * P:(c + 1) * P], ident[:])
                mm.then_inc(o_turned, 1)
                pe.wait_ge(oT_ready, b + 1)
                for t in range(T):
                    for c in range(C):
                        mm = pe.matmul(wide[:, t * E:(t + 1) * E], oT[:, c, t * P:(t + 1) * P], wvT[:, c, :], start=(c == 0), stop=(c == C - 1))
                mm.then_inc(proj_ready, 1)

        @block.vector
        def _(dve):
            step = Chain(dve, dve_step)
            dve.sem_inc(pT_ready, 2)
            dve.sem_inc(o_ready, 1)
            with dve.Fori(0, B) as b:
                step.restart()
                tile = lambda t: row_tile(X, b * T + t)
                norm.vector(dve, step, tile, b)
                for t in range(T):
                    for m in range(M):
                        n = (b * T + t) * M + m
                        dve.wait_ge(scores_copied, n + 3)
                        dve.reduce_max(mx[:, t, m:m + 1], sc[:, t, m * MW:(m + 1) * MW], AX.X).then_inc(mx_ready, 1)
                    dve.wait_ge(mx_ready, (b * T + t + 1) * M)
                    step(dve.reduce_max(nmax[:, t:t + 1], mx[:, t], AX.X))
                    dve.tensor_scalar(nmax[:, t:t + 1], nmax[:, t:t + 1], -1.0 / 16.0, None, ALU.mult).then_inc(nmax_ready, 1)
                for t in range(T):
                    for w in range(W):
                        n = (b * T + t) * W + w
                        dve.wait_ge(turned, n + 1)
                        dve.wait_ge(pv_done, WC + n - 1)
                        dve.tensor_copy(pT[:, w % 2], turn(w)).then_inc(pT_ready, 1)
                    dve.wait_ge(exp_ready, (b * T + t + 1) * M)
                    step(dve.reduce_sum(recip[:, t:t + 1], den[:, t], AX.X))
                    step(dve.reciprocal(recip[:, t:t + 1], recip[:, t:t + 1]))
                    dve.wait_ge(pv_done, WC + (b * T + t + 1) * W)
                    dve.tensor_scalar(o[:, t], acc, recip[:, t:t + 1], None, ALU.mult).then_inc(o_ready, 1)
                dve.wait_ge(proj_ready, b + 1)
                for t in range(T):
                    dve.tensor_tensor(tile(t), tile(t), wide[:, t * E:(t + 1) * E], ALU.add).then_inc(x_added, 1)
                dve.wait_ge(x_added, T * b + T)


N_STATE = 16
TAPS = 4
RANK = 8
TIME = B * S
HALVES = TIME // 512


def state_space(nc, a, X, ps, ident):
    ctx, sb, sem = scope(nc, "ssm")
    with ctx:
        norm = Norm(sb, sem, ps[:, 0, :])
        nw, nb = sb("nw", [P, E]), sb("nb", [P, E])
        win = sb("win", [P, 2, 4 * P])
        cw, cb = sb("cw", [P, 2, C, TAPS]), sb("cb", [P, 2, C])
        wx = sb("wx", [P, 2, C, RANK + 2 * N_STATE])
        wdt = sb("wdt", [40, 2, E])
        bdt = sb("bdt", [P, 2, C])
        alog = sb("alog", [P, 2, C, N_STATE])
        dcol = sb("dcol", [P, 2, C])
        wout = sb("wout", [P, 2, C, P])
        A = sb("A", [P, 2, C, N_STATE])
        sel = sb("sel", [96, 2 * N_STATE, P], BF16)
        diag = sb("diag", [P, C, P])
        mirror = sb("mirror", [P, P])
        xT = sb("xT", [P, 2, B, S])
        xcp = sb("xcp", [P, C, B, S + TAPS - 1])
        sz = sb("sz", [P, C, TIME])
        cv = sb("cv", [P, C, TIME])
        xc = sb("xc", [P, C, TIME])
        bc = sb("bc", [96, TIME], BF16)
        bcr = sb("bcr", [32, TIME])
        dtr = sb("dtr", [40, TIME])
        v = sb("v", [P, C, TIME])
        dt = sb("dt", [P, C, TIME])
        du = sb("du", [P, C, TIME])
        decay = [sb(f"decay{i}", [P, C, TIME]) for i in range(2)]
        bu = sb("bu", [P, C, TIME])
        h = sb("h", [P, C, TIME])
        hc = [sb(f"hc{i}", [P, C, TIME]) for i in range(2)]

        loaded, consts, zeroed = sem("loaded"), sem("consts"), sem("zeroed")
        h_done, mirror_ready = sem("h_done"), sem("mirror_ready")
        a_exp, a_ready, sel_ready = sem("a_exp"), sem("a_ready"), sem("sel_ready")
        xT_ready, xz_made, xc_copied, sz_ready = sem("xT_ready"), sem("xz_made"), sem("xc_copied"), sem("sz_ready")
        cv_ready, xc_ready, xd_made, bc_ready, dtr_ready = sem("cv_ready"), sem("xc_ready"), sem("xd_made"), sem("bc_ready"), sem("dtr_ready")
        dt_made, v_ready, l_ready, dt_ready, diag_ready = sem("dt_made"), sem("v_ready"), sem("l_ready"), sem("dt_ready"), sem("diag_ready")
        act_step, dve_step = sem("act_step"), sem("dve_step")
        b_made, c_made, bu_done, hc_ready, summed = sem("b_made"), sem("c_made"), sem("bu_done"), sem("hc_ready"), sem("summed")
        decay_ready, scanned, gated, out_made, x_added = sem("decay_ready"), sem("scanned"), sem("gated"), sem("out_made"), sem("x_added")

        two = lambda i: ps[:, 2 * i:2 * i + 2, :]
        flat = lambda v: v.rearrange("p a q -> p (a q)")
        PAIRS = N_STATE // 2

        def each_pair(eng, body):
            with eng.Fori(0, PAIRS - 1) as i:
                body(2 * i, False)
            body(N_STATE - 2, True)

        block = ctx.enter_context(nc.Block())

        @block.sync
        def _(sp):
            for w, name in ((nw, "nw"), (nb, "nb")):
                sp.dma_start(w[:], a[name].partition_broadcast(P)).then_inc(loaded, 16)
            for w, name in ((win, "win"), (cw, "cw"), (cb, "cb"), (wx, "wx"), (bdt, "bdt"), (alog, "alog"), (dcol, "dcol"), (wout, "wout")):
                sp.dma_start(w[:], a[name]).then_inc(loaded, 16)
            sp.dma_start(wdt[32:32 + RANK], a["wdt"]).then_inc(loaded, 16)

        LOADS = 16 * 11

        @block.gpsimd
        def _(pool):
            pool.memset(norm.mhalf[:], -0.5).then_inc(consts, 1)
            pool.memset(mirror[:], 0.0).then_inc(consts, 1)
            pool.wait_ge(consts, 2)
            pool.affine_select(out=mirror[:], in_=mirror[:], compare_op=ALU.not_equal, fill=1.0, base=1 - P,
                               pattern=[[1, P]], channel_multiplier=1).then_inc(mirror_ready, 1)
            pool.memset(xcp[:], 0.0).then_inc(zeroed, 1)
            with pool.Fori(0, B) as b:
                for k in range(2):
                    pool.wait_ge(norm.var_ready, 2 * b + k + 1)
                    pool.tensor_tensor(norm.rstd[:], norm.ve[:], norm.mhalf[:], ALU.pow).then_inc(norm.rstd_ready, 1)

        @block.scalar
        def _(act):
            act.sem_inc(decay_ready, 1)
            act.wait_ge(loaded, LOADS)
            act.activation(A[:], alog[:], ACT.Exp).then_inc(a_exp, 1)
            with act.Fori(0, B) as b:
                act.wait_ge(norm.xn_turned, b + 1)
                for d in range(2):
                    dst = xT[:, d, bass.ds(b, 1), :].rearrange("p a s -> p (a s)")
                    act.copy(dst, norm.bank[:, d * S:(d + 1) * S]).then_inc(xT_ready, 1)
            act.wait_ge(zeroed, 1)
            for d in range(2):
                act.wait_ge(xz_made, 4 * d + 2)
                if d:
                    act.wait_ge(cv_ready, C * d)
                for k in range(C):
                    act.copy(xcp[:, k, :, TAPS - 1:], flat(two(k)).rearrange("p (b s) -> p b s", b=B)).then_inc(xc_copied, 1)
                act.wait_ge(xz_made, 4 * d + 4)
                for k in range(C):
                    act.activation(sz[:, k], flat(two(2 + k)), ACT.Silu).then_inc(sz_ready, 1)
                for k in range(C):
                    act.wait_ge(cv_ready, C * d + k + 1)
                    act.activation(xc[:, k], cv[:, k], ACT.Silu).then_inc(xc_ready, 1)
                act.wait_ge(xd_made, d + 1)
                act.copy(dtr[32:32 + RANK], flat(two(0))[32:32 + RANK]).then_inc(dtr_ready, 1)
                for k in range(C):
                    n = 2 * (C * d + k)
                    act.wait_ge(dt_made, C * d + k + 1)
                    act.activation(v[:, k], flat(two(1 + k)), ACT.Identity, bias=bdt[:, d, k:k + 1]).then_inc(v_ready, 1)
                    act.wait_ge(v_ready, C * d + k + 1)
                    act.activation(dt[:, k], v[:, k], ACT.Abs).then_inc(act_step, 1)
                    act.wait_ge(act_step, n + 1)
                    act.activation(dt[:, k], dt[:, k], ACT.Exp, scale=-1.0).then_inc(act_step, 1)
                    act.wait_ge(act_step, n + 2)
                    act.activation(dt[:, k], dt[:, k], ACT.Ln, bias=1.0).then_inc(l_ready, 1)
                act.wait_ge(dt_ready, C * d + C)
                act.wait_ge(a_ready, 1)

                def decays(n, last):
                    for j in range(2):
                        act.wait_ge(scanned, d * N_STATE + n + j + 1)
                        for k in range(C):
                            ins = act.activation(decay[j][:, k], dt[:, k], ACT.Exp, scale=A[:, d, k, bass.ds(n + j, 1)])
                        ins.then_inc(decay_ready, 1)

                each_pair(act, decays)

        @block.tensor
        def _(pe):
            pe.sem_inc(summed, 2)
            pe.wait_ge(mirror_ready, 1)
            with pe.Fori(0, B) as b:
                pe.wait_ge(norm.xn_ready, b + 1)
                pe.wait_ge(xT_ready, 2 * b + 2)
                for t in range(T):
                    pe.transpose(norm.bank[:, t * P:(t + 1) * P], norm.xn[:, t, 0:P], ident[:])
                    mm = pe.transpose(norm.bank[:, S + (T - 1 - t) * P:S + (T - t) * P], norm.xn[:, t, P:2 * P], mirror[:])
                mm.then_inc(norm.xn_turned, 1)
            pe.wait_ge(xT_ready, 2 * B + 2)
            pe.wait_ge(loaded, LOADS)
            for d in range(2):
                if d:
                    pe.wait_ge(gated, 1)
                    pe.wait_ge(x_added, 1)
                for m in range(4):
                    for w in range(HALVES):
                        mm = pe.matmul(two(m)[:, w, :], win[:, d, m * P:(m + 1) * P], xT[:, d, 2 * w:2 * w + 2, :].rearrange("p b s -> p (b s)"),
                                       start=True, stop=True)
                    mm.then_inc(xz_made, 1)
                pe.wait_ge(xc_ready, C * d + C)
                pe.wait_ge(xc_copied, C * d + C)
                for w in range(HALVES):
                    for k in range(C):
                        mm = pe.matmul(two(0)[0:40, w, :], wx[:, d, k, :], xc[:, k, w * 512:(w + 1) * 512], start=(k == 0), stop=(k == C - 1))
                mm.then_inc(xd_made, 1)
                pe.wait_ge(dtr_ready, d + 1)
                pe.wait_ge(sz_ready, C * d + C)
                for k in range(C):
                    for w in range(HALVES):
                        mm = pe.matmul(two(1 + k)[:, w, :], wdt[32:32 + RANK, d, k * P:(k + 1) * P], dtr[32:32 + RANK, w * 512:(w + 1) * 512],
                                       start=True, stop=True)
                    mm.then_inc(dt_made, 1)
                pe.wait_ge(diag_ready, d + 1)
                pe.wait_ge(sel_ready, 1)
                pe.wait_ge(bc_ready, d + 1)
                pe.wait_ge(v_ready, C * d + C)
                for k in range(C):
                    for w in range(HALVES):
                        pe.matmul(two(k)[:, w, :], diag[:, k, :], xc[:, k, w * 512:(w + 1) * 512], start=True, stop=False, skip_group_check=True)

                def spread(i, row):
                    for w in range(HALVES):
                        mm = pe.matmul(two(i)[:, w, :], sel[:, bass.ds(row, 1), :].rearrange("p a m -> p (a m)"), bc[:, w * 512:(w + 1) * 512],
                                       start=True, stop=True)
                    return mm

                spread(2, 0).then_inc(b_made, 1)

                def states(n, last):
                    for j in range(2):
                        N = d * N_STATE + n + j
                        pe.wait_ge(hc_ready, N + 1)
                        spread(3, N_STATE + n + j).then_inc(c_made, 1)
                        if not (last and j == 1):
                            pe.wait_ge(bu_done, N + 1)
                            spread(2, n + j + 1).then_inc(b_made, 1)
                        pe.wait_ge(hc_ready, N + 2)
                        for k in range(C):
                            for w in range(HALVES):
                                mm = pe.matmul(two(k)[:, w, :], ident[:], hc[j][:, k, w * 512:(w + 1) * 512], start=False,
                                               stop=(last and j == 1), skip_group_check=True)
                        mm.then_inc(summed, 1)

                each_pair(pe, states)
                pe.wait_ge(gated, d + 1)
                out = flat(two(2)).rearrange("p (r n) -> p r n", n=P)
                for r in range(ROWS):
                    for k in range(C):
                        mm = pe.matmul(out[:, r], cv[:, k, r * P:(r + 1) * P], wout[:, d, k, :], start=(k == 0), stop=(k == C - 1))
                mm.then_inc(out_made, 1)

        @block.vector
        def _(dve):
            step = Chain(dve, dve_step)
            dve.sem_inc(scanned, 2)
            dve.sem_inc(hc_ready, 1)
            dve.sem_inc(xT_ready, 2)
            dve.wait_ge(loaded, LOADS)
            for i in range(3):
                step(dve.tensor_copy(sel[32 * i:32 * i + 32], ident[32 * i:32 * i + 32, 32 * i:32 * i + 32].unsqueeze(2).to_broadcast([32, 32, P])))
            dve.sem_inc(sel_ready, 1)
            dve.wait_ge(a_exp, 1)
            step(dve.tensor_scalar(A[:], A[:], -1.0, None, ALU.mult))
            dve.sem_inc(a_ready, 1)
            with dve.Fori(0, B) as b:
                step.restart()
                tile = lambda t: row_tile(X, b * T + t)
                for k in range(2):
                    src = tile if k == 0 else (lambda t: norm.xn[:, t])
                    for t in range(T):
                        step(dve.bn_stats(norm.stats[:, t], src(t)))
                        step(dve.bn_aggr(norm.mv[:, t], norm.stats[:, t]))
                    dve.tensor_scalar(norm.ve[:], norm.mv[:, :, 1], EPS, None, ALU.add).then_inc(norm.var_ready, 1)
                    dve.wait_ge(norm.rstd_ready, 2 * b + k + 1)
                    for t in range(T):
                        step(dve.tensor_scalar(norm.xn[:, t], src(t), norm.mv[:, t, 0:1], norm.rstd[:, t:t + 1], ALU.subtract, ALU.mult))
                        if k == 0:
                            step(dve.tensor_tensor(tile(t), tile(t), norm.xn[:, t], ALU.add))
                for t in range(T):
                    step(dve.tensor_tensor(norm.xn[:, t], norm.xn[:, t], nw[:], ALU.mult))
                    step(dve.tensor_tensor(norm.xn[:, t], norm.xn[:, t], nb[:], ALU.add))
                dve.sem_inc(norm.xn_ready, 1)
                dve.wait_ge(xT_ready, 2 * b + 4)
            for d in range(2):
                step.restart()
                for k in range(C):
                    step(dve.tensor_scalar(diag[:, k], ident[:], dcol[:, d, k:k + 1], None, ALU.mult))
                dve.sem_inc(diag_ready, 1)
                dve.wait_ge(xc_copied, C * d + C)
                for k in range(C):
                    out = cv[:, k].rearrange("p (b s) -> p b s", b=B)
                    tap = lambda i: xcp[:, k, :, i:i + S]
                    step(dve.tensor_scalar(out, tap(TAPS - 1), cw[:, d, k, TAPS - 1:TAPS], cb[:, d, k:k + 1], ALU.mult, ALU.add))
                    for i in range(TAPS - 1):
                        step(dve.scalar_tensor_tensor(out=out, in0=tap(i), scalar=cw[:, d, k, i:i + 1], in1=out, op0=ALU.mult, op1=ALU.add))
                    dve.sem_inc(cv_ready, 1)
                dve.wait_ge(xd_made, d + 1)
                dve.wait_ge(dtr_ready, d + 1)
                xd = flat(two(0))[0:32]
                step(dve.tensor_copy(bc[0:32], xd))
                step(dve.tensor_tensor(bcr[:], xd, bc[0:32], ALU.subtract))
                step(dve.tensor_copy(bc[32:64], bcr[:]))
                step(dve.tensor_copy(hc[0][0:32, 0, 0:TIME], bc[32:64]))
                step(dve.tensor_tensor(bc[64:96], bcr[:], hc[0][0:32, 0, 0:TIME], ALU.subtract))
                dve.sem_inc(bc_ready, 1)
                for k in range(C):
                    dve.wait_ge(l_ready, C * d + k + 1)
                    step(dve.scalar_tensor_tensor(out=dt[:, k], in0=v[:, k], scalar=0.0, in1=dt[:, k], op0=ALU.max, op1=ALU.add))
                    dve.sem_inc(dt_ready, 1)
                    step(dve.tensor_tensor(du[:, k], dt[:, k], xc[:, k], ALU.mult))
                spreadk = lambda i: flat(two(i)).unsqueeze(1).to_broadcast([P, C, TIME])

                def scans(n, last):
                    for j in range(2):
                        N = d * N_STATE + n + j
                        step.restart()
                        dve.wait_ge(decay_ready, N + 2)
                        step(dve.memset(decay[j][:].rearrange("p k (b s) -> p k b s", b=B)[:, :, :, 0], 0.0))
                        dve.wait_ge(b_made, N + 1)
                        dve.tensor_tensor(bu[:], spreadk(2), du[:], ALU.mult).then_inc(bu_done, 1)
                        dve.wait_ge(bu_done, N + 1)
                        for k in range(C):
                            dve.tensor_tensor_scan(h[:, k], decay[j][:, k], bu[:, k], 0.0, ALU.mult, ALU.add).then_inc(h_done, 1)
                        dve.wait_ge(h_done, C * (N + 1))
                        dve.sem_inc(scanned, 1)
                        dve.wait_ge(c_made, N + 1)
                        dve.wait_ge(summed, N + 1)
                        dve.tensor_tensor(hc[j][:], spreadk(3), h[:], ALU.mult).then_inc(hc_ready, 1)

                each_pair(dve, scans)
                step.restart()
                dve.wait_ge(summed, (d + 1) * N_STATE + 2)
                for k in range(C):
                    for b in range(B):
                        cols = slice(b * S, (b + 1) * S)
                        out = cv[:, k, cols]
                        step(dve.tensor_tensor(out if d == 0 else out[:, ::-1], flat(two(k))[:, cols], sz[:, k, cols], ALU.mult))
                dve.sem_inc(gated, 1)
                dve.wait_ge(out_made, d + 1)
                part = X[:, :, d * P:(d + 1) * P]
                dve.tensor_tensor(part, part, flat(two(2)).rearrange("p (r n) -> p r n", n=P), ALU.add).then_inc(x_added, 1)
                dve.wait_ge(x_added, d + 1)


def routed(nc, a, X, ps, ident, out):
    ctx, sb, sem = scope(nc, "ffn")
    with ctx:
        norm = Norm(sb, sem, ps[:, 0, :])
        sig = sb("sig", [P, C, EX])
        below = sb("below", [P, C, EX])
        w = sb("w", [P, C, EX, E])
        bias = sb("bias", [EX, E])
        count = sb("count", [P, EX])
        lg = sb("lg", [P, T, EX])
        best = sb("best", [P, T, 8])
        idx = sb("idx", [P, T, 8], U32)
        idxf = sb("idxf", [P, T])
        oh = sb("oh", [P, T, EX])
        ohT = sb("ohT", [EX, T, P])
        y = sb("y", [P, E])

        loaded, consts, sign_ready = sem("loaded"), sem("consts"), sem("sign_ready")
        lg_made, oh_ready, oh_turned, ohT_ready, bias_made = sem("lg_made"), sem("oh_ready"), sem("oh_turned"), sem("ohT_ready"), sem("bias_made")
        y_made, y_used, x_added, stored, dve_step = sem("y_made"), sem("y_used"), sem("x_added"), sem("stored"), sem("dve_step")
        PAIRS = EX // 2
        lgp = ps[:, 1, 0:T * EX].rearrange("p (t e) -> p t e", t=T)
        pairs = lambda p: ps[:, 2 + p, :].rearrange("p (e n) -> p e n", e=2)
        ohp = ps[0:EX, 6, 0:T * P]
        bp = ps[:, 7, :].rearrange("p (t n) -> p t n", t=T)

        block = ctx.enter_context(nc.Block())

        @block.sync
        def _(sp):
            sp.dma_start(sig[:], a["sigT"].rearrange("(c p) n -> p c n", p=P)).then_inc(loaded, 16)
            sp.dma_start(bias[:], a["bias3"]).then_inc(loaded, 16)
            for c in range(C):
                sp.dma_start(w[:, c], a["w3"][:, c * P:(c + 1) * P, :].rearrange("x p n -> p x n")).then_inc(loaded, 16)
            with sp.Fori(0, B) as b:
                sp.wait_ge(x_added, T * b + T)
                sp.dma_start(out[bass.ds(b, 1)].rearrange("a (t p) d -> p (a t) d", p=P), X[:, bass.ds(b * T, T), :]).then_inc(stored, 16)
            sp.wait_ge(stored, 16 * B)

        @block.gpsimd
        def _(pool):
            pool.memset(norm.mhalf[:], -0.5).then_inc(consts, 1)
            pool.iota(count[:], pattern=[[1, EX]], base=0, channel_multiplier=0, allow_small_or_imprecise_dtypes=True).then_inc(consts, 1)
            pool.wait_ge(consts, 2)
            with pool.Fori(0, B) as b:
                norm.gpsimd(pool, b)

        @block.scalar
        def _(act):
            with act.Fori(0, B) as b:
                norm.scalar(act, b)
                act.wait_ge(oh_turned, b + 1)
                act.copy(ohT[:].rearrange("e t q -> e (t q)"), ohp).then_inc(ohT_ready, 1)

        @block.tensor
        def _(pe):
            pe.wait_ge(loaded, 64)
            pe.wait_ge(sign_ready, 1)
            with pe.Fori(0, B) as b:
                norm.tensor(pe, b, ident)
                pe.wait_ge(norm.xnT_ready, b + 1)
                for t in range(T):
                    for c in range(C):
                        mm = pe.matmul(lgp[:, t], norm.xnT[:, c, t * P:(t + 1) * P], sig[:, c, :], start=(c == 0), stop=(c == C - 1))
                mm.then_inc(lg_made, 1)
                for t in range(T):
                    for p in range(PAIRS):
                        pe.wait_ge(y_used, (b * T + t) * PAIRS + p + 1)
                        for c in range(C):
                            mm = pe.matmul(ps[:, 2 + p, :], norm.xnT[:, c, t * P:(t + 1) * P], w[:, c, 2 * p:2 * p + 2, :].rearrange("p e n -> p (e n)"),
                                           start=(c == 0), stop=(c == C - 1))
                        mm.then_inc(y_made, 1)
                    if t == 0:
                        pe.wait_ge(oh_ready, b + 1)
                        for s in range(T):
                            mm = pe.transpose(ohp[:, s * P:(s + 1) * P], oh[:, s], ident[:])
                        mm.then_inc(oh_turned, 1)
                        pe.wait_ge(ohT_ready, b + 1)
                        for s in range(T):
                            mm = pe.matmul(bp[:, s], ohT[:, s, :], bias[:], start=True, stop=True)
                        mm.then_inc(bias_made, 1)

        @block.vector
        def _(dve):
            step = Chain(dve, dve_step)
            dve.sem_inc(y_used, PAIRS)
            dve.wait_ge(loaded, 64)
            dve.wait_ge(consts, 2)
            step(dve.tensor_scalar(below[:], sig[:], 0.0, None, ALU.is_lt))
            step(dve.tensor_scalar(sig[:], sig[:], 0.0, None, ALU.is_gt))
            dve.tensor_tensor(sig[:], sig[:], below[:], ALU.subtract).then_inc(sign_ready, 1)
            with dve.Fori(0, B) as b:
                step.restart()
                tile = lambda t: row_tile(X, b * T + t)
                norm.vector(dve, step, tile, b)
                dve.wait_ge(lg_made, b + 1)
                step(dve.tensor_copy(lg[:], lgp))
                argmax_row(dve, step, lg, best, idx, idxf, oh, count)
                dve.sem_inc(oh_ready, 1)
                dve.wait_ge(bias_made, b + 1)
                for t in range(T):
                    step(dve.tensor_tensor(y[:], tile(t), bp[:, t], ALU.add))
                    for x in range(EX):
                        if x % 2 == 0:
                            dve.wait_ge(y_made, (b * T + t) * PAIRS + x // 2 + 1)
                        ins = dve.scalar_tensor_tensor(out=tile(t) if x == EX - 1 else y[:], in0=pairs(x // 2)[:, x % 2], scalar=oh[:, t, x:x + 1], in1=y[:],
                                                       op0=ALU.mult, op1=ALU.add)
                        if x == EX - 1:
                            ins.then_inc(x_added, 1)
                            dve.wait_ge(x_added, b * T + t + 1)
                        else:
                            step(ins)
                        if x % 2:
                            dve.sem_inc(y_used, 1)


def program(nc, a, out, qscratch, last=9):
    with ExitStack() as ctx:
        X = ctx.enter_context(nc.sbuf_tensor("X", [P, ROWS, E], F32))
        ident = ctx.enter_context(nc.sbuf_tensor("ident", [P, P], F32))
        identb = ctx.enter_context(nc.sbuf_tensor("identb", [P, P], BF16))
        W2 = ctx.enter_context(nc.sbuf_tensor("W2", [P, C, E], F32))
        ps = ctx.enter_context(nc.psum_tensor("ps", [P, 8, 512], F32))
        prepare(nc, a, X, ps, ident, identb, W2, qscratch)
        cross_attention(nc, a, X, ps, ident, identb, W2, qscratch)
        if last >= 2:
            self_attention(nc, a, X, ps, ident)
        if last >= 3:
            experts(nc, a, X, ps, ident)
        if last >= 4:
            context_attention(nc, a, X, ps, ident)
        if last >= 5:
            state_space(nc, a, X, ps, ident)
        if last >= 6:
            routed(nc, a, X, ps, ident, out)
            return
        stored = ctx.enter_context(nc.semaphore("stored"))
        with nc.Block() as block:
            @block.sync
            def _(sp):
                sp.dma_start(out.rearrange("b s d -> (b s) d").rearrange("(r p) d -> p r d", p=P), X[:]).then_inc(stored, 16)
                sp.wait_ge(stored, 16)


def both(i, name):
    import numpy as np
    return [np.asarray(i[f"L1_attn_{d}_{name}"]) for d in ("fwd", "bwd")]


def layouts(i):
    import numpy as np
    c = lambda v: np.ascontiguousarray(v)
    ctx = np.asarray(i["ctx_1024"])
    return {
        "x": c(i["x"]),
        "mask": c(np.asarray(i["mask_Bx1xSxS2_if1"]).reshape(B, S, SK)),
        "ctxT": c(ctx.transpose(0, 2, 1).reshape(B * C, P, SK)),
        "ctxV": c(ctx.reshape(B, KT, P, H // HG, HG * D).transpose(0, 3, 2, 1, 4).reshape(B * H // HG, P, KT * HG * D)),
        "wq0": c(i["L0_xattn_Wq"]), "wk0": c(i["L0_xattn_Wk"]), "wv0": c(i["L0_xattn_Wv"]),
        "wo0T": c(np.asarray(i["L0_xattn_Wo"]).T), "bo0": c(i["L0_xattn_bo"]),
        "wq1T": c(np.asarray(i["L0_attn_Wq"]).T), "wk1T": c(np.asarray(i["L0_attn_Wk"]).T),
        "wv1T": c(np.asarray(i["L0_attn_Wv"]).T), "wo1T": c(np.asarray(i["L0_attn_Wo"]).T),
        "bq1": c(np.asarray(i["L0_attn_bq"]).reshape(H // HG, HG, D).transpose(1, 2, 0)),
        "bk1": c(np.asarray(i["L0_attn_bk"]).reshape(H // HG, HG, D).transpose(1, 2, 0)),
        "wg": c(i["L0_ffn_Wg"]), "we": c(i["L0_ffn_We"]), "be": c(i["L0_ffn_be"]), "ctx": c(ctx),
        "wq2": c(i["L1_xattn_w_q"]), "wk2": c(i["L1_xattn_w_k"]), "wv2T": c(np.asarray(i["L1_xattn_w_v"]).T),
        "nw": c(i["L1_attn_norm_w"]), "nb": c(i["L1_attn_norm_b"]),
        "win": c(np.stack([w.T for w in both(i, "in_proj_w")], 1)),
        "cw": c(np.stack([w.reshape(C, P, TAPS).transpose(1, 0, 2) for w in both(i, "conv_w")], 1)),
        "wx": c(np.stack([np.concatenate([w[RANK:], w[:RANK]]).T.reshape(C, P, -1).transpose(1, 0, 2) for w in both(i, "x_proj_w")], 1)),
        "wdt": c(np.stack([w.T for w in both(i, "dt_proj_w")], 1)),
        "cb": c(np.stack([w.reshape(C, P).T for w in both(i, "conv_b")], 1)),
        "bdt": c(np.stack([w.reshape(C, P).T for w in both(i, "dt_proj_b")], 1)),
        "dcol": c(np.stack([w.reshape(C, P).T for w in both(i, "D")], 1)),
        "alog": c(np.stack([w.reshape(C, P, N_STATE).transpose(1, 0, 2) for w in both(i, "A_log")], 1)),
        "wout": c(np.stack([w.T.reshape(C, P, P).transpose(1, 0, 2) for w in both(i, "out_proj_w")], 1)),
        "sigT": c(np.asarray(i["L1_ffn_tile_sigs"]).T), "w3": c(i["L1_ffn_W"]), "bias3": c(i["L1_ffn_b"]),
        "bv1": c(i["L0_attn_bv"]), "bo1": c(i["L0_attn_bo"]),
    }


def kernel(**inputs):
    import concourse.bacc as bacc
    from concourse.bass_utils import run_bass_kernel_spmd

    nc = bacc.Bacc("TRN2", target_bir_lowering=False, num_devices=1)
    arrays = layouts(inputs)
    a = {n: nc.dram_tensor(n, v.shape, mybir.dt.from_np(v.dtype), kind="ExternalInput").ap() for n, v in arrays.items()}
    out = nc.dram_tensor("out", (B, S, E), F32, kind="ExternalOutput").ap()
    qscratch = nc.dram_tensor("qscratch", (NB, B, C, P, S), BF16, kind="Internal").ap()
    program(nc, a, out, qscratch)
    r = run_bass_kernel_spmd(nc, [arrays], core_ids=[0])
    return r.results[0]["out"]
```

```python
from contextlib import ExitStack

import concourse.bass as bass
from concourse import mybir

ALU = mybir.AluOpType
ACT = mybir.ActivationFunctionType
AX = mybir.AxisListType
F32 = mybir.dt.float32
BF16 = mybir.dt.bfloat16
I32 = mybir.dt.int32
U32 = mybir.dt.uint32

P = 128
B, S, E, SK = 4, 256, 256, 4096
H, D = 16, 16
T = S // P
ROWS = B * T
C = E // P
KT = SK // P
HG = 4
GC = H // HG // C
RING = 3
PARTS = [0, 0, 0, 1, 1, 2]
QPARTS = [0, 1, 2, 0, 1, 0]
NB = len(PARTS)
KR = NB * D
NEG = -1.0e20
MC = SK // 2
BOUND = 64.0
LOW = -3.0e38
EPS = 1e-5
TOPK = 64
EX = 8
CAP = 4 * 256 // EX
VP = D + 1


class Chain:

    def __init__(self, eng, sem):
        self.eng, self.sem, self.n = eng, sem, 0

    def hold(self):
        self.n += 1
        self.eng.sem_inc(self.sem, 1)

    def restart(self):
        self.hold()
        self.eng.sem_clear(self.sem)
        self.n = 0

    def __call__(self, ins):
        self.n += 1
        ins.then_inc(self.sem, 1)
        self.eng.wait_ge(self.sem, self.n)


def row_tile(X, t):
    return X[:, bass.ds(t, 1), :].rearrange("p a d -> p (a d)")


def scope(nc, stage):
    ctx = ExitStack()
    sems = []

    def clear():
        nc.clear_and_free_semaphores(sems)
        nc.all_engine_barrier()

    ctx.callback(clear)
    sb = lambda name, shape, dt=F32: ctx.enter_context(nc.sbuf_tensor(f"{stage}_{name}", shape, dt))

    def sem(name):
        sems.append(nc.alloc_semaphore(f"{stage}_{name}"))
        return sems[-1]

    return ctx, sb, sem


def prepare(nc, a, X, ps, ident, identb, W2, qmax, qscratch):
    ctx, sb, sem = scope(nc, "prepare")
    with ctx:
        w16 = sb("w16", [D, 2, D])
        m16 = sb("m16", [D, D])
        Mbd = sb("Mbd", [P, P])
        Vbd = sb("Vbd", [P, P])
        woT = sb("woT", [P, C, E])
        bo = sb("bo", [P, E])
        stats = sb("stats", [P, 6])
        mv = sb("mv", [P, 2])
        ve = sb("ve", [P, 1])
        rstd = sb("rstd", [P, 1])
        mhalf = sb("mhalf", [P, 1])
        xn = sb("xn", [P, E])
        xnT = sb("xnT", [P, C, P])
        qrest = sb("qrest", [P, C, P])
        qparts = sb("qparts", [P, 3, C, ROWS, P], BF16)

        x_loaded, w_loaded, zeroed = sem("x_loaded"), sem("w_loaded"), sem("zeroed")
        m_made, m_copied, m_placed = sem("m_made"), sem("m_copied"), sem("m_placed")
        v_placed, w2_made, ident_ready = sem("v_placed"), sem("w2_made"), sem("ident_ready")
        var_ready, rstd_ready, xn_ready = sem("var_ready"), sem("rstd_ready"), sem("xn_ready")
        xn_turned, xnT_ready, q_ready, q_split = sem("xn_turned"), sem("xnT_ready"), sem("q_ready"), sem("q_split")
        q_stored, dve_step, pool_step = sem("q_stored"), sem("dve_step"), sem("pool_step")
        w2_copied, bo_added = sem("w2_copied"), sem("bo_added")

        block = ctx.enter_context(nc.Block())

        @block.sync
        def _(sp):
            sp.dma_start(X[:], a["x"].rearrange("b s d -> (b s) d").rearrange("(r p) d -> p r d", p=P)).then_inc(x_loaded, 16)
            sp.dma_start(w16[:, 0, :], a["wq0"]).then_inc(w_loaded, 16)
            sp.dma_start(w16[:, 1, :], a["wk0"]).then_inc(w_loaded, 16)
            sp.dma_start(woT[:], a["wo0T"].rearrange("(c p) n -> p c n", p=P)).then_inc(w_loaded, 16)
            sp.dma_start(bo[:], a["bo0"].partition_broadcast(P)).then_inc(w_loaded, 16)
            sp.wait_ge(zeroed, 2)
            for h in range(P // D):
                sp.dma_start(Vbd[h * D:(h + 1) * D, h * D:(h + 1) * D], a["wv0"]).then_inc(v_placed, 16)
            sp.wait_ge(m_copied, 1)
            for h in range(P // D):
                sp.dma_start(Mbd[h * D:(h + 1) * D, h * D:(h + 1) * D], m16[:]).then_inc(m_placed, 16)
            sp.wait_ge(q_split, ROWS)
            for n, part in enumerate(QPARTS):
                for c in range(C):
                    sp.dma_start(qscratch[n, :, c].rearrange("b p q -> p b q"),
                                 qparts[:, part, c].rearrange("p (b t) q -> p b (t q)", t=T)).then_inc(q_stored, 16)
            sp.wait_ge(q_stored, 16 * NB * C)

        @block.gpsimd
        def _(pool):
            pool.memset(Mbd[:], 0.0).then_inc(zeroed, 1)
            pool.memset(Vbd[:], 0.0).then_inc(zeroed, 1)
            pool.memset(ident[:], 0.0).then_inc(pool_step, 1)
            pool.memset(identb[:], 0.0).then_inc(pool_step, 1)
            pool.memset(mhalf[:], -0.5).then_inc(pool_step, 1)
            pool.wait_ge(pool_step, 3)
            for t in (ident, identb):
                pool.affine_select(out=t[:], in_=t[:], compare_op=ALU.not_equal, fill=1.0, base=0,
                                   pattern=[[-1, P]], channel_multiplier=1).then_inc(ident_ready, 1)
            with pool.Fori(0, ROWS) as t:
                pool.wait_ge(var_ready, t + 1)
                pool.tensor_tensor(rstd[:], ve[:], mhalf[:], ALU.pow).then_inc(rstd_ready, 1)

        @block.scalar
        def _(act):
            with act.Fori(0, ROWS) as t:
                act.wait_ge(xn_turned, t + 1)
                act.copy(xnT[:], ps[:, 0, 0:C * P].rearrange("p (c q) -> p c q", c=C)).then_inc(xnT_ready, 1)

        @block.tensor
        def _(pe):
            pe.wait_ge(w_loaded, 64)
            pe.matmul(ps[0:D, 2, 0:D], w16[:, 0, :], w16[:, 1, :], start=True, stop=True).then_inc(m_made, 1)
            pe.wait_ge(v_placed, 16 * (P // D))
            for c in range(C):
                pe.matmul(ps[:, 3, c * E:(c + 1) * E], Vbd[:], woT[:, c, :], start=True, stop=True).then_inc(w2_made, 1)
            pe.wait_ge(ident_ready, 2)
            pe.wait_ge(m_placed, 16 * (P // D))
            with pe.Fori(0, ROWS) as t:
                pe.wait_ge(xn_ready, t + 1)
                for c in range(C):
                    mm = pe.transpose(ps[:, 0, c * P:(c + 1) * P], xn[:, c * P:(c + 1) * P], ident[:])
                mm.then_inc(xn_turned, 1)
                pe.wait_ge(xnT_ready, t + 1)
                for c in range(C):
                    mm = pe.matmul(ps[:, 1, c * P:(c + 1) * P], Mbd[:], xnT[:, c, :], start=True, stop=True)
                mm.then_inc(q_ready, 1)

        @block.vector
        def _(dve):
            step = Chain(dve, dve_step)
            dve.wait_ge(m_made, 1)
            dve.tensor_copy(m16[:], ps[0:D, 2, 0:D]).then_inc(m_copied, 1)
            dve.wait_ge(w2_made, C)
            dve.tensor_copy(W2[:], ps[:, 3, :].rearrange("p (c n) -> p c n", c=C)).then_inc(w2_copied, 1)
            dve.wait_ge(x_loaded, 16)
            with dve.Fori(0, ROWS) as t:
                step.restart()
                x_t = row_tile(X, t)
                step(dve.bn_stats(stats[:], x_t))
                step(dve.bn_aggr(mv[:], stats[:]))
                dve.tensor_scalar(ve[:], mv[:, 1:2], EPS, None, ALU.add).then_inc(var_ready, 1)
                dve.wait_ge(rstd_ready, t + 1)
                dve.tensor_scalar(xn[:], x_t, mv[:, 0:1], rstd[:], ALU.subtract, ALU.mult).then_inc(xn_ready, 1)
                dve.wait_ge(q_ready, t + 1)
                q = ps[:, 1, 0:C * P].rearrange("p (c q) -> p c q", c=C)
                part = lambda i: qparts[:, i, :, bass.ds(t, 1), :].rearrange("p c a q -> p c (a q)")
                step(dve.tensor_reduce(qmax[:, bass.ds(t, 1)], ps[:, 1, 0:C * P], AX.X, ALU.max, apply_absolute_value=True))
                step(dve.tensor_copy(part(0), q))
                step(dve.tensor_tensor(qrest[:], q, part(0), ALU.subtract))
                step(dve.tensor_copy(part(1), qrest[:]))
                dve.tensor_tensor(part(2), qrest[:], part(1), ALU.subtract).then_inc(q_split, 1)
            step.restart()
            for t in range(ROWS):
                dve.tensor_tensor(X[:, t, :], X[:, t, :], bo[:], ALU.add).then_inc(bo_added, 1)
            dve.wait_ge(bo_added, ROWS)
            dve.wait_ge(w2_copied, 1)


def cross_attention(nc, a, X, ps, ident, identb, W2, qmax, qscratch):
    ctx, sb, sem = scope(nc, "cross")
    with ctx:
        stage = sb("stage", [P, SK])
        kparts = sb("kparts", [P, 3, SK], BF16)
        kstack = [sb(f"kstack{i}", [P, HG, SK], BF16) for i in range(GC)]
        qstack = [sb(f"qstack{i}", [P, HG, S], BF16) for i in range(GC)]
        mstage = sb("mstage", [P, MC], I32)
        maskb = sb("maskb", [P, 2 * T, SK], BF16)
        vstage = sb("vstage", [P, KT, HG, D])
        values = [sb(f"values{i}", [P, KT, HG * VP + 32 - VP]) for i in range(GC)]
        probs = [sb(f"probs{i}", [P, HG, S]) for i in range(RING)]
        maxima = sb("maxima", [P, HG * T, 4])
        shift = sb("shift", [P, HG * T])
        rest = sb("rest", [P, 2, HG * T])
        shiftp = sb("shiftp", [P, HG * T, 3], BF16)
        accT = sb("accT", [P, S])
        recip = sb("recip", [P, T, HG])
        heads = sb("heads", [P, T, P])
        headsT = sb("headsT", [P, S])
        bounds = sb("bounds", [P, 3])
        widest = sb("widest", [P, 3])
        least = sb("least", [P, 1])
        general = sb("general", [P, 1], I32)

        ctx_loaded, mask_loaded, v_loaded = sem("ctx_loaded"), sem("mask_loaded"), sem("v_loaded")
        kparts_ready, mask_ready, values_ready = sem("kparts_ready"), sem("mask_ready"), sem("values_ready")
        v_free = sem("v_free")
        stack_loaded, stack_free = [sem(f"stack_loaded{g}") for g in range(GC)], sem("stack_free")
        bounds_ready, general_ready, pool_step = sem("bounds_ready"), sem("general_ready"), sem("pool_step")
        way_read = sem("way_read")
        natural_ready, natural_reduced = sem("natural_ready"), sem("natural_reduced")
        shift_ready, shift_turned, shift_placed = sem("shift_ready"), sem("shift_turned"), sem("shift_placed")
        scores_ready, exp_done, pv_done = sem("scores_ready"), sem("exp_done"), sem("pv_done")
        acc_copied, acc_turned, heads_ready = sem("acc_copied"), sem("acc_turned"), sem("heads_ready")
        heads_turned, headsT_ready, proj_ready, x_added = (
            sem("heads_turned"), sem("headsT_ready"), sem("proj_ready"), sem("x_added"))
        passed = [sem(f"passed_{e}") for e in ("act", "pe", "sp", "pool")]
        dve_step, ones_ready = sem("dve_step"), sem("ones_ready")

        slot = lambda m: ps[:, 2 * (m % RING):2 * (m % RING) + 2, :]
        acc = lambda g: ps[:, 6, g * S:(g + 1) * S]
        PER = HG * NB + NB
        NAT = HG * T * 4
        PIECES = SK // MC
        FIRST = [RING - 1, RING, RING - 2]
        TURN, HEADS, PROJECT = 6, 10, 14

        block = ctx.enter_context(nc.Block())

        @block.sync
        def _(sp):
            sp.dma_start(stage[:], a["ctxT"][0]).then_inc(ctx_loaded, 16)
            with sp.Fori(0, B) as b:
                with sp.Fori(0, C) as c:
                    i = b * C + c
                    sp.wait_ge(kparts_ready, i + 1)
                    sp.sem_inc(passed[2], 1)
                    with sp.If(i < B * C - 1):
                        sp.dma_start(stage[:], a["ctxT"][bass.ds((i + 1) % (B * C), 1)].rearrange("a p k -> p (a k)")).then_inc(ctx_loaded, 16)
                    for g in range(GC):
                        sp.wait_ge(stack_free, i * GC + g + 1)
                        for j in range(HG):
                            r = (g * HG + j) * D
                            for n, part in enumerate(PARTS):
                                sp.dma_start(kstack[g][n * D:(n + 1) * D, j, :], kparts[r:r + D, part, :]).then_inc(stack_loaded[g], 16)
                        for n in range(NB):
                            src = qscratch[n, bass.ds(b, 1), bass.ds(c, 1), g * HG * D:(g + 1) * HG * D, :]
                            sp.dma_start(qstack[g][n * D:(n + 1) * D, :, :],
                                         src.rearrange("a c (j d) q -> (a c j) d q", d=D).rearrange("j d q -> d j q")).then_inc(stack_loaded[g], 16)

        @block.gpsimd
        def _(pool):
            step = Chain(pool, pool_step)

            def load_values(n):
                pool.wait_ge(v_free, n + 1)
                pool.dma_start(vstage[:], a["ctxV"][bass.ds(n % (B * H // HG), 1)].rearrange("a p (k j d) -> p (a k) j d", j=HG, d=D)).then_inc(v_loaded, 16)

            def load_mask(b, t, piece, n):
                pool.wait_ge(mask_ready, n + 1)
                pool.dma_start(mstage[:], a["mask"][bass.ds(b, 1), bass.ds(t * P, P), piece * MC:(piece + 1) * MC]
                               .rearrange("a p k -> p (a k)")).then_inc(mask_loaded, 16)

            def decide(i):
                pool.wait_ge(bounds_ready, i + 1)
                step.restart()
                step(pool.partition_all_reduce(widest[:], bounds[:], P, bass.bass_isa.ReduceOp.absmax))
                step(pool.tensor_tensor(widest[:, 0:1], widest[:, 0:1], widest[:, 1:2], ALU.mult))
                step(pool.tensor_tensor(widest[:, 0:1], widest[:, 0:1], widest[:, 2:3], ALU.add))
                pool.wait_ge(way_read, 3 * i + 3)
                step.hold()
                pool.tensor_scalar(general[:], widest[:, 0:1], BOUND, None, ALU.is_gt).then_inc(general_ready, 1)

            load_values(0)
            with pool.Fori(0, T) as t:
                for piece in range(PIECES):
                    load_mask(0, t, piece, t * PIECES + piece)
            with pool.Fori(0, B * C) as i:
                decide(i)
                load_values(2 * i + 1)
                with pool.If(i < (B - 1) * C):
                    b, t = (i + C) // C % B, i % C
                    for piece in range(PIECES):
                        load_mask(b, t, piece, (T + i) * PIECES + piece)
                pool.sem_inc(passed[3], 1)
                with pool.If(i < B * C - 1):
                    load_values(2 * i + 2)

        @block.scalar
        def _(act):
            def exps(n, k, m):
                act.wait_ge(scores_ready, n * KT + k + 1)
                act.wait_ge(pv_done, n * KT + (FIRST[m % RING] if m < RING else m + 1))
                act.activation(probs[m % RING][:], slot(m).rearrange("p a (h q) -> p (a h) q", h=2), ACT.Exp,
                               scale=1.0 / 16.0).then_inc(exp_done, 1)

            def take_sums(n, g):
                act.wait_ge(pv_done, (n + 1) * KT + RING)
                act.wait_ge(acc_turned, n + 1)
                act.copy(accT[:], acc(g)).then_inc(acc_copied, 1)

            def take_heads(i):
                act.wait_ge(heads_turned, i + 1)
                act.copy(headsT[:], ps[:, 7, 0:S]).then_inc(headsT_ready, 1)

            act.sem_inc(exp_done, RING)
            act.sem_inc(acc_copied, 2)
            with act.Fori(0, B * C) as i:
                act.wait_ge(general_ready, i + 1)
                act.sem_inc(passed[0], 1)
                way = act.value_load(general[0:1, 0:1])
                act.sem_inc(way_read, 1)
                with act.If(way == 1):
                    with act.If(i > 0):
                        take_heads(i - 1)
                    for g in range(GC):
                        n = i * GC + g
                        act.wait_ge(shift_turned, n + 1)
                        act.copy(qstack[g][KR:KR + 3, :, :], ps[:].bitcast(BF16)[KR:KR + 3, 7, :]
                                 .rearrange("p (j q) -> p j q", j=HG)).then_inc(shift_placed, 1)
                        for k in range(KT):
                            exps(n, k, k)
                        take_sums(n, g)
                with act.Else():
                    for m in range(GC * KT):
                        exps(i * GC, m, m)
                        if m % KT == 0 and m:
                            take_sums(i * GC + m // KT - 1, m // KT - 1)
                        if m == HEADS:
                            act.sem_inc(shift_placed, GC)
                            with act.If(i > 0):
                                take_heads(i - 1)
                    take_sums(i * GC + GC - 1, GC - 1)
            take_heads(B * C - 1)

        @block.tensor
        def _(pe):
            def turn(n, i):
                pe.wait_ge(acc_copied, n + 3)
                pe.wait_ge(heads_ready, n + 1)
                pe.wait_ge(x_added, i + 1)
                for t in range(T):
                    mm = pe.transpose(ps[:, 7, t * P:(t + 1) * P], accT[:, t * P:(t + 1) * P], ident[:])
                mm.then_inc(acc_turned, 1)

            def turn_heads(i):
                pe.wait_ge(heads_ready, i * GC + GC + 1)
                for t in range(T):
                    mm = pe.transpose(ps[:, 7, t * P:(t + 1) * P], heads[:, t, :], ident[:])
                mm.then_inc(heads_turned, 1)

            def project(i, c):
                pe.wait_ge(headsT_ready, i + 1)
                pe.sem_inc(passed[1], 1)
                for t in range(T):
                    mm = pe.matmul(ps[:, 7, t * E:(t + 1) * E], headsT[:, t * P:(t + 1) * P],
                                   W2[:, bass.ds(c, 1), :].rearrange("p a n -> p (a n)"), start=True, stop=True)
                mm.then_inc(proj_ready, 1)

            def scores(g, k, m, rows, last):
                for j in range(HG):
                    mm = pe.matmul(slot(m)[:, j // 2, (j % 2) * S:(j % 2 + 1) * S], kstack[g][0:rows, j, k * P:(k + 1) * P],
                                   qstack[g][0:rows, j, :], start=(j % 2 == 0), stop=last, skip_group_check=True)
                return mm

            def products(n, g, k, m, base):
                if k == 0:
                    pe.wait_ge(values_ready, n + 1)
                    pe.wait_ge(acc_copied, n + 2)
                pe.wait_ge(exp_done, base + RING + m + 1)
                for j in range(HG):
                    mm = pe.matmul(acc(g)[32 * j:32 * j + 32, :], values[g][:, k, j * VP:j * VP + 32], probs[m % RING][:, j, :],
                                   start=(k == 0), stop=(k == KT - 1), skip_group_check=True)
                mm.then_inc(pv_done, 1)

            def release(n):
                pe.wait_ge(scores_ready, (n + 1) * KT)
                pe.sem_inc(stack_free, 1)

            def masked(b2, add_mask):
                with pe.If(b2 == 0):
                    add_mask(0)
                with pe.Else():
                    add_mask(T)

            def general_half(b2, i, c):
                with pe.If(i > 0):
                    turn(i * GC - 1, i - 1)
                    turn_heads(i - 1)
                    project(i - 1, 1 - c)
                for g in range(GC):
                    n = i * GC + g
                    pe.wait_ge(stack_loaded[g], (i + 1) * (16 * PER))
                    for u in range(NAT):
                        j, t, part = u // (4 * T), u // 4 % T, u % 4
                        if u < RING:
                            pe.wait_ge(exp_done, n * KT + FIRST[u])
                        else:
                            pe.wait_ge(natural_reduced, n * NAT + u - RING + 1)
                        for w in range(2):
                            k0 = part * 1024 + w * 512
                            pe.matmul(slot(u)[:, w, :], qstack[g][0:KR, j, t * P:(t + 1) * P], kstack[g][0:KR, j, k0:k0 + 512],
                                      start=True, stop=False)

                        def add_mask(first):
                            for w in range(2):
                                k0 = part * 1024 + w * 512
                                mm = pe.matmul(slot(u)[:, w, :], identb[:], maskb[:, first + t, k0:k0 + 512], start=False, stop=True)
                            mm.then_inc(natural_ready, 1)

                        masked(b2, add_mask)
                    pe.wait_ge(shift_ready, n + 1)
                    pe.wait_ge(heads_ready, n + 1)
                    pe.wait_ge(x_added, i + 1)
                    for u in range(HG * T):
                        mm = pe.transpose(ps[:].bitcast(BF16)[KR:KR + 3, 7, u * P:(u + 1) * P], shiftp[:, u, :], identb[:])
                    mm.then_inc(shift_turned, 1)
                    pe.wait_ge(shift_placed, n + 1)
                    pe.wait_ge(natural_reduced, (n + 1) * NAT)
                    for k in range(KT + 2):
                        if k < KT:
                            if k >= RING:
                                pe.wait_ge(exp_done, n * KT + k + 1)
                            scores(g, k, k, KR + 3, False)

                            def add_mask(first):
                                for w in range(2):
                                    for t in range(T):
                                        mm = pe.matmul(slot(k)[:, w, :].rearrange("p (h t q) -> p h t q", h=2, t=T)[:, :, t, :],
                                                       maskb[:, first + t, k * P:(k + 1) * P],
                                                       identb[:].unsqueeze(1).to_broadcast([P, 2, P]), start=False,
                                                       stop=(t == T - 1), skip_group_check=True)
                                mm.then_inc(scores_ready, 1)

                            masked(b2, add_mask)
                        else:
                            if k == KT:
                                release(n)
                        if k >= 2:
                            products(n, g, k - 2, k - 2, n * KT)
                    if g < GC - 1:
                        turn(n, i)

            def plain_half(i, c):
                pe.sem_inc(natural_ready, GC * NAT)
                pe.sem_inc(shift_turned, GC)
                n = i * GC
                for m in range(GC * KT + 2):
                    g, k = m // KT, m % KT
                    if m < GC * KT:
                        if k == 0:
                            pe.wait_ge(stack_loaded[g], (i + 1) * (16 * PER))
                        pe.wait_ge(exp_done, n * KT + (FIRST[m] if m < RING else m + 1))
                        scores(g, k, m, KR, True).then_inc(scores_ready, 1)
                    if m == TURN:
                        with pe.If(i > 0):
                            turn(n - 1, i - 1)
                    if m == HEADS:
                        with pe.If(i > 0):
                            turn_heads(i - 1)
                    if m == PROJECT:
                        with pe.If(i > 0):
                            project(i - 1, 1 - c)
                    if g and k == 1:
                        release(n + g - 1)
                    if m > KT and k == TURN:
                        turn(n + g - 1, i)
                    if m >= 2:
                        products(n + (m - 2) // KT, (m - 2) // KT, (m - 2) % KT, m - 2, n * KT)

            pe.sem_inc(pv_done, RING)
            pe.sem_inc(stack_free, 2)
            pe.sem_inc(acc_turned, 1)
            pe.wait_ge(ones_ready, 2)
            with pe.Fori(0, B // 2) as bb:
                with pe.Fori(0, 2) as b2:
                    with pe.Fori(0, C) as c:
                        i = (bb * 2 + b2) * C + c
                        pe.wait_ge(general_ready, i + 1)
                        pe.sem_inc(passed[1], 1)
                        way = pe.value_load(general[0:1, 0:1])
                        pe.sem_inc(way_read, 1)
                        with pe.If(way == 1):
                            general_half(b2, i, c)
                        with pe.Else():
                            plain_half(i, c)
            turn(B * H // HG - 1, B * C - 1)
            turn_heads(B * C - 1)
            project(B * C - 1, C - 1)

        @block.vector
        def _(dve):
            step = Chain(dve, dve_step)

            def place_values(n, g):
                dve.wait_ge(v_loaded, (n + 1) * 16)
                dve.wait_ge(acc_copied, n + 1)
                step(dve.tensor_copy(values[g][:, :, 0:HG * VP].rearrange("p k (j v) -> p k j v", v=VP)[:, :, :, 0:D], vstage[:]))
                dve.sem_inc(v_free, 1)
                dve.sem_inc(values_ready, 1)

            def place_mask(tile, piece, n):
                dve.wait_ge(mask_loaded, (n + 1) * 16)
                step.hold()
                part = maskb[:, bass.ds(tile, 1), piece * MC:(piece + 1) * MC].rearrange("p a k -> p (a k)")
                step(dve.tensor_scalar(part, mstage[:], 0.0, NEG, ALU.is_equal, ALU.mult))
                dve.sem_inc(mask_ready, 1)
                step(dve.tensor_reduce(least[:], part, AX.X, ALU.min))
                step(dve.tensor_tensor(bounds[:, 2:3], bounds[:, 2:3], least[:], ALU.min))

            def split(i):
                dve.wait_ge(ctx_loaded, (i + 1) * 16)
                step(dve.tensor_reduce(bounds[:, 0:1], stage[:], AX.X, ALU.max, apply_absolute_value=True))
                dve.sem_inc(bounds_ready, 1)
                step(dve.tensor_copy(kparts[:, 0, :], stage[:]))
                step(dve.tensor_tensor(stage[:], stage[:], kparts[:, 0, :], ALU.subtract))
                step(dve.tensor_copy(kparts[:, 1, :], stage[:]))
                step(dve.tensor_tensor(kparts[:, 2, :], stage[:], kparts[:, 1, :], ALU.subtract))
                dve.sem_inc(kparts_ready, 1)

            def divide(n, g):
                dve.wait_ge(acc_turned, n + 2)
                turned = ps[:, 7, 0:S].rearrange("p (t j v) -> p t j v", t=T, j=HG)
                step(dve.reciprocal(recip[:], turned[:, :, :, D]))
                dve.tensor_tensor(heads[:, :, g * HG * D:(g + 1) * HG * D].rearrange("p t (j d) -> p t j d", d=D), turned[:, :, :, 0:D],
                                  recip[:].unsqueeze(3).to_broadcast([P, T, HG, D]), ALU.mult).then_inc(heads_ready, 1)

            def add(i, tile):
                dve.wait_ge(proj_ready, i + 1)
                step.hold()
                for t in range(T):
                    x_t = row_tile(X, tile + t)
                    ins = dve.tensor_tensor(x_t, x_t, ps[:, 7, t * E:(t + 1) * E], ALU.add)
                    if t < T - 1:
                        step(ins)
                ins.then_inc(x_added, 1)

            def reduce_natural(n):
                for u in range(NAT):
                    dve.wait_ge(natural_ready, n * NAT + u + 1)
                    dve.reduce_max(maxima[:, u // 4, u % 4:u % 4 + 1], slot(u), AX.XY).then_inc(natural_reduced, 1)
                dve.wait_ge(natural_reduced, (n + 1) * NAT)
                step(dve.reduce_max(shift[:], maxima[:], AX.X))
                step(dve.tensor_scalar(rest[:, 0, :], shift[:], -1.0, None, ALU.mult))
                step(dve.tensor_copy(shiftp[:, :, 0], rest[:, 0, :]))
                step(dve.tensor_tensor(rest[:, 1, :], rest[:, 0, :], shiftp[:, :, 0], ALU.subtract))
                step(dve.tensor_copy(shiftp[:, :, 1], rest[:, 1, :]))
                dve.tensor_tensor(shiftp[:, :, 2], rest[:, 1, :], shiftp[:, :, 1], ALU.subtract).then_inc(shift_ready, 1)

            def maxima_of(n, way):
                step.hold()
                with dve.If(way == 1):
                    first = step.n
                    reduce_natural(n)
                    used = step.n - first
                with dve.Else():
                    dve.sem_inc(natural_reduced, NAT)
                    dve.sem_inc(shift_ready, 1)
                    dve.sem_inc(dve_step, used)

            for i in range(GC):
                dve.memset(values[i][:], 1.0).then_inc(dve_step, 1)
                dve.memset(kstack[i][96:128, :, :], 1.0).then_inc(ones_ready, 1)
            dve.memset(bounds[:, 2:3], 0.0).then_inc(dve_step, 1)
            step.n = 3
            dve.sem_inc(v_free, 1)
            dve.sem_inc(mask_ready, 1)
            dve.sem_inc(way_read, 3)
            dve.sem_inc(heads_ready, 1)
            dve.sem_inc(x_added, 1)
            dve.wait_ge(dve_step, 3)
            step(dve.reduce_max(bounds[:, 1:2], qmax[:], AX.X))
            place_values(0, 0)
            for t in range(T):
                for piece in range(PIECES):
                    place_mask(t, piece, t * PIECES + piece)
            split(0)
            with dve.Fori(0, B // 2) as bb:
                with dve.Fori(0, 2) as b2:
                    with dve.Fori(0, C) as c:
                        b = bb * 2 + b2
                        i = b * C + c
                        n = i * GC
                        step.restart()
                        dve.wait_ge(general_ready, i + 1)
                        step.hold()
                        way = dve.value_load(general[0:1, 0:1])
                        dve.sem_inc(way_read, 1)
                        with dve.If(i > 0):
                            divide(n - 1, GC - 1)
                            add(i - 1, (b + c + B - 1) % B * T)
                            step.restart()
                        with dve.Else():
                            step.restart()
                        place_values(n + 1, 1)
                        maxima_of(n, way)
                        step.restart()
                        with dve.If(b < B - 1):
                            for piece in range(PIECES):
                                place_mask((1 - b2) * T + c, piece, (T + i) * PIECES + piece)
                            step.restart()
                        with dve.Else():
                            step.restart()
                        dve.wait_ge(stack_loaded[1], (i + 1) * (16 * PER))
                        step.hold()
                        with dve.If(i < B * C - 1):
                            split(i + 1)
                            step.restart()
                        with dve.Else():
                            step.restart()
                        divide(n, 0)
                        dve.wait_ge(heads_ready, n + 2)
                        step.restart()
                        with dve.If(i < B * C - 1):
                            place_values(n + 2, 0)
                            step.restart()
                        with dve.Else():
                            step.restart()
                        maxima_of(n + 1, way)
            divide(B * H // HG - 1, GC - 1)
            add(B * C - 1, ROWS - T)
            dve.wait_ge(x_added, B * C + 1)


def self_attention(nc, a, X, ps, ident):
    ctx, sb, sem = scope(nc, "self")
    with ctx:
        wqT = sb("wqT", [P, C, HG, HG, 32])
        wkT = sb("wkT", [P, C, HG, HG, 32])
        wvT = sb("wvT", [P, C, E])
        woT = sb("woT", [P, C, E])
        bq = sb("bq", [P, HG])
        bk = sb("bk", [P, HG])
        bv = sb("bv", [P, E])
        bo = sb("bo", [P, E])
        stats = sb("stats", [P, T, 6])
        mv = sb("mv", [P, T, 2])
        ve = sb("ve", [P, T])
        rstd = sb("rstd", [P, T])
        mhalf = sb("mhalf", [P, T])
        xn = sb("xn", [P, T, E])
        xnT = sb("xnT", [P, C, S])
        qT = sb("qT", [P, HG, S])
        kT = sb("kT", [P, HG, S])
        v = sb("v", [P, T, H, VP])
        qg = sb("qg", [P, S])
        kg = sb("kg", [P, HG, S])
        s = sb("s", [P, 2, 2, S])
        top = sb("top", [P, 2, TOPK // 8, 8])
        work = sb("work", [P, 2, S])
        nmax = sb("nmax", [P, 2])
        e = sb("e", [P, 2, S])
        pm = sb("pm", [P, 2, S])
        pT = sb("pT", [P, 2, T, P])
        recip = sb("recip", [P, T, HG])
        ao = sb("ao", [P, T, E])
        aoT = sb("aoT", [P, C, S])

        w_loaded, w_zeroed, mhalf_ready = sem("w_loaded"), sem("w_zeroed"), sem("mhalf_ready")
        var_ready, rstd_ready, xn_ready = sem("var_ready"), sem("rstd_ready"), sem("xn_ready")
        xn_turned, xnT_ready = sem("xn_turned"), sem("xnT_ready")
        qk_made, qk_copied, v_made, v_ready = sem("qk_made"), sem("qk_copied"), sem("v_made"), sem("v_ready")
        kg_ready, scores_made, first_max, scores_read = sem("kg_ready"), sem("scores_made"), sem("first_max"), sem("scores_read")
        scores_copied = sem("scores_copied")
        nmax_ready, e_ready, pm_ready, pm_turned = sem("nmax_ready"), sem("e_ready"), sem("pm_ready"), sem("pm_turned")
        pT_ready, pv_done, heads_ready = sem("pT_ready"), sem("pv_done"), sem("heads_ready")
        ao_turned, aoT_ready, proj_ready, x_added = sem("ao_turned"), sem("aoT_ready"), sem("proj_ready"), sem("x_added")
        dve_step, pool_step = sem("dve_step"), sem("pool_step")
        passed, passed2 = sem("passed"), sem("passed2")

        NG = H // HG
        UNITS = HG * T
        pair, turn, wide = ps[:, 0, :], ps[:, 1, :], ps[:, 2, :]
        sums = wide[:, 0:T * HG * VP].rearrange("p (t j v) -> p t j v", t=T, j=HG)
        unit = lambda u: (2 * (u // 4) + u % 2, u // 2 % 2)

        block = ctx.enter_context(nc.Block())

        @block.sync
        def _(sp):
            sp.wait_ge(w_zeroed, 4)
            for w, name in ((wqT, "wq1T"), (wkT, "wk1T")):
                for c in range(C):
                    sp.dma_start(w[:, c, :, :, 0:D].rearrange("p g j d -> p (g j) d"),
                                 a[name][c * P:(c + 1) * P, :].rearrange("p (h d) -> p h d", d=D)).then_inc(w_loaded, 16)
            for w, name in ((wvT, "wv1T"), (woT, "wo1T")):
                sp.dma_start(w[:], a[name].rearrange("(c p) n -> p c n", p=P)).then_inc(w_loaded, 16)
            for w, name in ((bv, "bv1"), (bo, "bo1")):
                sp.dma_start(w[:], a[name].partition_broadcast(P)).then_inc(w_loaded, 16)
            for w, name in ((bq, "bq1"), (bk, "bk1")):
                for j in range(HG):
                    sp.dma_start(w[32 * j:32 * j + D, :], a[name][j]).then_inc(w_loaded, 16)

        @block.gpsimd
        def _(pool):
            pool.memset(mhalf[:], -0.5).then_inc(mhalf_ready, 1)
            for w in (wqT, wkT, bq, bk):
                pool.memset(w[:], 0.0).then_inc(w_zeroed, 1)
            pool.memset(kg[:], 0.0).then_inc(mhalf_ready, 1)
            step = Chain(pool, pool_step)
            pool.wait_ge(mhalf_ready, 2)
            with pool.Fori(0, B) as b:
                pool.wait_ge(var_ready, b + 1)
                pool.tensor_tensor(rstd[:], ve[:], mhalf[:], ALU.pow).then_inc(rstd_ready, 1)
                pool.wait_ge(qk_copied, 2 * NG * (b + 1))
                pool.sem_inc(passed2, 1)
                with pool.Fori(0, NG) as g:
                    n = b * NG + g
                    pool.wait_ge(scores_made, n * HG + 1)
                    step.restart()
                    step(pool.tensor_copy(qg[:], row_tile(qT, g)))
                    for j in range(HG):
                        rows = slice(32 * j, 32 * j + 32)
                        step(pool.tensor_copy(kg[rows, j, :], kT[rows, bass.ds(g, 1), :].rearrange("p a q -> p (a q)")))
                    pool.sem_inc(kg_ready, 1)

        @block.scalar
        def _(act):
            act.sem_inc(e_ready, 3)
            act.sem_inc(pT_ready, 2)
            act.sem_inc(scores_copied, 1)
            act.wait_ge(w_loaded, 256)
            with act.Fori(0, B) as b:
                act.wait_ge(xn_turned, b + 1)
                act.copy(xnT[:], turn.rearrange("p (c s) -> p c s", c=C)).then_inc(xnT_ready, 1)
                for g in range(NG):
                    act.wait_ge(qk_made, b * NG + g + 1)
                    act.activation(qT[:, g, :], pair[:, 0:S], ACT.Identity, bias=bq[:, g:g + 1]).then_inc(qk_copied, 1)
                    act.activation(kT[:, g, :], pair[:, S:2 * S], ACT.Identity, bias=bk[:, g:g + 1]).then_inc(qk_copied, 1)
                with act.Fori(0, NG) as g:
                    n = (b * NG + g) * UNITS

                    def turned(u):
                        act.wait_ge(pm_turned, n + u + 3)
                        act.wait_ge(pv_done, n + u + 1)
                        act.copy(pT[:, u % 2].rearrange("p t q -> p (t q)"), turn[:, 0:S]).then_inc(pT_ready, 1)

                    def copied(p):
                        act.wait_ge(scores_made, (b * NG + g) * HG + p + 2)
                        act.wait_ge(scores_read, n + 2 * p + 1)
                        act.copy(s[:, p % 2].rearrange("p j k -> p (j k)"), pair).then_inc(scores_copied, 1)

                    copied(0)
                    copied(1)
                    for u in range(UNITS):
                        act.wait_ge(first_max, n + u + 1)
                        act.mul(nmax[:, u % 2:u % 2 + 1], top[:, u % 2, 0, 0:1], -0.25).then_inc(nmax_ready, 1)
                        act.wait_ge(nmax_ready, n + u + 1)
                        act.wait_ge(pm_ready, n + u + 1)
                        act.activation(e[:, u % 2], s[:, u // 2 % 2, u % 2], ACT.Exp, scale=0.25,
                                       bias=nmax[:, u % 2:u % 2 + 1]).then_inc(e_ready, 1)
                        if u >= 1:
                            turned(u - 1)
                        if u % 2 == 1 and u // 2 + 2 < HG:
                            copied(u // 2 + 2)
                    turned(UNITS - 1)
                act.wait_ge(ao_turned, b + 1)
                act.copy(aoT[:], turn.rearrange("p (c s) -> p c s", c=C)).then_inc(aoT_ready, 1)

        @block.tensor
        def _(pe):
            pe.sem_inc(pm_turned, 2)
            pe.sem_inc(pv_done, 2)
            pe.sem_inc(scores_made, 1)
            pe.wait_ge(w_loaded, 256)
            with pe.Fori(0, B) as b:
                pe.wait_ge(xn_ready, b + 1)
                for c in range(C):
                    for t in range(T):
                        mm = pe.transpose(turn[:, c * S + t * P:c * S + (t + 1) * P], xn[:, t, c * P:(c + 1) * P], ident[:])
                mm.then_inc(xn_turned, 1)
                pe.wait_ge(xnT_ready, b + 1)
                for g in range(NG):
                    if g >= 1:
                        pe.wait_ge(qk_copied, 2 * NG * b + 2 * g)
                    for i, w in enumerate((wqT, wkT)):
                        for c in range(C):
                            mm = pe.matmul(pair[:, i * S:(i + 1) * S], w[:, c, g].rearrange("p j d -> p (j d)"), xnT[:, c, :],
                                           start=(c == 0), stop=(c == C - 1))
                    mm.then_inc(qk_made, 1)
                for t in range(T):
                    for c in range(C):
                        mm = pe.matmul(wide[:, t * E:(t + 1) * E], xnT[:, c, t * P:(t + 1) * P], wvT[:, c, :],
                                       start=(c == 0), stop=(c == C - 1))
                mm.then_inc(v_made, 1)
                pe.wait_ge(qk_copied, 2 * NG * (b + 1))
                pe.wait_ge(v_ready, b + 1)
                pe.sem_inc(passed, 1)
                with pe.Fori(0, NG) as g:
                    q = b * NG + g
                    n = q * UNITS
                    pe.wait_ge(kg_ready, q + 1)
                    pe.wait_ge(heads_ready, q + 1)

                    def scores(p):
                        pe.wait_ge(scores_copied, q * HG + p + 1)
                        j, t = unit(2 * p)
                        pe.matmul(pair, qg[:, t * P:(t + 1) * P], kg[:, j:j + 2, :].rearrange("p j k -> p (j k)"),
                                  start=True, stop=True).then_inc(scores_made, 1)

                    def product(u):
                        j, t = unit(u)
                        pe.wait_ge(pT_ready, n + u + 3)
                        for k in range(T):
                            mm = pe.matmul(sums[:, t, j, :], pT[:, u % 2, k, :],
                                           v[:, k, bass.ds(g * HG + j, 1), :].rearrange("p a v -> p (a v)"), start=(k == 0), stop=(k == T - 1))
                        mm.then_inc(pv_done, 1)

                    scores(0)
                    scores(1)
                    for u in range(UNITS):
                        pe.wait_ge(pm_ready, n + u + 3)
                        pe.wait_ge(pT_ready, n + u + 2)
                        for k in range(T):
                            mm = pe.transpose(turn[:, k * P:(k + 1) * P], pm[:, u % 2, k * P:(k + 1) * P], ident[:])
                        mm.then_inc(pm_turned, 1)
                        if u % 2 == 1 and u // 2 + 2 < HG:
                            scores(u // 2 + 2)
                        if u >= 1:
                            product(u - 1)
                    product(UNITS - 1)
                pe.wait_ge(heads_ready, (b + 1) * NG + 1)
                for c in range(C):
                    for t in range(T):
                        mm = pe.transpose(turn[:, c * S + t * P:c * S + (t + 1) * P], ao[:, t, c * P:(c + 1) * P], ident[:])
                mm.then_inc(ao_turned, 1)
                pe.wait_ge(aoT_ready, b + 1)
                for t in range(T):
                    for c in range(C):
                        mm = pe.matmul(wide[:, t * E:(t + 1) * E], aoT[:, c, t * P:(t + 1) * P], woT[:, c, :],
                                       start=(c == 0), stop=(c == C - 1))
                mm.then_inc(proj_ready, 1)

        @block.vector
        def _(dve):
            step = Chain(dve, dve_step)
            dve.memset(v[:], 1.0).then_inc(dve_step, 1)
            dve.wait_ge(dve_step, 1)
            dve.sem_inc(scores_read, 3)
            dve.sem_inc(pm_ready, 2)
            dve.sem_inc(heads_ready, 1)
            dve.wait_ge(w_loaded, 256)
            with dve.Fori(0, B) as b:
                step.restart()
                for t in range(T):
                    step(dve.bn_stats(stats[:, t], row_tile(X, b * T + t)))
                    step(dve.bn_aggr(mv[:, t], stats[:, t]))
                dve.tensor_scalar(ve[:], mv[:, :, 1], EPS, None, ALU.add).then_inc(var_ready, 1)
                dve.wait_ge(rstd_ready, b + 1)
                for t in range(T):
                    step(dve.tensor_scalar(xn[:, t], row_tile(X, b * T + t), mv[:, t, 0:1], rstd[:, t:t + 1], ALU.subtract, ALU.mult))
                dve.sem_inc(xn_ready, 1)
                for t in range(T):
                    step(dve.tensor_tensor(row_tile(X, b * T + t), row_tile(X, b * T + t), bo[:], ALU.add))
                dve.wait_ge(v_made, b + 1)
                for t in range(T):
                    step(dve.tensor_tensor(v[:, t, :, 0:D], wide[:, t * E:(t + 1) * E].rearrange("p (h d) -> p h d", d=D),
                                           bv[:].rearrange("p (h d) -> p h d", d=D), ALU.add))
                dve.sem_inc(v_ready, 1)
                with dve.Fori(0, NG) as g:
                    q = b * NG + g
                    n = q * UNITS
                    step.restart()
                    for u in range(UNITS):
                        w = work[:, u % 2]
                        dve.wait_ge(scores_copied, q * HG + u // 2 + 2)
                        for r in range(TOPK // 8):
                            if r == 0:
                                step.hold()
                            best, src = top[:, u % 2, r], (s[:, u // 2 % 2, u % 2] if r == 0 else w)
                            step(dve.max(best, src))
                            if r == 0:
                                dve.sem_inc(first_max, 1)
                            step(dve.match_replace(w, best, src, LOW))
                            if r == 0:
                                dve.sem_inc(scores_read, 1)
                        dve.wait_ge(e_ready, n + u + 4)
                        dve.wait_ge(pm_turned, n + u + 1)
                        dve.scalar_tensor_tensor(out=pm[:, u % 2], in0=w, scalar=LOW, in1=e[:, u % 2], op0=ALU.is_equal, op1=ALU.mult).then_inc(pm_ready, 1)
                    dve.wait_ge(pv_done, n + UNITS + 2)
                    step(dve.reciprocal(recip[:], sums[:, :, :, D]))
                    dve.tensor_tensor(ao[:, :, bass.ds(g * (HG * D), HG * D)].rearrange("p t (j d) -> p t j d", d=D), sums[:, :, :, 0:D],
                                      recip[:].unsqueeze(3).to_broadcast([P, T, HG, D]), ALU.mult).then_inc(heads_ready, 1)
                dve.wait_ge(proj_ready, b + 1)
                step.restart()
                for t in range(T):
                    x_t = row_tile(X, b * T + t)
                    step(dve.tensor_tensor(x_t, x_t, wide[:, t * E:(t + 1) * E], ALU.add))
                dve.sem_inc(x_added, 1)


class Norm:

    def __init__(self, sb, sem, bank):
        self.stats, self.mv = sb("stats", [P, T, 6]), sb("mv", [P, T, 2])
        self.ve, self.rstd, self.mhalf = sb("ve", [P, T]), sb("rstd", [P, T]), sb("mhalf", [P, T])
        self.xn, self.xnT, self.bank = sb("xn", [P, T, E]), sb("xnT", [P, C, S]), bank
        self.var_ready, self.rstd_ready, self.xn_ready = sem("var_ready"), sem("rstd_ready"), sem("xn_ready")
        self.xn_turned, self.xnT_ready = sem("xn_turned"), sem("xnT_ready")

    def vector(self, dve, step, tile, b):
        for t in range(T):
            step(dve.bn_stats(self.stats[:, t], tile(t)))
            step(dve.bn_aggr(self.mv[:, t], self.stats[:, t]))
        dve.tensor_scalar(self.ve[:], self.mv[:, :, 1], EPS, None, ALU.add).then_inc(self.var_ready, 1)
        dve.wait_ge(self.rstd_ready, b + 1)
        for t in range(T):
            step(dve.tensor_scalar(self.xn[:, t], tile(t), self.mv[:, t, 0:1], self.rstd[:, t:t + 1], ALU.subtract, ALU.mult))
        dve.sem_inc(self.xn_ready, 1)

    def gpsimd(self, pool, b):
        pool.wait_ge(self.var_ready, b + 1)
        pool.tensor_tensor(self.rstd[:], self.ve[:], self.mhalf[:], ALU.pow).then_inc(self.rstd_ready, 1)

    def tensor(self, pe, b, ident):
        pe.wait_ge(self.xn_ready, b + 1)
        for c in range(C):
            for t in range(T):
                mm = pe.transpose(self.bank[:, c * S + t * P:c * S + (t + 1) * P], self.xn[:, t, c * P:(c + 1) * P], ident[:])
        mm.then_inc(self.xn_turned, 1)

    def scalar(self, act, b):
        act.wait_ge(self.xn_turned, b + 1)
        act.copy(self.xnT[:], self.bank.rearrange("p (c s) -> p c s", c=C)).then_inc(self.xnT_ready, 1)


def argmax_row(dve, step, lg, best, idx, idxf, oh, count):
    for t in range(T):
        step(dve.max(best[:, t], lg[:, t]))
        step(dve.max_index(idx[:, t], best[:, t], lg[:, t]))
    step(dve.tensor_copy(idxf[:], idx[:, :, 0]))
    for t in range(T):
        step(dve.tensor_scalar(oh[:, t], count[:], idxf[:, t:t + 1], None, ALU.is_equal))


def experts(nc, a, X, ps, ident):
    ctx, sb, sem = scope(nc, "moe")
    with ctx:
        norm = Norm(sb, sem, ps[:, 0, :])
        wg = sb("wg", [P, C, EX])
        we = sb("we", [P, C, E])
        be = sb("be", [P, E])
        count = sb("count", [P, EX])
        upto = sb("upto", [P, P])
        ones = sb("ones", [P, P])
        lg = sb("lg", [P, T, EX])
        best = sb("best", [P, T, 8])
        idx = sb("idx", [P, T, 8], U32)
        idxf = sb("idxf", [P, T])
        oh = sb("oh", [P, T, EX])
        seen = sb("seen", [P, EX])
        nmax = sb("nmax", [P, T])
        ex = sb("ex", [P, T, EX])
        den = sb("den", [P, T])
        gate = sb("gate", [P, T])
        place = sb("place", [P, T, EX])
        rank = sb("rank", [P, T])
        keep = sb("keep", [P, T])
        hb = sb("hb", [P, T, E])

        loaded, consts, consts2 = sem("loaded"), sem("consts"), sem("consts2")
        lg_made, h_made, nmax_ready, den_ready = sem("lg_made"), sem("h_made"), sem("nmax_ready"), sem("den_ready")
        oh_ready, place_made, x_added, dve_step = sem("oh_ready"), sem("place_made"), sem("x_added"), sem("dve_step")
        lgp = ps[:, 1, 0:T * EX].rearrange("p (t e) -> p t e", t=T)
        hp = ps[:, 2, :].rearrange("p (t n) -> p t n", t=T)
        pp = ps[:, 3, 0:T * EX].rearrange("p (t e) -> p t e", t=T)

        block = ctx.enter_context(nc.Block())

        @block.sync
        def _(sp):
            sp.dma_start(wg[:], a["wg"].rearrange("(c p) n -> p c n", p=P)).then_inc(loaded, 16)
            sp.dma_start(we[:], a["we"].rearrange("(c p) n -> p c n", p=P)).then_inc(loaded, 16)
            sp.dma_start(be[:], a["be"].partition_broadcast(P)).then_inc(loaded, 16)

        @block.gpsimd
        def _(pool):
            pool.memset(norm.mhalf[:], -0.5).then_inc(consts, 1)
            pool.memset(ones[:], 1.0).then_inc(consts, 1)
            pool.memset(upto[:], 1.0).then_inc(consts, 1)
            pool.memset(seen[:], 0.0).then_inc(consts, 1)
            pool.iota(count[:], pattern=[[1, EX]], base=0, channel_multiplier=0, allow_small_or_imprecise_dtypes=True).then_inc(consts, 1)
            pool.wait_ge(consts, 5)
            pool.affine_select(out=upto[:], in_=upto[:], compare_op=ALU.is_ge, fill=0.0, base=0,
                               pattern=[[1, P]], channel_multiplier=-1).then_inc(consts2, 1)
            with pool.Fori(0, B) as b:
                norm.gpsimd(pool, b)

        @block.scalar
        def _(act):
            with act.Fori(0, B) as b:
                norm.scalar(act, b)
                act.wait_ge(nmax_ready, b + 1)
                for t in range(T):
                    act.activation(ex[:, t], lg[:, t], ACT.Exp, bias=nmax[:, t:t + 1], accum_out=den[:, t:t + 1]).then_inc(den_ready, 1)

        @block.tensor
        def _(pe):
            pe.wait_ge(loaded, 48)
            pe.wait_ge(consts2, 1)
            with pe.Fori(0, B) as b:
                norm.tensor(pe, b, ident)
                pe.wait_ge(norm.xnT_ready, b + 1)
                for t in range(T):
                    for c in range(C):
                        mm = pe.matmul(lgp[:, t], norm.xnT[:, c, t * P:(t + 1) * P], wg[:, c, :], start=(c == 0), stop=(c == C - 1))
                mm.then_inc(lg_made, 1)
                for t in range(T):
                    for c in range(C):
                        mm = pe.matmul(hp[:, t], norm.xnT[:, c, t * P:(t + 1) * P], we[:, c, :], start=(c == 0), stop=(c == C - 1))
                mm.then_inc(h_made, 1)
                pe.wait_ge(oh_ready, b + 1)
                for t in range(T):
                    pe.matmul(pp[:, t], ones[:], seen[:], start=True, stop=False)
                    for before in range(t):
                        pe.matmul(pp[:, t], ones[:], oh[:, before], start=False, stop=False)
                    mm = pe.matmul(pp[:, t], upto[:], oh[:, t], start=False, stop=True)
                mm.then_inc(place_made, 1)

        @block.vector
        def _(dve):
            step = Chain(dve, dve_step)
            dve.wait_ge(loaded, 48)
            dve.wait_ge(consts, 5)
            with dve.Fori(0, B) as b:
                step.restart()
                tile = lambda t: row_tile(X, b * T + t)
                norm.vector(dve, step, tile, b)
                dve.wait_ge(lg_made, b + 1)
                step(dve.tensor_copy(lg[:], lgp))
                argmax_row(dve, step, lg, best, idx, idxf, oh, count)
                dve.sem_inc(oh_ready, 1)
                dve.tensor_scalar(nmax[:], best[:, :, 0], -1.0, None, ALU.mult).then_inc(nmax_ready, 1)
                dve.wait_ge(h_made, b + 1)
                step(dve.tensor_tensor(hb[:], hp, be[:].unsqueeze(1).to_broadcast([P, T, E]), ALU.add))
                dve.wait_ge(den_ready, T * (b + 1))
                step(dve.reciprocal(gate[:], den[:]))
                dve.wait_ge(place_made, b + 1)
                step(dve.tensor_tensor(place[:], pp, oh[:], ALU.mult))
                for t in range(T):
                    step(dve.tensor_tensor(seen[:], seen[:], oh[:, t], ALU.add))
                step(dve.reduce_sum(rank[:], place[:], AX.X))
                step(dve.tensor_scalar(keep[:], rank[:], float(CAP), None, ALU.is_le))
                step(dve.tensor_tensor(keep[:], keep[:], gate[:], ALU.mult))
                for t in range(T):
                    ins = dve.scalar_tensor_tensor(out=tile(t), in0=hb[:, t], scalar=keep[:, t:t + 1], in1=tile(t), op0=ALU.mult, op1=ALU.add)
                    ins.then_inc(x_added, 1)
                dve.wait_ge(x_added, T * b + T)


def context_attention(nc, a, X, ps, ident):
    ctx, sb, sem = scope(nc, "ctx")
    with ctx:
        norm = Norm(sb, sem, ps[:, 7, :])
        M, MW = 4, SK // 4
        W = 8
        wq = sb("wq", [P, C, E])
        wk = sb("wk", [P, C, E])
        wvT = sb("wvT", [P, C, E])
        G = sb("G", [P, C, E])
        qT = sb("qT", [P, C, S])
        kx = sb("kx", [P, M, C, MW])
        vx = sb("vx", [P, KT, E])
        sc = sb("sc", [P, T, SK])
        mx = sb("mx", [P, T, M])
        nmax = sb("nmax", [P, T])
        den = sb("den", [P, T, M])
        recip = sb("recip", [P, T])
        pT = sb("pT", [P, 2, 4 * P])
        o = sb("o", [P, T, E])
        oT = sb("oT", [P, C, S])

        loaded, g_made, g_copied, consts = sem("loaded"), sem("g_made"), sem("g_copied"), sem("consts")
        k_loaded = [sem(f"k_loaded{m}") for m in range(M)]
        v_loaded = [sem(f"v_loaded{m}") for m in range(M)]
        q_made, qT_ready, scores_made, scores_copied = sem("q_made"), sem("qT_ready"), sem("scores_made"), sem("scores_copied")
        mx_ready, nmax_ready, exp_ready = sem("mx_ready"), sem("nmax_ready"), sem("exp_ready")
        turned, pT_ready, pv_done, o_ready = sem("turned"), sem("pT_ready"), sem("pv_done"), sem("o_ready")
        o_turned, oT_ready, proj_ready, dve_step = sem("o_turned"), sem("oT_ready"), sem("proj_ready"), sem("dve_step")
        x_added = sem("x_added")
        MC, WC = T * M, T * W

        slot = lambda m: ps[:, 2 * (m % 2):2 * (m % 2) + 2, :]
        turn = lambda w: ps[:, 4 + w % 2, :]
        acc, wide = ps[:, 6, 0:E], ps[:, 7, :]

        block = ctx.enter_context(nc.Block())

        @block.sync
        def _(sp):
            for w, name in ((wq, "wq2"), (wk, "wk2"), (wvT, "wv2T")):
                sp.dma_start(w[:], a[name].rearrange("(c p) n -> p c n", p=P)).then_inc(loaded, 16)
            with sp.Fori(0, B) as b:
                for m in range(M):
                    sp.wait_ge(scores_made, MC * b + M + m + 1)
                    for c in range(C):
                        sp.dma_start(kx[:, m, c, :], a["ctxT"][bass.ds(b * C + c, 1), :, m * MW:(m + 1) * MW].rearrange("a p k -> p (a k)")).then_inc(k_loaded[m], 16)
                for m in range(M):
                    sp.wait_ge(pv_done, WC * b + W + 2 * m + 2)
                    sp.dma_start(vx[:, m * 8:(m + 1) * 8, :], a["ctx"][bass.ds(b, 1), m * MW:(m + 1) * MW, :]
                                 .rearrange("a (k p) d -> p (a k) d", p=P)).then_inc(v_loaded[m], 16)

        @block.gpsimd
        def _(pool):
            pool.memset(norm.mhalf[:], -0.5).then_inc(consts, 1)
            pool.wait_ge(consts, 1)
            with pool.Fori(0, B) as b:
                norm.gpsimd(pool, b)

        @block.scalar
        def _(act):
            act.sem_inc(scores_copied, 2)
            act.wait_ge(g_made, 1)
            act.copy(G[:].rearrange("p c n -> p (c n)"), wide).then_inc(g_copied, 1)
            with act.Fori(0, B) as b:
                norm.scalar(act, b)
                act.wait_ge(q_made, b + 1)
                act.copy(qT[:].rearrange("p c s -> p (c s)"), wide).then_inc(qT_ready, 1)
                for t in range(T):
                    for m in range(M):
                        n = (b * T + t) * M + m
                        act.wait_ge(scores_made, MC + n + 1)
                        act.copy(sc[:, t, m * MW:(m + 1) * MW], slot(m).rearrange("p a k -> p (a k)")).then_inc(scores_copied, 1)
                for t in range(T):
                    act.wait_ge(nmax_ready, b * T + t + 1)
                    for m in range(M):
                        part = sc[:, t, m * MW:(m + 1) * MW]
                        act.activation(part, part, ACT.Exp, scale=1.0 / 16.0, bias=nmax[:, t:t + 1], accum_out=den[:, t, m:m + 1]).then_inc(exp_ready, 1)
                act.wait_ge(o_turned, b + 1)
                act.copy(oT[:].rearrange("p c s -> p (c s)"), wide).then_inc(oT_ready, 1)

        @block.tensor
        def _(pe):
            pe.sem_inc(scores_made, MC)
            pe.sem_inc(pv_done, WC)
            pe.wait_ge(loaded, 48)
            for i in range(C):
                for c in range(C):
                    mm = pe.matmul(wide[:, i * E:(i + 1) * E], wq[:, c, i * P:(i + 1) * P], wk[:, c, :], start=(c == 0), stop=(c == C - 1))
            mm.then_inc(g_made, 1)
            pe.wait_ge(g_copied, 1)
            with pe.Fori(0, B) as b:
                norm.tensor(pe, b, ident)
                pe.wait_ge(norm.xnT_ready, b + 1)
                for j in range(C):
                    for c in range(C):
                        mm = pe.matmul(wide[:, j * S:(j + 1) * S], G[:, c, j * P:(j + 1) * P], norm.xnT[:, c, :], start=(c == 0), stop=(c == C - 1))
                mm.then_inc(q_made, 1)
                pe.wait_ge(qT_ready, b + 1)
                for t in range(T):
                    for m in range(M):
                        n = (b * T + t) * M + m
                        if t == 0:
                            pe.wait_ge(k_loaded[m], 16 * C * (b + 1))
                        pe.wait_ge(scores_copied, n + 1)
                        for w in range(2):
                            for c in range(C):
                                mm = pe.matmul(slot(m)[:, w, :], qT[:, c, t * P:(t + 1) * P], kx[:, m, c, w * 512:(w + 1) * 512], start=(c == 0), stop=(c == C - 1))
                        mm.then_inc(scores_made, 1)
                for t in range(T):
                    n = (b * T + t) * W

                    def product(w):
                        if t == 0 and w % 2 == 0:
                            pe.wait_ge(v_loaded[w // 2], 16 * (b + 1))
                        if w == 0:
                            pe.wait_ge(o_ready, b * T + t + 1)
                        pe.wait_ge(pT_ready, n + w + 3)
                        for i in range(4):
                            mm = pe.matmul(acc, pT[:, w % 2, i * P:(i + 1) * P], vx[:, 4 * w + i, :], start=(w == 0 and i == 0), stop=(w == W - 1 and i == 3))
                        mm.then_inc(pv_done, 1)

                    for w in range(W):
                        pe.wait_ge(exp_ready, (b * T + t) * M + w // 2 + 1)
                        pe.wait_ge(pT_ready, n + w + 1)
                        for i in range(4):
                            k = 4 * w + i
                            mm = pe.transpose(turn(w)[:, i * P:(i + 1) * P], sc[:, t, k * P:(k + 1) * P], ident[:])
                        mm.then_inc(turned, 1)
                        if w >= 1:
                            product(w - 1)
                    product(W - 1)
                pe.wait_ge(o_ready, b * T + T + 1)
                for c in range(C):
                    for t in range(T):
                        mm = pe.transpose(wide[:, c * S + t * P:c * S + (t + 1) * P], o[:, t, c * P:(c + 1) * P], ident[:])
                mm.then_inc(o_turned, 1)
                pe.wait_ge(oT_ready, b + 1)
                for t in range(T):
                    for c in range(C):
                        mm = pe.matmul(wide[:, t * E:(t + 1) * E], oT[:, c, t * P:(t + 1) * P], wvT[:, c, :], start=(c == 0), stop=(c == C - 1))
                mm.then_inc(proj_ready, 1)

        @block.vector
        def _(dve):
            step = Chain(dve, dve_step)
            dve.sem_inc(pT_ready, 2)
            dve.sem_inc(o_ready, 1)
            with dve.Fori(0, B) as b:
                step.restart()
                tile = lambda t: row_tile(X, b * T + t)
                norm.vector(dve, step, tile, b)
                for t in range(T):
                    for m in range(M):
                        n = (b * T + t) * M + m
                        dve.wait_ge(scores_copied, n + 3)
                        dve.reduce_max(mx[:, t, m:m + 1], sc[:, t, m * MW:(m + 1) * MW], AX.X).then_inc(mx_ready, 1)
                    dve.wait_ge(mx_ready, (b * T + t + 1) * M)
                    step(dve.reduce_max(nmax[:, t:t + 1], mx[:, t], AX.X))
                    dve.tensor_scalar(nmax[:, t:t + 1], nmax[:, t:t + 1], -1.0 / 16.0, None, ALU.mult).then_inc(nmax_ready, 1)
                for t in range(T):
                    for w in range(W):
                        n = (b * T + t) * W + w
                        dve.wait_ge(turned, n + 1)
                        dve.wait_ge(pv_done, WC + n - 1)
                        dve.tensor_copy(pT[:, w % 2], turn(w)).then_inc(pT_ready, 1)
                    dve.wait_ge(exp_ready, (b * T + t + 1) * M)
                    step(dve.reduce_sum(recip[:, t:t + 1], den[:, t], AX.X))
                    step(dve.reciprocal(recip[:, t:t + 1], recip[:, t:t + 1]))
                    dve.wait_ge(pv_done, WC + (b * T + t + 1) * W)
                    dve.tensor_scalar(o[:, t], acc, recip[:, t:t + 1], None, ALU.mult).then_inc(o_ready, 1)
                dve.wait_ge(proj_ready, b + 1)
                for t in range(T):
                    dve.tensor_tensor(tile(t), tile(t), wide[:, t * E:(t + 1) * E], ALU.add).then_inc(x_added, 1)
                dve.wait_ge(x_added, T * b + T)


N_STATE = 16
TAPS = 4
RANK = 8
TIME = B * S
HALVES = TIME // 512


def state_space(nc, a, X, ps, ident):
    ctx, sb, sem = scope(nc, "ssm")
    with ctx:
        norm = Norm(sb, sem, ps[:, 0, :])
        nw, nb = sb("nw", [P, E]), sb("nb", [P, E])
        win = sb("win", [P, 2, 4 * P])
        cw, cb = sb("cw", [P, 2, C, TAPS]), sb("cb", [P, 2, C])
        wx = sb("wx", [P, 2, C, RANK + 2 * N_STATE])
        wdt = sb("wdt", [40, 2, E])
        bdt = sb("bdt", [P, 2, C])
        alog = sb("alog", [P, 2, C, N_STATE])
        dcol = sb("dcol", [P, 2, C])
        wout = sb("wout", [P, 2, C, P])
        A = sb("A", [P, 2, C, N_STATE])
        sel = sb("sel", [96, 2 * N_STATE, P], BF16)
        diag = sb("diag", [P, C, P])
        mirror = sb("mirror", [P, P])
        xT = sb("xT", [P, 2, B, S])
        xcp = sb("xcp", [P, C, B, S + TAPS - 1])
        sz = sb("sz", [P, C, TIME])
        cv = sb("cv", [P, C, TIME])
        xc = sb("xc", [P, C, TIME])
        bc = sb("bc", [96, TIME], BF16)
        bcr = sb("bcr", [32, TIME])
        dtr = sb("dtr", [40, TIME])
        v = sb("v", [P, C, TIME])
        dt = sb("dt", [P, C, TIME])
        du = sb("du", [P, C, TIME])
        decay = [sb(f"decay{i}", [P, C, TIME]) for i in range(2)]
        bu = sb("bu", [P, C, TIME])
        h = sb("h", [P, C, TIME])
        hc = [sb(f"hc{i}", [P, C, TIME]) for i in range(2)]

        loaded, consts, zeroed = sem("loaded"), sem("consts"), sem("zeroed")
        h_done, mirror_ready = sem("h_done"), sem("mirror_ready")
        a_exp, a_ready, sel_ready = sem("a_exp"), sem("a_ready"), sem("sel_ready")
        xT_ready, xz_made, xc_copied, sz_ready = sem("xT_ready"), sem("xz_made"), sem("xc_copied"), sem("sz_ready")
        cv_ready, xc_ready, xd_made, bc_ready, dtr_ready = sem("cv_ready"), sem("xc_ready"), sem("xd_made"), sem("bc_ready"), sem("dtr_ready")
        dt_made, v_ready, l_ready, dt_ready, diag_ready = sem("dt_made"), sem("v_ready"), sem("l_ready"), sem("dt_ready"), sem("diag_ready")
        act_step, dve_step = sem("act_step"), sem("dve_step")
        b_made, c_made, bu_done, hc_ready, summed = sem("b_made"), sem("c_made"), sem("bu_done"), sem("hc_ready"), sem("summed")
        decay_ready, scanned, gated, out_made, x_added = sem("decay_ready"), sem("scanned"), sem("gated"), sem("out_made"), sem("x_added")

        two = lambda i: ps[:, 2 * i:2 * i + 2, :]
        flat = lambda v: v.rearrange("p a q -> p (a q)")
        PAIRS = N_STATE // 2

        def each_pair(eng, body):
            with eng.Fori(0, PAIRS - 1) as i:
                body(2 * i, False)
            body(N_STATE - 2, True)

        block = ctx.enter_context(nc.Block())

        @block.sync
        def _(sp):
            for w, name in ((nw, "nw"), (nb, "nb")):
                sp.dma_start(w[:], a[name].partition_broadcast(P)).then_inc(loaded, 16)
            for w, name in ((win, "win"), (cw, "cw"), (cb, "cb"), (wx, "wx"), (bdt, "bdt"), (alog, "alog"), (dcol, "dcol"), (wout, "wout")):
                sp.dma_start(w[:], a[name]).then_inc(loaded, 16)
            sp.dma_start(wdt[32:32 + RANK], a["wdt"]).then_inc(loaded, 16)

        LOADS = 16 * 11

        @block.gpsimd
        def _(pool):
            pool.memset(norm.mhalf[:], -0.5).then_inc(consts, 1)
            pool.memset(mirror[:], 0.0).then_inc(consts, 1)
            pool.wait_ge(consts, 2)
            pool.affine_select(out=mirror[:], in_=mirror[:], compare_op=ALU.not_equal, fill=1.0, base=1 - P,
                               pattern=[[1, P]], channel_multiplier=1).then_inc(mirror_ready, 1)
            pool.memset(xcp[:], 0.0).then_inc(zeroed, 1)
            with pool.Fori(0, B) as b:
                for k in range(2):
                    pool.wait_ge(norm.var_ready, 2 * b + k + 1)
                    pool.tensor_tensor(norm.rstd[:], norm.ve[:], norm.mhalf[:], ALU.pow).then_inc(norm.rstd_ready, 1)

        @block.scalar
        def _(act):
            act.sem_inc(decay_ready, 1)
            act.wait_ge(loaded, LOADS)
            act.activation(A[:], alog[:], ACT.Exp).then_inc(a_exp, 1)
            with act.Fori(0, B) as b:
                act.wait_ge(norm.xn_turned, b + 1)
                for d in range(2):
                    dst = xT[:, d, bass.ds(b, 1), :].rearrange("p a s -> p (a s)")
                    act.copy(dst, norm.bank[:, d * S:(d + 1) * S]).then_inc(xT_ready, 1)
            act.wait_ge(zeroed, 1)
            for d in range(2):
                act.wait_ge(xz_made, 4 * d + 2)
                if d:
                    act.wait_ge(cv_ready, C * d)
                for k in range(C):
                    act.copy(xcp[:, k, :, TAPS - 1:], flat(two(k)).rearrange("p (b s) -> p b s", b=B)).then_inc(xc_copied, 1)
                act.wait_ge(xz_made, 4 * d + 4)
                for k in range(C):
                    act.activation(sz[:, k], flat(two(2 + k)), ACT.Silu).then_inc(sz_ready, 1)
                for k in range(C):
                    act.wait_ge(cv_ready, C * d + k + 1)
                    act.activation(xc[:, k], cv[:, k], ACT.Silu).then_inc(xc_ready, 1)
                act.wait_ge(xd_made, d + 1)
                act.copy(dtr[32:32 + RANK], flat(two(0))[32:32 + RANK]).then_inc(dtr_ready, 1)
                for k in range(C):
                    n = 2 * (C * d + k)
                    act.wait_ge(dt_made, C * d + k + 1)
                    act.activation(v[:, k], flat(two(1 + k)), ACT.Identity, bias=bdt[:, d, k:k + 1]).then_inc(v_ready, 1)
                    act.wait_ge(v_ready, C * d + k + 1)
                    act.activation(dt[:, k], v[:, k], ACT.Abs).then_inc(act_step, 1)
                    act.wait_ge(act_step, n + 1)
                    act.activation(dt[:, k], dt[:, k], ACT.Exp, scale=-1.0).then_inc(act_step, 1)
                    act.wait_ge(act_step, n + 2)
                    act.activation(dt[:, k], dt[:, k], ACT.Ln, bias=1.0).then_inc(l_ready, 1)
                act.wait_ge(dt_ready, C * d + C)
                act.wait_ge(a_ready, 1)

                def decays(n, last):
                    for j in range(2):
                        act.wait_ge(scanned, d * N_STATE + n + j + 1)
                        for k in range(C):
                            ins = act.activation(decay[j][:, k], dt[:, k], ACT.Exp, scale=A[:, d, k, bass.ds(n + j, 1)])
                        ins.then_inc(decay_ready, 1)

                each_pair(act, decays)

        @block.tensor
        def _(pe):
            pe.sem_inc(summed, 2)
            pe.wait_ge(mirror_ready, 1)
            with pe.Fori(0, B) as b:
                pe.wait_ge(norm.xn_ready, b + 1)
                pe.wait_ge(xT_ready, 2 * b + 2)
                for t in range(T):
                    pe.transpose(norm.bank[:, t * P:(t + 1) * P], norm.xn[:, t, 0:P], ident[:])
                    mm = pe.transpose(norm.bank[:, S + (T - 1 - t) * P:S + (T - t) * P], norm.xn[:, t, P:2 * P], mirror[:])
                mm.then_inc(norm.xn_turned, 1)
            pe.wait_ge(xT_ready, 2 * B + 2)
            pe.wait_ge(loaded, LOADS)
            for d in range(2):
                if d:
                    pe.wait_ge(gated, 1)
                    pe.wait_ge(x_added, 1)
                for m in range(4):
                    for w in range(HALVES):
                        mm = pe.matmul(two(m)[:, w, :], win[:, d, m * P:(m + 1) * P], xT[:, d, 2 * w:2 * w + 2, :].rearrange("p b s -> p (b s)"),
                                       start=True, stop=True)
                    mm.then_inc(xz_made, 1)
                pe.wait_ge(xc_ready, C * d + C)
                pe.wait_ge(xc_copied, C * d + C)
                for w in range(HALVES):
                    for k in range(C):
                        mm = pe.matmul(two(0)[0:40, w, :], wx[:, d, k, :], xc[:, k, w * 512:(w + 1) * 512], start=(k == 0), stop=(k == C - 1))
                mm.then_inc(xd_made, 1)
                pe.wait_ge(dtr_ready, d + 1)
                pe.wait_ge(sz_ready, C * d + C)
                for k in range(C):
                    for w in range(HALVES):
                        mm = pe.matmul(two(1 + k)[:, w, :], wdt[32:32 + RANK, d, k * P:(k + 1) * P], dtr[32:32 + RANK, w * 512:(w + 1) * 512],
                                       start=True, stop=True)
                    mm.then_inc(dt_made, 1)
                pe.wait_ge(diag_ready, d + 1)
                pe.wait_ge(sel_ready, 1)
                pe.wait_ge(bc_ready, d + 1)
                pe.wait_ge(v_ready, C * d + C)
                for k in range(C):
                    for w in range(HALVES):
                        pe.matmul(two(k)[:, w, :], diag[:, k, :], xc[:, k, w * 512:(w + 1) * 512], start=True, stop=False, skip_group_check=True)

                def spread(i, row):
                    for w in range(HALVES):
                        mm = pe.matmul(two(i)[:, w, :], sel[:, bass.ds(row, 1), :].rearrange("p a m -> p (a m)"), bc[:, w * 512:(w + 1) * 512],
                                       start=True, stop=True)
                    return mm

                spread(2, 0).then_inc(b_made, 1)

                def states(n, last):
                    for j in range(2):
                        N = d * N_STATE + n + j
                        pe.wait_ge(hc_ready, N + 1)
                        spread(3, N_STATE + n + j).then_inc(c_made, 1)
                        if not (last and j == 1):
                            pe.wait_ge(bu_done, N + 1)
                            spread(2, n + j + 1).then_inc(b_made, 1)
                        pe.wait_ge(hc_ready, N + 2)
                        for k in range(C):
                            for w in range(HALVES):
                                mm = pe.matmul(two(k)[:, w, :], ident[:], hc[j][:, k, w * 512:(w + 1) * 512], start=False,
                                               stop=(last and j == 1), skip_group_check=True)
                        mm.then_inc(summed, 1)

                each_pair(pe, states)
                pe.wait_ge(gated, d + 1)
                out = flat(two(2)).rearrange("p (r n) -> p r n", n=P)
                for r in range(ROWS):
                    for k in range(C):
                        mm = pe.matmul(out[:, r], cv[:, k, r * P:(r + 1) * P], wout[:, d, k, :], start=(k == 0), stop=(k == C - 1))
                mm.then_inc(out_made, 1)

        @block.vector
        def _(dve):
            step = Chain(dve, dve_step)
            dve.sem_inc(scanned, 2)
            dve.sem_inc(hc_ready, 1)
            dve.sem_inc(xT_ready, 2)
            dve.wait_ge(loaded, LOADS)
            for i in range(3):
                step(dve.tensor_copy(sel[32 * i:32 * i + 32], ident[32 * i:32 * i + 32, 32 * i:32 * i + 32].unsqueeze(2).to_broadcast([32, 32, P])))
            dve.sem_inc(sel_ready, 1)
            dve.wait_ge(a_exp, 1)
            step(dve.tensor_scalar(A[:], A[:], -1.0, None, ALU.mult))
            dve.sem_inc(a_ready, 1)
            with dve.Fori(0, B) as b:
                step.restart()
                tile = lambda t: row_tile(X, b * T + t)
                for k in range(2):
                    src = tile if k == 0 else (lambda t: norm.xn[:, t])
                    for t in range(T):
                        step(dve.bn_stats(norm.stats[:, t], src(t)))
                        step(dve.bn_aggr(norm.mv[:, t], norm.stats[:, t]))
                    dve.tensor_scalar(norm.ve[:], norm.mv[:, :, 1], EPS, None, ALU.add).then_inc(norm.var_ready, 1)
                    dve.wait_ge(norm.rstd_ready, 2 * b + k + 1)
                    for t in range(T):
                        step(dve.tensor_scalar(norm.xn[:, t], src(t), norm.mv[:, t, 0:1], norm.rstd[:, t:t + 1], ALU.subtract, ALU.mult))
                        if k == 0:
                            step(dve.tensor_tensor(tile(t), tile(t), norm.xn[:, t], ALU.add))
                for t in range(T):
                    step(dve.tensor_tensor(norm.xn[:, t], norm.xn[:, t], nw[:], ALU.mult))
                    step(dve.tensor_tensor(norm.xn[:, t], norm.xn[:, t], nb[:], ALU.add))
                dve.sem_inc(norm.xn_ready, 1)
                dve.wait_ge(xT_ready, 2 * b + 4)
            for d in range(2):
                step.restart()
                for k in range(C):
                    step(dve.tensor_scalar(diag[:, k], ident[:], dcol[:, d, k:k + 1], None, ALU.mult))
                dve.sem_inc(diag_ready, 1)
                dve.wait_ge(xc_copied, C * d + C)
                for k in range(C):
                    out = cv[:, k].rearrange("p (b s) -> p b s", b=B)
                    tap = lambda i: xcp[:, k, :, i:i + S]
                    step(dve.tensor_scalar(out, tap(TAPS - 1), cw[:, d, k, TAPS - 1:TAPS], cb[:, d, k:k + 1], ALU.mult, ALU.add))
                    for i in range(TAPS - 1):
                        step(dve.scalar_tensor_tensor(out=out, in0=tap(i), scalar=cw[:, d, k, i:i + 1], in1=out, op0=ALU.mult, op1=ALU.add))
                    dve.sem_inc(cv_ready, 1)
                dve.wait_ge(xd_made, d + 1)
                dve.wait_ge(dtr_ready, d + 1)
                xd = flat(two(0))[0:32]
                step(dve.tensor_copy(bc[0:32], xd))
                step(dve.tensor_tensor(bcr[:], xd, bc[0:32], ALU.subtract))
                step(dve.tensor_copy(bc[32:64], bcr[:]))
                step(dve.tensor_copy(hc[0][0:32, 0, 0:TIME], bc[32:64]))
                step(dve.tensor_tensor(bc[64:96], bcr[:], hc[0][0:32, 0, 0:TIME], ALU.subtract))
                dve.sem_inc(bc_ready, 1)
                for k in range(C):
                    dve.wait_ge(l_ready, C * d + k + 1)
                    step(dve.scalar_tensor_tensor(out=dt[:, k], in0=v[:, k], scalar=0.0, in1=dt[:, k], op0=ALU.max, op1=ALU.add))
                    dve.sem_inc(dt_ready, 1)
                    step(dve.tensor_tensor(du[:, k], dt[:, k], xc[:, k], ALU.mult))
                spreadk = lambda i: flat(two(i)).unsqueeze(1).to_broadcast([P, C, TIME])

                def scans(n, last):
                    for j in range(2):
                        N = d * N_STATE + n + j
                        step.restart()
                        dve.wait_ge(decay_ready, N + 2)
                        step(dve.memset(decay[j][:].rearrange("p k (b s) -> p k b s", b=B)[:, :, :, 0], 0.0))
                        dve.wait_ge(b_made, N + 1)
                        dve.tensor_tensor(bu[:], spreadk(2), du[:], ALU.mult).then_inc(bu_done, 1)
                        dve.wait_ge(bu_done, N + 1)
                        for k in range(C):
                            dve.tensor_tensor_scan(h[:, k], decay[j][:, k], bu[:, k], 0.0, ALU.mult, ALU.add).then_inc(h_done, 1)
                        dve.wait_ge(h_done, C * (N + 1))
                        dve.sem_inc(scanned, 1)
                        dve.wait_ge(c_made, N + 1)
                        dve.wait_ge(summed, N + 1)
                        dve.tensor_tensor(hc[j][:], spreadk(3), h[:], ALU.mult).then_inc(hc_ready, 1)

                each_pair(dve, scans)
                step.restart()
                dve.wait_ge(summed, (d + 1) * N_STATE + 2)
                for k in range(C):
                    for b in range(B):
                        cols = slice(b * S, (b + 1) * S)
                        out = cv[:, k, cols]
                        step(dve.tensor_tensor(out if d == 0 else out[:, ::-1], flat(two(k))[:, cols], sz[:, k, cols], ALU.mult))
                dve.sem_inc(gated, 1)
                dve.wait_ge(out_made, d + 1)
                part = X[:, :, d * P:(d + 1) * P]
                dve.tensor_tensor(part, part, flat(two(2)).rearrange("p (r n) -> p r n", n=P), ALU.add).then_inc(x_added, 1)
                dve.wait_ge(x_added, d + 1)


def routed(nc, a, X, ps, ident, out):
    ctx, sb, sem = scope(nc, "ffn")
    with ctx:
        norm = Norm(sb, sem, ps[:, 0, :])
        sig = sb("sig", [P, C, EX])
        below = sb("below", [P, C, EX])
        w = sb("w", [P, C, EX, E])
        bias = sb("bias", [EX, E])
        count = sb("count", [P, EX])
        lg = sb("lg", [P, T, EX])
        best = sb("best", [P, T, 8])
        idx = sb("idx", [P, T, 8], U32)
        idxf = sb("idxf", [P, T])
        oh = sb("oh", [P, T, EX])
        ohT = sb("ohT", [EX, T, P])
        y = sb("y", [P, E])

        loaded, consts, sign_ready = sem("loaded"), sem("consts"), sem("sign_ready")
        lg_made, oh_ready, oh_turned, ohT_ready, bias_made = sem("lg_made"), sem("oh_ready"), sem("oh_turned"), sem("ohT_ready"), sem("bias_made")
        y_made, y_used, x_added, stored, dve_step = sem("y_made"), sem("y_used"), sem("x_added"), sem("stored"), sem("dve_step")
        PAIRS = EX // 2
        lgp = ps[:, 1, 0:T * EX].rearrange("p (t e) -> p t e", t=T)
        pairs = lambda p: ps[:, 2 + p, :].rearrange("p (e n) -> p e n", e=2)
        ohp = ps[0:EX, 6, 0:T * P]
        bp = ps[:, 7, :].rearrange("p (t n) -> p t n", t=T)

        block = ctx.enter_context(nc.Block())

        @block.sync
        def _(sp):
            sp.dma_start(sig[:], a["sigT"].rearrange("(c p) n -> p c n", p=P)).then_inc(loaded, 16)
            sp.dma_start(bias[:], a["bias3"]).then_inc(loaded, 16)
            for c in range(C):
                sp.dma_start(w[:, c], a["w3"][:, c * P:(c + 1) * P, :].rearrange("x p n -> p x n")).then_inc(loaded, 16)
            with sp.Fori(0, B) as b:
                sp.wait_ge(x_added, T * b + T)
                sp.dma_start(out[bass.ds(b, 1)].rearrange("a (t p) d -> p (a t) d", p=P), X[:, bass.ds(b * T, T), :]).then_inc(stored, 16)
            sp.wait_ge(stored, 16 * B)

        @block.gpsimd
        def _(pool):
            pool.memset(norm.mhalf[:], -0.5).then_inc(consts, 1)
            pool.iota(count[:], pattern=[[1, EX]], base=0, channel_multiplier=0, allow_small_or_imprecise_dtypes=True).then_inc(consts, 1)
            pool.wait_ge(consts, 2)
            with pool.Fori(0, B) as b:
                norm.gpsimd(pool, b)

        @block.scalar
        def _(act):
            with act.Fori(0, B) as b:
                norm.scalar(act, b)
                act.wait_ge(oh_turned, b + 1)
                act.copy(ohT[:].rearrange("e t q -> e (t q)"), ohp).then_inc(ohT_ready, 1)

        @block.tensor
        def _(pe):
            pe.wait_ge(loaded, 64)
            pe.wait_ge(sign_ready, 1)
            with pe.Fori(0, B) as b:
                norm.tensor(pe, b, ident)
                pe.wait_ge(norm.xnT_ready, b + 1)
                for t in range(T):
                    for c in range(C):
                        mm = pe.matmul(lgp[:, t], norm.xnT[:, c, t * P:(t + 1) * P], sig[:, c, :], start=(c == 0), stop=(c == C - 1))
                mm.then_inc(lg_made, 1)
                for t in range(T):
                    for p in range(PAIRS):
                        pe.wait_ge(y_used, (b * T + t) * PAIRS + p + 1)
                        for c in range(C):
                            mm = pe.matmul(ps[:, 2 + p, :], norm.xnT[:, c, t * P:(t + 1) * P], w[:, c, 2 * p:2 * p + 2, :].rearrange("p e n -> p (e n)"),
                                           start=(c == 0), stop=(c == C - 1))
                        mm.then_inc(y_made, 1)
                    if t == 0:
                        pe.wait_ge(oh_ready, b + 1)
                        for s in range(T):
                            mm = pe.transpose(ohp[:, s * P:(s + 1) * P], oh[:, s], ident[:])
                        mm.then_inc(oh_turned, 1)
                        pe.wait_ge(ohT_ready, b + 1)
                        for s in range(T):
                            mm = pe.matmul(bp[:, s], ohT[:, s, :], bias[:], start=True, stop=True)
                        mm.then_inc(bias_made, 1)

        @block.vector
        def _(dve):
            step = Chain(dve, dve_step)
            dve.sem_inc(y_used, PAIRS)
            dve.wait_ge(loaded, 64)
            dve.wait_ge(consts, 2)
            step(dve.tensor_scalar(below[:], sig[:], 0.0, None, ALU.is_lt))
            step(dve.tensor_scalar(sig[:], sig[:], 0.0, None, ALU.is_gt))
            dve.tensor_tensor(sig[:], sig[:], below[:], ALU.subtract).then_inc(sign_ready, 1)
            with dve.Fori(0, B) as b:
                step.restart()
                tile = lambda t: row_tile(X, b * T + t)
                norm.vector(dve, step, tile, b)
                dve.wait_ge(lg_made, b + 1)
                step(dve.tensor_copy(lg[:], lgp))
                argmax_row(dve, step, lg, best, idx, idxf, oh, count)
                dve.sem_inc(oh_ready, 1)
                dve.wait_ge(bias_made, b + 1)
                for t in range(T):
                    step(dve.tensor_tensor(y[:], tile(t), bp[:, t], ALU.add))
                    for x in range(EX):
                        if x % 2 == 0:
                            dve.wait_ge(y_made, (b * T + t) * PAIRS + x // 2 + 1)
                        ins = dve.scalar_tensor_tensor(out=tile(t) if x == EX - 1 else y[:], in0=pairs(x // 2)[:, x % 2], scalar=oh[:, t, x:x + 1], in1=y[:],
                                                       op0=ALU.mult, op1=ALU.add)
                        if x == EX - 1:
                            ins.then_inc(x_added, 1)
                            dve.wait_ge(x_added, b * T + t + 1)
                        else:
                            step(ins)
                        if x % 2:
                            dve.sem_inc(y_used, 1)


def program(nc, a, out, qscratch, last=9):
    with ExitStack() as ctx:
        X = ctx.enter_context(nc.sbuf_tensor("X", [P, ROWS, E], F32))
        ident = ctx.enter_context(nc.sbuf_tensor("ident", [P, P], F32))
        identb = ctx.enter_context(nc.sbuf_tensor("identb", [P, P], BF16))
        W2 = ctx.enter_context(nc.sbuf_tensor("W2", [P, C, E], F32))
        qmax = ctx.enter_context(nc.sbuf_tensor("qmax", [P, ROWS], F32))
        ps = ctx.enter_context(nc.psum_tensor("ps", [P, 8, 512], F32))
        prepare(nc, a, X, ps, ident, identb, W2, qmax, qscratch)
        cross_attention(nc, a, X, ps, ident, identb, W2, qmax, qscratch)
        if last >= 2:
            self_attention(nc, a, X, ps, ident)
        if last >= 3:
            experts(nc, a, X, ps, ident)
        if last >= 4:
            context_attention(nc, a, X, ps, ident)
        if last >= 5:
            state_space(nc, a, X, ps, ident)
        if last >= 6:
            routed(nc, a, X, ps, ident, out)
            return
        stored = ctx.enter_context(nc.semaphore("stored"))
        with nc.Block() as block:
            @block.sync
            def _(sp):
                sp.dma_start(out.rearrange("b s d -> (b s) d").rearrange("(r p) d -> p r d", p=P), X[:]).then_inc(stored, 16)
                sp.wait_ge(stored, 16)


def both(i, name):
    import numpy as np
    return [np.asarray(i[f"L1_attn_{d}_{name}"]) for d in ("fwd", "bwd")]


def layouts(i):
    import numpy as np
    c = lambda v: np.ascontiguousarray(v)
    ctx = np.asarray(i["ctx_1024"])
    return {
        "x": c(i["x"]),
        "mask": c(np.asarray(i["mask_Bx1xSxS2_if1"]).reshape(B, S, SK)),
        "ctxT": c(ctx.transpose(0, 2, 1).reshape(B * C, P, SK)),
        "ctxV": c(ctx.reshape(B, KT, P, H // HG, HG * D).transpose(0, 3, 2, 1, 4).reshape(B * H // HG, P, KT * HG * D)),
        "wq0": c(i["L0_xattn_Wq"]), "wk0": c(i["L0_xattn_Wk"]), "wv0": c(i["L0_xattn_Wv"]),
        "wo0T": c(np.asarray(i["L0_xattn_Wo"]).T), "bo0": c(i["L0_xattn_bo"]),
        "wq1T": c(np.asarray(i["L0_attn_Wq"]).T), "wk1T": c(np.asarray(i["L0_attn_Wk"]).T),
        "wv1T": c(np.asarray(i["L0_attn_Wv"]).T), "wo1T": c(np.asarray(i["L0_attn_Wo"]).T),
        "bq1": c(np.asarray(i["L0_attn_bq"]).reshape(H // HG, HG, D).transpose(1, 2, 0)),
        "bk1": c(np.asarray(i["L0_attn_bk"]).reshape(H // HG, HG, D).transpose(1, 2, 0)),
        "wg": c(i["L0_ffn_Wg"]), "we": c(i["L0_ffn_We"]), "be": c(i["L0_ffn_be"]), "ctx": c(ctx),
        "wq2": c(i["L1_xattn_w_q"]), "wk2": c(i["L1_xattn_w_k"]), "wv2T": c(np.asarray(i["L1_xattn_w_v"]).T),
        "nw": c(i["L1_attn_norm_w"]), "nb": c(i["L1_attn_norm_b"]),
        "win": c(np.stack([w.T for w in both(i, "in_proj_w")], 1)),
        "cw": c(np.stack([w.reshape(C, P, TAPS).transpose(1, 0, 2) for w in both(i, "conv_w")], 1)),
        "wx": c(np.stack([np.concatenate([w[RANK:], w[:RANK]]).T.reshape(C, P, -1).transpose(1, 0, 2) for w in both(i, "x_proj_w")], 1)),
        "wdt": c(np.stack([w.T for w in both(i, "dt_proj_w")], 1)),
        "cb": c(np.stack([w.reshape(C, P).T for w in both(i, "conv_b")], 1)),
        "bdt": c(np.stack([w.reshape(C, P).T for w in both(i, "dt_proj_b")], 1)),
        "dcol": c(np.stack([w.reshape(C, P).T for w in both(i, "D")], 1)),
        "alog": c(np.stack([w.reshape(C, P, N_STATE).transpose(1, 0, 2) for w in both(i, "A_log")], 1)),
        "wout": c(np.stack([w.T.reshape(C, P, P).transpose(1, 0, 2) for w in both(i, "out_proj_w")], 1)),
        "sigT": c(np.asarray(i["L1_ffn_tile_sigs"]).T), "w3": c(i["L1_ffn_W"]), "bias3": c(i["L1_ffn_b"]),
        "bv1": c(i["L0_attn_bv"]), "bo1": c(i["L0_attn_bo"]),
    }


def kernel(**inputs):
    import concourse.bacc as bacc
    from concourse.bass_utils import run_bass_kernel_spmd

    nc = bacc.Bacc("TRN2", target_bir_lowering=False, num_devices=1)
    arrays = layouts(inputs)
    a = {n: nc.dram_tensor(n, v.shape, mybir.dt.from_np(v.dtype), kind="ExternalInput").ap() for n, v in arrays.items()}
    out = nc.dram_tensor("out", (B, S, E), F32, kind="ExternalOutput").ap()
    qscratch = nc.dram_tensor("qscratch", (NB, B, C, P, S), BF16, kind="Internal").ap()
    program(nc, a, out, qscratch)
    r = run_bass_kernel_spmd(nc, [arrays], core_ids=[0])
    return r.results[0]["out"]
```

```python
from contextlib import ExitStack

import concourse.bass as bass
from concourse import mybir

ALU = mybir.AluOpType
ACT = mybir.ActivationFunctionType
AX = mybir.AxisListType
F32 = mybir.dt.float32
BF16 = mybir.dt.bfloat16
I32 = mybir.dt.int32
U32 = mybir.dt.uint32

P = 128
B, S, E, SK = 4, 256, 256, 4096
H, D = 16, 16
T = S // P
ROWS = B * T
C = E // P
KT = SK // P
HG = 4
GC = H // HG // C
RING = 3
PARTS = [0, 0, 0, 1, 1, 2]
QPARTS = [0, 1, 2, 0, 1, 0]
NB = len(PARTS)
KR = NB * D
NEG = -1.0e20
MC = SK // 2
BOUND = 64.0
LOW = -3.0e38
EPS = 1e-5
TOPK = 64
EX = 8
CAP = 4 * 256 // EX
VP = D + 1


class Chain:

    def __init__(self, eng, sem):
        self.eng, self.sem, self.n = eng, sem, 0

    def hold(self):
        self.n += 1
        self.eng.sem_inc(self.sem, 1)

    def restart(self):
        self.hold()
        self.eng.sem_clear(self.sem)
        self.n = 0

    def __call__(self, ins):
        self.n += 1
        ins.then_inc(self.sem, 1)
        self.eng.wait_ge(self.sem, self.n)


def row_tile(X, t):
    return X[:, bass.ds(t, 1), :].rearrange("p a d -> p (a d)")


def scope(nc, stage):
    ctx = ExitStack()
    sems = []

    def clear():
        nc.clear_and_free_semaphores(sems)
        nc.all_engine_barrier()

    ctx.callback(clear)
    sb = lambda name, shape, dt=F32: ctx.enter_context(nc.sbuf_tensor(f"{stage}_{name}", shape, dt))

    def sem(name):
        sems.append(nc.alloc_semaphore(f"{stage}_{name}"))
        return sems[-1]

    return ctx, sb, sem


class Norm:

    def __init__(self, sb, sem, banks, turned=True):
        self.stats, self.mv = sb("stats", [P, ROWS, 6]), sb("mv", [P, ROWS, 2])
        self.ve, self.rstd, self.mhalf = sb("ve", [P, ROWS]), sb("rstd", [P, ROWS]), sb("mhalf", [P, ROWS])
        self.xn, self.banks = sb("xn", [P, ROWS, E]), banks
        self.stats_ready, self.mv_ready = sem("stats_ready"), sem("mv_ready")
        self.var_ready, self.rstd_ready, self.xn_ready = sem("var_ready"), sem("rstd_ready"), sem("xn_ready")
        if turned:
            self.xnT = sb("xnT", [P, C, B * S])
            self.xn_turned, self.xnT_ready = sem("xn_turned"), sem("xnT_ready")

    def vector(self, dve, src, k=0):
        for r in range(ROWS):
            dve.bn_stats(self.stats[:, r], src[:, r]).then_inc(self.stats_ready, 1)
        dve.wait_ge(self.stats_ready, (k + 1) * ROWS)
        for r in range(ROWS):
            dve.bn_aggr(self.mv[:, r], self.stats[:, r]).then_inc(self.mv_ready, 1)
        dve.wait_ge(self.mv_ready, (k + 1) * ROWS)
        dve.tensor_scalar(self.ve[:], self.mv[:, :, 1], EPS, None, ALU.add).then_inc(self.var_ready, 1)
        dve.wait_ge(self.rstd_ready, k + 1)
        for r in range(ROWS):
            dve.tensor_scalar(self.xn[:, r], src[:, r], self.mv[:, r, 0:1], self.rstd[:, r:r + 1], ALU.subtract, ALU.mult).then_inc(self.xn_ready, 1)

    def gpsimd(self, pool, k=0):
        pool.wait_ge(self.var_ready, k + 1)
        pool.tensor_tensor(self.rstd[:], self.ve[:], self.mhalf[:], ALU.pow).then_inc(self.rstd_ready, 1)

    def tensor(self, pe, ident):
        for b in range(B):
            pe.wait_ge(self.xn_ready, (b + 1) * T)
            if b >= 2:
                pe.wait_ge(self.xnT_ready, b - 1)
            for c in range(C):
                for t in range(T):
                    mm = pe.transpose(self.banks[b % 2][:, c * S + t * P:c * S + (t + 1) * P], self.xn[:, b * T + t, c * P:(c + 1) * P], ident[:])
            mm.then_inc(self.xn_turned, 1)

    def scalar(self, act):
        for b in range(B):
            act.wait_ge(self.xn_turned, b + 1)
            act.copy(self.xnT[:, :, b * S:(b + 1) * S], self.banks[b % 2].rearrange("p (c s) -> p c s", c=C)).then_inc(self.xnT_ready, 1)


def prepare(nc, a, X, ps, ident, identb, W2, qmax, qscratch):
    ctx, sb, sem = scope(nc, "prepare")
    with ctx:
        w16 = sb("w16", [D, 2, D])
        m16 = sb("m16", [D, D])
        Mbd = sb("Mbd", [P, P])
        Vbd = sb("Vbd", [P, P])
        woT = sb("woT", [P, C, E])
        bo = sb("bo", [P, E])
        norm = Norm(sb, sem, [ps[:, 0, :], ps[:, 1, :]])
        HALF = 2 * S
        qrest = sb("qrest", [P, C * 2, HALF])
        qparts = sb("qparts", [P, 3, C, B * S], BF16)

        x_loaded, w_loaded, zeroed = sem("x_loaded"), sem("w_loaded"), sem("zeroed")
        m_made, m_copied, m_placed = sem("m_made"), sem("m_copied"), sem("m_placed")
        v_placed, w2_made, ident_ready = sem("v_placed"), sem("w2_made"), sem("ident_ready")
        q_ready, q_read, q_split = sem("q_ready"), sem("q_read"), sem("q_split")
        q_stored, dve_step, pool_step = sem("q_stored"), sem("dve_step"), sem("pool_step")
        w2_copied, bo_added = sem("w2_copied"), sem("bo_added")

        block = ctx.enter_context(nc.Block())

        @block.sync
        def _(sp):
            sp.dma_start(X[:], a["x"].rearrange("b s d -> (b s) d").rearrange("(r p) d -> p r d", p=P)).then_inc(x_loaded, 16)
            sp.dma_start(w16[:, 0, :], a["wq0"]).then_inc(w_loaded, 16)
            sp.dma_start(w16[:, 1, :], a["wk0"]).then_inc(w_loaded, 16)
            sp.dma_start(woT[:], a["wo0T"].rearrange("(c p) n -> p c n", p=P)).then_inc(w_loaded, 16)
            sp.dma_start(bo[:], a["bo0"].partition_broadcast(P)).then_inc(w_loaded, 16)
            sp.wait_ge(zeroed, 2)
            for h in range(P // D):
                sp.dma_start(Vbd[h * D:(h + 1) * D, h * D:(h + 1) * D], a["wv0"]).then_inc(v_placed, 16)
            sp.wait_ge(m_copied, 1)
            for h in range(P // D):
                sp.dma_start(Mbd[h * D:(h + 1) * D, h * D:(h + 1) * D], m16[:]).then_inc(m_placed, 16)
            for c in range(C):
                sp.wait_ge(q_split, 2 * (c + 1))
                for n, part in enumerate(QPARTS):
                    sp.dma_start(qscratch[n, :, c].rearrange("b p q -> p b q"),
                                 qparts[:, part, c].rearrange("p (b q) -> p b q", b=B)).then_inc(q_stored, 16)
            sp.wait_ge(q_stored, 16 * NB * C)

        @block.gpsimd
        def _(pool):
            pool.memset(Mbd[:], 0.0).then_inc(zeroed, 1)
            pool.memset(Vbd[:], 0.0).then_inc(zeroed, 1)
            pool.memset(ident[:], 0.0).then_inc(pool_step, 1)
            pool.memset(identb[:], 0.0).then_inc(pool_step, 1)
            pool.memset(norm.mhalf[:], -0.5).then_inc(pool_step, 1)
            pool.wait_ge(pool_step, 3)
            for t in (ident, identb):
                pool.affine_select(out=t[:], in_=t[:], compare_op=ALU.not_equal, fill=1.0, base=0,
                                   pattern=[[-1, P]], channel_multiplier=1).then_inc(ident_ready, 1)
            norm.gpsimd(pool)

        @block.scalar
        def _(act):
            norm.scalar(act)

        @block.tensor
        def _(pe):
            pe.wait_ge(w_loaded, 64)
            pe.matmul(ps[0:D, 6, 0:D], w16[:, 0, :], w16[:, 1, :], start=True, stop=True).then_inc(m_made, 1)
            pe.wait_ge(v_placed, 16 * (P // D))
            for c in range(C):
                pe.matmul(ps[:, 7, c * E:(c + 1) * E], Vbd[:], woT[:, c, :], start=True, stop=True).then_inc(w2_made, 1)
            pe.wait_ge(ident_ready, 2)
            norm.tensor(pe, ident)
            pe.wait_ge(m_placed, 16 * (P // D))
            for c in range(C):
                for w in range(2):
                    pe.wait_ge(norm.xnT_ready, B if c else 2 * (w + 1))
                    pe.matmul(ps[:, 2 + 2 * c + w, :], Mbd[:], norm.xnT[:, c, w * HALF:(w + 1) * HALF], start=True, stop=True).then_inc(q_ready, 1)

        @block.vector
        def _(dve):
            step = Chain(dve, dve_step)
            dve.wait_ge(m_made, 1)
            dve.tensor_copy(m16[:], ps[0:D, 6, 0:D]).then_inc(m_copied, 1)
            dve.wait_ge(x_loaded, 16)
            norm.vector(dve, X)
            dve.wait_ge(w2_made, C)
            dve.tensor_copy(W2[:], ps[:, 7, :].rearrange("p (c n) -> p c n", c=C)).then_inc(w2_copied, 1)
            for c in range(C):
                for w in range(2):
                    i = 2 * c + w
                    q = ps[:, 2 + i, :]
                    part = lambda n: qparts[:, n, c, w * HALF:(w + 1) * HALF]
                    dve.wait_ge(q_ready, i + 1)
                    step(dve.tensor_copy(part(0), q))
                    dve.tensor_reduce(qmax[:, i:i + 1], q, AX.X, ALU.max, apply_absolute_value=True).then_inc(q_read, 1)
                    step(dve.tensor_tensor(qrest[:, i], q, part(0), ALU.subtract))
                    step(dve.tensor_copy(part(1), qrest[:, i]))
                    dve.tensor_tensor(part(2), qrest[:, i], part(1), ALU.subtract).then_inc(q_split, 1)
            dve.wait_ge(q_read, 2 * C)
            dve.wait_ge(norm.xn_ready, ROWS)
            for t in range(ROWS):
                dve.tensor_tensor(X[:, t, :], X[:, t, :], bo[:], ALU.add).then_inc(bo_added, 1)
            dve.wait_ge(bo_added, ROWS)
            dve.wait_ge(w2_copied, 1)


def cross_attention(nc, a, X, ps, ident, identb, W2, qmax, qscratch):
    ctx, sb, sem = scope(nc, "cross")
    with ctx:
        stage = sb("stage", [P, SK])
        kparts = sb("kparts", [P, 3, SK], BF16)
        kstack = [sb(f"kstack{i}", [P, HG, SK], BF16) for i in range(GC)]
        qstack = [sb(f"qstack{i}", [P, HG, S], BF16) for i in range(GC)]
        mstage = sb("mstage", [P, MC], I32)
        maskb = sb("maskb", [P, 2 * T, SK], BF16)
        vstage = sb("vstage", [P, KT, HG, D])
        values = [sb(f"values{i}", [P, KT, HG * VP + 32 - VP]) for i in range(GC)]
        probs = [sb(f"probs{i}", [P, HG, S]) for i in range(RING)]
        maxima = sb("maxima", [P, HG * T, 4])
        shift = sb("shift", [P, HG * T])
        rest = sb("rest", [P, 2, HG * T])
        shiftp = sb("shiftp", [P, HG * T, 3], BF16)
        accT = sb("accT", [P, S])
        recip = sb("recip", [P, T, HG])
        heads = sb("heads", [P, T, P])
        headsT = sb("headsT", [P, S])
        bounds = sb("bounds", [P, 3])
        widest = sb("widest", [P, 3])
        least = sb("least", [P, 1])
        general = sb("general", [P, 1], I32)

        ctx_loaded, mask_loaded, v_loaded = sem("ctx_loaded"), sem("mask_loaded"), sem("v_loaded")
        kparts_ready, mask_ready, values_ready = sem("kparts_ready"), sem("mask_ready"), sem("values_ready")
        v_free = sem("v_free")
        stack_loaded, stack_free = [sem(f"stack_loaded{g}") for g in range(GC)], sem("stack_free")
        bounds_ready, general_ready, pool_step = sem("bounds_ready"), sem("general_ready"), sem("pool_step")
        way_read = sem("way_read")
        natural_ready, natural_reduced = sem("natural_ready"), sem("natural_reduced")
        shift_ready, shift_turned, shift_placed = sem("shift_ready"), sem("shift_turned"), sem("shift_placed")
        scores_ready, exp_done, pv_done = sem("scores_ready"), sem("exp_done"), sem("pv_done")
        acc_copied, acc_turned, heads_ready = sem("acc_copied"), sem("acc_turned"), sem("heads_ready")
        heads_turned, headsT_ready, proj_ready, x_added = (
            sem("heads_turned"), sem("headsT_ready"), sem("proj_ready"), sem("x_added"))
        passed = [sem(f"passed_{e}") for e in ("act", "pe", "sp", "pool")]
        dve_step, ones_ready = sem("dve_step"), sem("ones_ready")

        slot = lambda m: ps[:, 2 * (m % RING):2 * (m % RING) + 2, :]
        acc = lambda g: ps[:, 6, g * S:(g + 1) * S]
        PER = HG * NB + NB
        NAT = HG * T * 4
        PIECES = SK // MC
        FIRST = [RING - 1, RING, RING - 2]
        TURN, HEADS, PROJECT = 6, 10, 14

        block = ctx.enter_context(nc.Block())

        @block.sync
        def _(sp):
            sp.dma_start(stage[:], a["ctxT"][0]).then_inc(ctx_loaded, 16)
            with sp.Fori(0, B) as b:
                with sp.Fori(0, C) as c:
                    i = b * C + c
                    sp.wait_ge(kparts_ready, i + 1)
                    sp.sem_inc(passed[2], 1)
                    with sp.If(i < B * C - 1):
                        sp.dma_start(stage[:], a["ctxT"][bass.ds((i + 1) % (B * C), 1)].rearrange("a p k -> p (a k)")).then_inc(ctx_loaded, 16)
                    for g in range(GC):
                        sp.wait_ge(stack_free, i * GC + g + 1)
                        for j in range(HG):
                            r = (g * HG + j) * D
                            for n, part in enumerate(PARTS):
                                sp.dma_start(kstack[g][n * D:(n + 1) * D, j, :], kparts[r:r + D, part, :]).then_inc(stack_loaded[g], 16)
                        for n in range(NB):
                            src = qscratch[n, bass.ds(b, 1), bass.ds(c, 1), g * HG * D:(g + 1) * HG * D, :]
                            sp.dma_start(qstack[g][n * D:(n + 1) * D, :, :],
                                         src.rearrange("a c (j d) q -> (a c j) d q", d=D).rearrange("j d q -> d j q")).then_inc(stack_loaded[g], 16)

        @block.gpsimd
        def _(pool):
            step = Chain(pool, pool_step)

            def load_values(n):
                pool.wait_ge(v_free, n + 1)
                pool.dma_start(vstage[:], a["ctxV"][bass.ds(n % (B * H // HG), 1)].rearrange("a p (k j d) -> p (a k) j d", j=HG, d=D)).then_inc(v_loaded, 16)

            def load_mask(b, t, piece, n):
                pool.wait_ge(mask_ready, n + 1)
                pool.dma_start(mstage[:], a["mask"][bass.ds(b, 1), bass.ds(t * P, P), piece * MC:(piece + 1) * MC]
                               .rearrange("a p k -> p (a k)")).then_inc(mask_loaded, 16)

            def decide(i):
                pool.wait_ge(bounds_ready, i + 1)
                step.restart()
                step(pool.partition_all_reduce(widest[:], bounds[:], P, bass.bass_isa.ReduceOp.absmax))
                step(pool.tensor_tensor(widest[:, 0:1], widest[:, 0:1], widest[:, 1:2], ALU.mult))
                step(pool.tensor_tensor(widest[:, 0:1], widest[:, 0:1], widest[:, 2:3], ALU.add))
                pool.wait_ge(way_read, 3 * i + 3)
                step.hold()
                pool.tensor_scalar(general[:], widest[:, 0:1], BOUND, None, ALU.is_gt).then_inc(general_ready, 1)

            load_values(0)
            with pool.Fori(0, T) as t:
                for piece in range(PIECES):
                    load_mask(0, t, piece, t * PIECES + piece)
            with pool.Fori(0, B * C) as i:
                decide(i)
                load_values(2 * i + 1)
                with pool.If(i < (B - 1) * C):
                    b, t = (i + C) // C % B, i % C
                    for piece in range(PIECES):
                        load_mask(b, t, piece, (T + i) * PIECES + piece)
                pool.sem_inc(passed[3], 1)
                with pool.If(i < B * C - 1):
                    load_values(2 * i + 2)

        @block.scalar
        def _(act):
            def exps(n, k, m):
                act.wait_ge(scores_ready, n * KT + k + 1)
                act.wait_ge(pv_done, n * KT + (FIRST[m % RING] if m < RING else m + 1))
                act.activation(probs[m % RING][:], slot(m).rearrange("p a (h q) -> p (a h) q", h=2), ACT.Exp,
                               scale=1.0 / 16.0).then_inc(exp_done, 1)

            def take_sums(n, g):
                act.wait_ge(pv_done, (n + 1) * KT + RING)
                act.wait_ge(acc_turned, n + 1)
                act.copy(accT[:], acc(g)).then_inc(acc_copied, 1)

            def take_heads(i):
                act.wait_ge(heads_turned, i + 1)
                act.copy(headsT[:], ps[:, 7, 0:S]).then_inc(headsT_ready, 1)

            act.sem_inc(exp_done, RING)
            act.sem_inc(acc_copied, 2)
            with act.Fori(0, B * C) as i:
                act.wait_ge(general_ready, i + 1)
                act.sem_inc(passed[0], 1)
                way = act.value_load(general[0:1, 0:1])
                act.sem_inc(way_read, 1)
                with act.If(way == 1):
                    with act.If(i > 0):
                        take_heads(i - 1)
                    for g in range(GC):
                        n = i * GC + g
                        act.wait_ge(shift_turned, n + 1)
                        act.copy(qstack[g][KR:KR + 3, :, :], ps[:].bitcast(BF16)[KR:KR + 3, 7, :]
                                 .rearrange("p (j q) -> p j q", j=HG)).then_inc(shift_placed, 1)
                        for k in range(KT):
                            exps(n, k, k)
                        take_sums(n, g)
                with act.Else():
                    for m in range(GC * KT):
                        exps(i * GC, m, m)
                        if m % KT == 0 and m:
                            take_sums(i * GC + m // KT - 1, m // KT - 1)
                        if m == HEADS:
                            act.sem_inc(shift_placed, GC)
                            with act.If(i > 0):
                                take_heads(i - 1)
                    take_sums(i * GC + GC - 1, GC - 1)
            take_heads(B * C - 1)

        @block.tensor
        def _(pe):
            def turn(n, i):
                pe.wait_ge(acc_copied, n + 3)
                pe.wait_ge(heads_ready, n + 1)
                pe.wait_ge(x_added, i + 1)
                for t in range(T):
                    mm = pe.transpose(ps[:, 7, t * P:(t + 1) * P], accT[:, t * P:(t + 1) * P], ident[:])
                mm.then_inc(acc_turned, 1)

            def turn_heads(i):
                pe.wait_ge(heads_ready, i * GC + GC + 1)
                for t in range(T):
                    mm = pe.transpose(ps[:, 7, t * P:(t + 1) * P], heads[:, t, :], ident[:])
                mm.then_inc(heads_turned, 1)

            def project(i, c):
                pe.wait_ge(headsT_ready, i + 1)
                pe.sem_inc(passed[1], 1)
                for t in range(T):
                    mm = pe.matmul(ps[:, 7, t * E:(t + 1) * E], headsT[:, t * P:(t + 1) * P],
                                   W2[:, bass.ds(c, 1), :].rearrange("p a n -> p (a n)"), start=True, stop=True)
                mm.then_inc(proj_ready, 1)

            def scores(g, k, m, rows, last):
                for j in range(HG):
                    mm = pe.matmul(slot(m)[:, j // 2, (j % 2) * S:(j % 2 + 1) * S], kstack[g][0:rows, j, k * P:(k + 1) * P],
                                   qstack[g][0:rows, j, :], start=(j % 2 == 0), stop=last, skip_group_check=True)
                return mm

            def products(n, g, k, m, base):
                if k == 0:
                    pe.wait_ge(values_ready, n + 1)
                    pe.wait_ge(acc_copied, n + 2)
                pe.wait_ge(exp_done, base + RING + m + 1)
                for j in range(HG):
                    mm = pe.matmul(acc(g)[32 * j:32 * j + 32, :], values[g][:, k, j * VP:j * VP + 32], probs[m % RING][:, j, :],
                                   start=(k == 0), stop=(k == KT - 1), skip_group_check=True)
                mm.then_inc(pv_done, 1)

            def release(n):
                pe.wait_ge(scores_ready, (n + 1) * KT)
                pe.sem_inc(stack_free, 1)

            def masked(b2, add_mask):
                with pe.If(b2 == 0):
                    add_mask(0)
                with pe.Else():
                    add_mask(T)

            def general_half(b2, i, c):
                pe.wait_ge(ones_ready, GC * HG)
                with pe.If(i > 0):
                    turn(i * GC - 1, i - 1)
                    turn_heads(i - 1)
                    project(i - 1, 1 - c)
                for g in range(GC):
                    n = i * GC + g
                    pe.wait_ge(stack_loaded[g], (i + 1) * (16 * PER))
                    for u in range(NAT):
                        j, t, part = u // (4 * T), u // 4 % T, u % 4
                        if u < RING:
                            pe.wait_ge(exp_done, n * KT + FIRST[u])
                        else:
                            pe.wait_ge(natural_reduced, n * NAT + u - RING + 1)
                        for w in range(2):
                            k0 = part * 1024 + w * 512
                            pe.matmul(slot(u)[:, w, :], qstack[g][0:KR, j, t * P:(t + 1) * P], kstack[g][0:KR, j, k0:k0 + 512],
                                      start=True, stop=False)

                        def add_mask(first):
                            for w in range(2):
                                k0 = part * 1024 + w * 512
                                mm = pe.matmul(slot(u)[:, w, :], identb[:], maskb[:, first + t, k0:k0 + 512], start=False, stop=True)
                            mm.then_inc(natural_ready, 1)

                        masked(b2, add_mask)
                    pe.wait_ge(shift_ready, n + 1)
                    pe.wait_ge(heads_ready, n + 1)
                    pe.wait_ge(x_added, i + 1)
                    for u in range(HG * T):
                        mm = pe.transpose(ps[:].bitcast(BF16)[KR:KR + 3, 7, u * P:(u + 1) * P], shiftp[:, u, :], identb[:])
                    mm.then_inc(shift_turned, 1)
                    pe.wait_ge(shift_placed, n + 1)
                    pe.wait_ge(natural_reduced, (n + 1) * NAT)
                    for k in range(KT + 2):
                        if k < KT:
                            if k >= RING:
                                pe.wait_ge(exp_done, n * KT + k + 1)
                            scores(g, k, k, KR + 3, False)

                            def add_mask(first):
                                for w in range(2):
                                    for t in range(T):
                                        mm = pe.matmul(slot(k)[:, w, :].rearrange("p (h t q) -> p h t q", h=2, t=T)[:, :, t, :],
                                                       maskb[:, first + t, k * P:(k + 1) * P],
                                                       identb[:].unsqueeze(1).to_broadcast([P, 2, P]), start=False,
                                                       stop=(t == T - 1), skip_group_check=True)
                                mm.then_inc(scores_ready, 1)

                            masked(b2, add_mask)
                        else:
                            if k == KT:
                                release(n)
                        if k >= 2:
                            products(n, g, k - 2, k - 2, n * KT)
                    if g < GC - 1:
                        turn(n, i)

            def plain_half(i, c):
                pe.sem_inc(natural_ready, GC * NAT)
                pe.sem_inc(shift_turned, GC)
                n = i * GC
                for m in range(GC * KT + 2):
                    g, k = m // KT, m % KT
                    if m < GC * KT:
                        if k == 0:
                            pe.wait_ge(stack_loaded[g], (i + 1) * (16 * PER))
                        pe.wait_ge(exp_done, n * KT + (FIRST[m] if m < RING else m + 1))
                        scores(g, k, m, KR, True).then_inc(scores_ready, 1)
                    if m == TURN:
                        with pe.If(i > 0):
                            turn(n - 1, i - 1)
                    if m == HEADS:
                        with pe.If(i > 0):
                            turn_heads(i - 1)
                    if m == PROJECT:
                        with pe.If(i > 0):
                            project(i - 1, 1 - c)
                    if g and k == 1:
                        release(n + g - 1)
                    if m > KT and k == TURN:
                        turn(n + g - 1, i)
                    if m >= 2:
                        products(n + (m - 2) // KT, (m - 2) // KT, (m - 2) % KT, m - 2, n * KT)

            pe.sem_inc(pv_done, RING)
            pe.sem_inc(stack_free, 2)
            pe.sem_inc(acc_turned, 1)
            with pe.Fori(0, B // 2) as bb:
                with pe.Fori(0, 2) as b2:
                    with pe.Fori(0, C) as c:
                        i = (bb * 2 + b2) * C + c
                        pe.wait_ge(general_ready, i + 1)
                        pe.sem_inc(passed[1], 1)
                        way = pe.value_load(general[0:1, 0:1])
                        pe.sem_inc(way_read, 1)
                        with pe.If(way == 1):
                            general_half(b2, i, c)
                        with pe.Else():
                            plain_half(i, c)
            turn(B * H // HG - 1, B * C - 1)
            turn_heads(B * C - 1)
            project(B * C - 1, C - 1)

        @block.vector
        def _(dve):
            step = Chain(dve, dve_step)

            def place_values(n, g):
                dve.wait_ge(v_loaded, (n + 1) * 16)
                dve.wait_ge(acc_copied, n + 1)
                step(dve.tensor_copy(values[g][:, :, 0:HG * VP].rearrange("p k (j v) -> p k j v", v=VP)[:, :, :, 0:D], vstage[:]))
                dve.sem_inc(v_free, 1)
                dve.sem_inc(values_ready, 1)

            def place_mask(tile, piece, n):
                dve.wait_ge(mask_loaded, (n + 1) * 16)
                step.hold()
                part = maskb[:, bass.ds(tile, 1), piece * MC:(piece + 1) * MC].rearrange("p a k -> p (a k)")
                step(dve.tensor_scalar(part, mstage[:], 0.0, NEG, ALU.is_equal, ALU.mult))
                dve.sem_inc(mask_ready, 1)
                step(dve.tensor_reduce(least[:], part, AX.X, ALU.min))
                step(dve.tensor_tensor(bounds[:, 2:3], bounds[:, 2:3], least[:], ALU.min))

            def place_ones(head):
                for stack in kstack:
                    dve.memset(stack[96:128, head, :].bitcast(I32), 0x3F803F80).then_inc(ones_ready, 1)

            def largest_key(i):
                dve.wait_ge(ctx_loaded, (i + 1) * 16)
                step(dve.tensor_reduce(bounds[:, 0:1], stage[:], AX.X, ALU.max, apply_absolute_value=True))

            def split():
                step(dve.tensor_copy(kparts[:, 0, :], stage[:]))
                step(dve.tensor_tensor(stage[:], stage[:], kparts[:, 0, :], ALU.subtract))
                step(dve.tensor_copy(kparts[:, 1, :], stage[:]))
                step(dve.tensor_tensor(kparts[:, 2, :], stage[:], kparts[:, 1, :], ALU.subtract))
                dve.sem_inc(kparts_ready, 1)

            def divide(n, g):
                dve.wait_ge(acc_turned, n + 2)
                turned = ps[:, 7, 0:S].rearrange("p (t j v) -> p t j v", t=T, j=HG)
                step(dve.reciprocal(recip[:], turned[:, :, :, D]))
                dve.tensor_tensor(heads[:, :, g * HG * D:(g + 1) * HG * D].rearrange("p t (j d) -> p t j d", d=D), turned[:, :, :, 0:D],
                                  recip[:].unsqueeze(3).to_broadcast([P, T, HG, D]), ALU.mult).then_inc(heads_ready, 1)

            def add(i, tile):
                dve.wait_ge(proj_ready, i + 1)
                step.hold()
                for t in range(T):
                    x_t = row_tile(X, tile + t)
                    ins = dve.tensor_tensor(x_t, x_t, ps[:, 7, t * E:(t + 1) * E], ALU.add)
                    if t < T - 1:
                        step(ins)
                ins.then_inc(x_added, 1)

            def reduce_natural(n):
                for u in range(NAT):
                    dve.wait_ge(natural_ready, n * NAT + u + 1)
                    dve.reduce_max(maxima[:, u // 4, u % 4:u % 4 + 1], slot(u), AX.XY).then_inc(natural_reduced, 1)
                dve.wait_ge(natural_reduced, (n + 1) * NAT)
                step(dve.reduce_max(shift[:], maxima[:], AX.X))
                step(dve.tensor_scalar(rest[:, 0, :], shift[:], -1.0, None, ALU.mult))
                step(dve.tensor_copy(shiftp[:, :, 0], rest[:, 0, :]))
                step(dve.tensor_tensor(rest[:, 1, :], rest[:, 0, :], shiftp[:, :, 0], ALU.subtract))
                step(dve.tensor_copy(shiftp[:, :, 1], rest[:, 1, :]))
                dve.tensor_tensor(shiftp[:, :, 2], rest[:, 1, :], shiftp[:, :, 1], ALU.subtract).then_inc(shift_ready, 1)

            def maxima_of(n, way):
                step.hold()
                with dve.If(way == 1):
                    first = step.n
                    reduce_natural(n)
                    used = step.n - first
                with dve.Else():
                    dve.sem_inc(natural_reduced, NAT)
                    dve.sem_inc(shift_ready, 1)
                    dve.sem_inc(dve_step, used)

            for i in range(GC):
                dve.memset(values[i][:], 1.0).then_inc(dve_step, 1)
            dve.memset(bounds[:, 2:3], 0.0).then_inc(dve_step, 1)
            step.n = 3
            dve.sem_inc(v_free, 1)
            dve.sem_inc(mask_ready, 1)
            dve.sem_inc(way_read, 3)
            dve.sem_inc(heads_ready, 1)
            dve.sem_inc(x_added, 1)
            dve.wait_ge(dve_step, 3)
            step(dve.reduce_max(bounds[:, 1:2], qmax[:], AX.X))
            place_ones(0)
            largest_key(0)
            split()
            for t in range(T):
                for piece in range(PIECES):
                    place_mask(t, piece, t * PIECES + piece)
                    if t * PIECES + piece + 1 < HG:
                        place_ones(t * PIECES + piece + 1)
            dve.sem_inc(bounds_ready, 1)
            place_values(0, 0)
            with dve.Fori(0, B // 2) as bb:
                with dve.Fori(0, 2) as b2:
                    with dve.Fori(0, C) as c:
                        b = bb * 2 + b2
                        i = b * C + c
                        n = i * GC
                        step.restart()
                        dve.wait_ge(general_ready, i + 1)
                        step.hold()
                        way = dve.value_load(general[0:1, 0:1])
                        dve.sem_inc(way_read, 1)
                        with dve.If(i > 0):
                            divide(n - 1, GC - 1)
                            add(i - 1, (b + c + B - 1) % B * T)
                            step.restart()
                        with dve.Else():
                            step.restart()
                        place_values(n + 1, 1)
                        maxima_of(n, way)
                        step.restart()
                        with dve.If(i < B * C - 1):
                            largest_key(i + 1)
                            dve.wait_ge(stack_loaded[1], (i + 1) * (16 * PER))
                            step.hold()
                            split()
                            step.restart()
                        with dve.Else():
                            step.restart()
                        divide(n, 0)
                        dve.wait_ge(heads_ready, n + 2)
                        step.restart()
                        with dve.If(b < B - 1):
                            for piece in range(PIECES):
                                place_mask((1 - b2) * T + c, piece, (T + i) * PIECES + piece)
                            step.restart()
                        with dve.Else():
                            step.restart()
                        dve.sem_inc(bounds_ready, 1)
                        with dve.If(i < B * C - 1):
                            place_values(n + 2, 0)
                            step.restart()
                        with dve.Else():
                            step.restart()
                        maxima_of(n + 1, way)
            divide(B * H // HG - 1, GC - 1)
            add(B * C - 1, ROWS - T)
            dve.wait_ge(x_added, B * C + 1)


def self_attention(nc, a, X, ps, ident):
    ctx, sb, sem = scope(nc, "self")
    with ctx:
        wqT = sb("wqT", [P, C, HG, HG, 32])
        wkT = sb("wkT", [P, C, HG, HG, 32])
        wvT = sb("wvT", [P, C, E])
        woT = sb("woT", [P, C, E])
        bq = sb("bq", [P, HG])
        bk = sb("bk", [P, HG])
        bv = sb("bv", [P, E])
        bo = sb("bo", [P, E])
        stats = sb("stats", [P, T, 6])
        mv = sb("mv", [P, T, 2])
        ve = sb("ve", [P, T])
        rstd = sb("rstd", [P, T])
        mhalf = sb("mhalf", [P, T])
        xn = sb("xn", [P, T, E])
        xnT = sb("xnT", [P, C, S])
        NG = H // HG
        qT = sb("qT", [P, 2 * NG, S])
        kT = sb("kT", [P, 2 * NG, S])
        v = sb("v", [P, 2 * T, H, VP])
        qg = sb("qg", [P, 2, S])
        kg = sb("kg", [P, 2, HG, S])
        s = sb("s", [P, 2, 2, S])
        top = sb("top", [P, 2, TOPK // 8, 8])
        work = sb("work", [P, 2, S])
        nmax = sb("nmax", [P, 2])
        e = sb("e", [P, 2, S])
        pm = sb("pm", [P, 2, S])
        pT = sb("pT", [P, 2, T, P])
        sums = sb("sums", [P, T, HG, VP])
        recip = sb("recip", [P, T, HG])
        ao = sb("ao", [P, T, E])
        aoT = sb("aoT", [P, C, S])

        w_loaded, w_zeroed, mhalf_ready = sem("w_loaded"), sem("w_zeroed"), sem("mhalf_ready")
        var_ready, rstd_ready, xn_ready = sem("var_ready"), sem("rstd_ready"), sem("xn_ready")
        xn_turned, xnT_ready = sem("xn_turned"), sem("xnT_ready")
        qk_made, qk_copied, v_made, v_ready = sem("qk_made"), sem("qk_copied"), sem("v_made"), sem("v_ready")
        kg_ready, scores_made, scores_copied = sem("kg_ready"), sem("scores_made"), sem("scores_copied")
        first_max, scores_read = sem("first_max"), sem("scores_read")
        nmax_ready, e_ready, pm_ready, pm_turned = sem("nmax_ready"), sem("e_ready"), sem("pm_ready"), sem("pm_turned")
        pT_ready, pv_done, sums_copied, heads_ready = sem("pT_ready"), sem("pv_done"), sem("sums_copied"), sem("heads_ready")
        ao_turned, aoT_ready, proj_ready, x_added = sem("ao_turned"), sem("aoT_ready"), sem("proj_ready"), sem("x_added")
        dve_step, pool_step = sem("dve_step"), sem("pool_step")
        passed = [sem(f"passed_{e}") for e in ("act", "pe", "pool", "dve")]

        GP = HG * T // 2
        NP = NG * GP
        pair = lambda q: ps[:, q % 2, :]
        turn, made, qk, vals, turned_x, wide = (ps[:, i, :] for i in range(2, 8))
        made = made[:, 0:T * HG * VP].rearrange("p (t j v) -> p t j v", t=T, j=HG)
        where = lambda q: (q // GP, 2 * (q % GP // T), q % T)
        NORM, TURN_X, QK, V = 2, 3, 4, 8
        TURN_AO, PROJECT, ADD = 2, 3, 4

        block = ctx.enter_context(nc.Block())

        @block.sync
        def _(sp):
            sp.wait_ge(w_zeroed, 4)
            for w, name in ((wqT, "wq1T"), (wkT, "wk1T")):
                for c in range(C):
                    sp.dma_start(w[:, c, :, :, 0:D].rearrange("p g j d -> p (g j) d"),
                                 a[name][c * P:(c + 1) * P, :].rearrange("p (h d) -> p h d", d=D)).then_inc(w_loaded, 16)
            for w, name in ((bv, "bv1"), (bo, "bo1")):
                sp.dma_start(w[:], a[name].partition_broadcast(P)).then_inc(w_loaded, 16)
            for w, name in ((wvT, "wv1T"), (woT, "wo1T")):
                sp.dma_start(w[:], a[name].rearrange("(c p) n -> p c n", p=P)).then_inc(w_loaded, 16)
            for w, name in ((bq, "bq1"), (bk, "bk1")):
                for j in range(HG):
                    sp.dma_start(w[32 * j:32 * j + D, :], a[name][j]).then_inc(w_loaded, 16)

        @block.gpsimd
        def _(pool):
            step = Chain(pool, pool_step)

            def root(b):
                pool.wait_ge(var_ready, b + 1)
                pool.tensor_tensor(rstd[:], ve[:], mhalf[:], ALU.pow).then_inc(rstd_ready, 1)

            for w in (wqT, wkT, bq, bk):
                pool.memset(w[:], 0.0).then_inc(w_zeroed, 1)
            pool.memset(mhalf[:], -0.5).then_inc(mhalf_ready, 1)
            pool.memset(kg[:], 0.0).then_inc(mhalf_ready, 1)
            pool.wait_ge(mhalf_ready, 2)
            root(0)
            with pool.Fori(0, B) as b:
                for g in range(NG):
                    if g == NG - 1:
                        with pool.If(b < B - 1):
                            root(b + 1)
                    n = b * NG + g
                    pool.wait_ge(qk_copied, 2 * n + 3)
                    pool.wait_ge(scores_made, n * GP + 1)
                    step.restart()
                    step(pool.tensor_copy(qg[:, g % 2], row_tile(qT, b % 2 * NG + g)))
                    for j in range(HG):
                        rows = slice(32 * j, 32 * j + 32)
                        step(pool.tensor_copy(kg[rows, g % 2, j, :], kT[rows, bass.ds(b % 2 * NG + g, 1), :].rearrange("p a q -> p (a q)")))
                    pool.sem_inc(kg_ready, 1)

        @block.scalar
        def _(act):
            def take_x(b):
                act.wait_ge(xn_turned, b + 1)
                act.copy(xnT[:], turned_x.rearrange("p (c s) -> p c s", c=C)).then_inc(xnT_ready, 1)

            def take_qk(b, par, g):
                act.wait_ge(qk_made, b * NG + g + 1)
                act.sem_inc(passed[0], 1)
                act.activation(row_tile(qT, par * NG + g), qk[:, 0:S], ACT.Identity, bias=bq[:, g:g + 1]).then_inc(qk_copied, 1)
                act.activation(row_tile(kT, par * NG + g), qk[:, S:2 * S], ACT.Identity, bias=bk[:, g:g + 1]).then_inc(qk_copied, 1)

            def take_scores(r, q):
                act.wait_ge(scores_made, r + GP + 2)
                act.wait_ge(scores_read, r + 1)
                act.copy(s[:, q % 2].rearrange("p j k -> p (j k)"), pair(q)).then_inc(scores_copied, 1)

            act.sem_inc(pT_ready, 1)
            act.sem_inc(qk_copied, 1)
            act.sem_inc(scores_copied, 2)
            act.sem_inc(sums_copied, 1)
            take_x(0)
            act.wait_ge(w_loaded, 256)
            for g in range(NG):
                take_qk(0, 0, g)
            for q in range(2):
                take_scores(q, q)
            with act.Fori(0, B) as b:
                for q in range(NP):
                    r = b * NP + q
                    act.wait_ge(first_max, r + 1)
                    act.mul(nmax[:], top[:, :, 0, 0], -0.25).then_inc(nmax_ready, 1)
                    act.wait_ge(nmax_ready, r + 1)
                    act.wait_ge(pm_ready, 2 * r + 2)
                    for j in range(2):
                        act.activation(e[:, j], s[:, q % 2, j], ACT.Exp, scale=0.25, bias=nmax[:, j:j + 1]).then_inc(e_ready, 1)
                    act.wait_ge(e_ready, 2 * r + 2)
                    if q + 2 < NP:
                        take_scores(r + 2, q)
                    else:
                        act.sem_inc(passed[0], 1)
                        with act.If(b < B - 1):
                            take_scores(r + 2, q)
                    if q == TURN_X:
                        with act.If(b < B - 1):
                            take_x(b + 1)
                    if QK <= q < QK + NG:
                        with act.If(b < B - 1):
                            take_qk(b + 1, (b + 1) % 2, q - QK)
                    if q == TURN_AO:
                        with act.If(b > 0):
                            act.wait_ge(ao_turned, b + 1)
                            act.copy(aoT[:], wide.rearrange("p (c s) -> p c s", c=C)).then_inc(aoT_ready, 1)
                    act.wait_ge(pm_turned, r + 2)
                    act.wait_ge(pv_done, r + 1)
                    act.copy(pT[:].rearrange("p j t q -> p (j t q)"), turn).then_inc(pT_ready, 1)
                    if q % GP == GP - 1:
                        act.wait_ge(pv_done, r + 2)
                        act.wait_ge(heads_ready, b * NG + q // GP + 1)
                        act.copy(sums[:], made).then_inc(sums_copied, 1)
            act.wait_ge(ao_turned, B + 1)
            act.copy(aoT[:], wide.rearrange("p (c s) -> p c s", c=C)).then_inc(aoT_ready, 1)

        @block.tensor
        def _(pe):
            def turn_x(b):
                pe.wait_ge(xn_ready, b + 1)
                for c in range(C):
                    for t in range(T):
                        mm = pe.transpose(turned_x[:, c * S + t * P:c * S + (t + 1) * P], xn[:, t, c * P:(c + 1) * P], ident[:])
                mm.then_inc(xn_turned, 1)

            def make_qk(b, g):
                pe.wait_ge(xnT_ready, b + 1)
                pe.wait_ge(qk_copied, 2 * (b * NG + g) + 1)
                for i, w in enumerate((wqT, wkT)):
                    for c in range(C):
                        mm = pe.matmul(qk[:, i * S:(i + 1) * S], w[:, c, g].rearrange("p j d -> p (j d)"), xnT[:, c, :],
                                       start=(c == 0), stop=(c == C - 1))
                mm.then_inc(qk_made, 1)

            def make_v(b):
                pe.wait_ge(v_ready, b + 1)
                for t in range(T):
                    for c in range(C):
                        mm = pe.matmul(vals[:, t * E:(t + 1) * E], xnT[:, c, t * P:(t + 1) * P], wvT[:, c, :],
                                       start=(c == 0), stop=(c == C - 1))
                mm.then_inc(v_made, 1)

            def turn_ao(b):
                pe.wait_ge(heads_ready, (b + 1) * NG + 1)
                pe.wait_ge(x_added, b + 1)
                for c in range(C):
                    for t in range(T):
                        mm = pe.transpose(wide[:, c * S + t * P:c * S + (t + 1) * P], ao[:, t, c * P:(c + 1) * P], ident[:])
                mm.then_inc(ao_turned, 1)

            def project(b):
                pe.wait_ge(aoT_ready, b + 1)
                for t in range(T):
                    for c in range(C):
                        mm = pe.matmul(wide[:, t * E:(t + 1) * E], aoT[:, c, t * P:(t + 1) * P], woT[:, c, :],
                                       start=(c == 0), stop=(c == C - 1))
                mm.then_inc(proj_ready, 1)

            def scores(r, G, q):
                g, j, t = where(q)
                pe.wait_ge(kg_ready, G + 1)
                pe.wait_ge(scores_copied, r + 1)
                pe.matmul(pair(q), qg[:, g % 2, t * P:(t + 1) * P], kg[:, g % 2, j:j + 2, :].rearrange("p j k -> p (j k)"),
                          start=True, stop=True).then_inc(scores_made, 1)

            pe.sem_inc(pm_turned, 1)
            pe.sem_inc(pv_done, 1)
            pe.sem_inc(ao_turned, 1)
            pe.sem_inc(scores_made, GP + 1)
            turn_x(0)
            pe.wait_ge(w_loaded, 256)
            for g in range(NG):
                make_qk(0, g)
            make_v(0)
            for q in range(2):
                scores(q, 0, q)
            with pe.Fori(0, B) as b:
                for q in range(NP):
                    g, j0, t = where(q)
                    r = b * NP + q
                    if q + 2 < NP:
                        scores(r + 2, b * NG + (q + 2) // GP, q + 2)
                    else:
                        with pe.If(b < B - 1):
                            scores(r + 2, b * NG + NG, q + 2 - NP)
                    if q == TURN_X:
                        with pe.If(b < B - 1):
                            turn_x(b + 1)
                    if QK <= q < QK + NG:
                        with pe.If(b < B - 1):
                            make_qk(b + 1, q - QK)
                    if q == TURN_AO:
                        with pe.If(b > 0):
                            turn_ao(b - 1)
                    if q == PROJECT:
                        with pe.If(b > 0):
                            project(b - 1)
                    if q == V:
                        with pe.If(b < B - 1):
                            make_v(b + 1)
                    pe.wait_ge(pm_ready, 2 * r + 4)
                    pe.wait_ge(pT_ready, r + 1)
                    for i in range(2):
                        for k in range(T):
                            mm = pe.transpose(turn[:, (i * T + k) * P:(i * T + k + 1) * P], pm[:, i, k * P:(k + 1) * P], ident[:])
                    mm.then_inc(pm_turned, 1)
                    pe.wait_ge(pT_ready, r + 2)
                    if q == 0:
                        pe.wait_ge(v_ready, b + 2)
                    if q % GP == 0:
                        pe.wait_ge(sums_copied, b * NG + g + 1)
                    pe.sem_inc(passed[1], 1)
                    for i in range(2):
                        for k in range(T):
                            mm = pe.matmul(made[:, t, j0 + i, :], pT[:, i, k, :],
                                           v[:, bass.ds(b % 2 * T + k, 1), g * HG + j0 + i, :].rearrange("p a v -> p (a v)"),
                                           start=(k == 0), stop=(k == T - 1))
                    mm.then_inc(pv_done, 1)
            turn_ao(B - 1)
            project(B - 1)

        @block.vector
        def _(dve):
            step = Chain(dve, dve_step)

            def normalise(b, bt, first=False):
                step.restart()
                for t in range(T):
                    step(dve.bn_stats(stats[:, t], row_tile(X, bt + t)))
                    step(dve.bn_aggr(mv[:, t], stats[:, t]))
                dve.tensor_scalar(ve[:], mv[:, :, 1], EPS, None, ALU.add).then_inc(var_ready, 1)
                dve.wait_ge(rstd_ready, b + 1)
                step.hold()
                for t in range(T):
                    step(dve.tensor_scalar(xn[:, t], row_tile(X, bt + t), mv[:, t, 0:1], rstd[:, t:t + 1], ALU.subtract, ALU.mult))
                dve.sem_inc(xn_ready, 1)
                if first:
                    dve.wait_ge(w_loaded, 256)
                for t in range(T):
                    step(dve.tensor_tensor(row_tile(X, bt + t), row_tile(X, bt + t), bo[:], ALU.add))
                step.restart()

            def add_v(b, par):
                step.restart()
                dve.wait_ge(v_made, b + 1)
                step.hold()
                for t in range(T):
                    step(dve.tensor_tensor(v[:, bass.ds(par * T + t, 1), :, 0:D].rearrange("p a h d -> p (a h) d"),
                                           vals[:, t * E:(t + 1) * E].rearrange("p (h d) -> p h d", d=D),
                                           bv[:].rearrange("p (h d) -> p h d", d=D), ALU.add))
                dve.sem_inc(v_ready, 1)
                step.restart()

            def divide(n, g):
                dve.wait_ge(sums_copied, n + 2)
                step(dve.reciprocal(recip[:], sums[:, :, :, D]))
                dve.tensor_tensor(ao[:, :, g * HG * D:(g + 1) * HG * D].rearrange("p t (j d) -> p t j d", d=D), sums[:, :, :, 0:D],
                                  recip[:].unsqueeze(3).to_broadcast([P, T, HG, D]), ALU.mult).then_inc(heads_ready, 1)

            def add(b, bt):
                dve.wait_ge(proj_ready, b + 1)
                step.restart()
                for t in range(T):
                    step(dve.tensor_tensor(row_tile(X, bt + t), row_tile(X, bt + t), wide[:, t * E:(t + 1) * E], ALU.add))
                dve.sem_inc(x_added, 1)
                step.restart()

            def select(r, q):
                dve.wait_ge(scores_copied, r + 3)
                step.restart()
                done = [0, 0]

                def next(i, ins):
                    step.n += 1
                    ins.then_inc(dve_step, 1)
                    done[i] = step.n

                for turn in range(TOPK // 8):
                    for i in range(2):
                        if done[i]:
                            dve.wait_ge(dve_step, done[i])
                        if turn == 1 and i == 1:
                            dve.sem_inc(scores_read, 1)
                        next(i, dve.max(top[:, i, turn], s[:, q % 2, i] if turn == 0 else work[:, i]))
                    for i in range(2):
                        if turn == 0 and i == 0:
                            dve.wait_ge(pm_ready, 2 * r + 2)
                            dve.sem_inc(passed[3], 1)
                        dve.wait_ge(dve_step, done[i])
                        if turn == 0 and i == 1:
                            dve.sem_inc(first_max, 1)
                        next(i, dve.match_replace(work[:, i], top[:, i, turn], s[:, q % 2, i] if turn == 0 else work[:, i], LOW))
                dve.wait_ge(e_ready, 2 * r + 2)
                dve.wait_ge(pm_turned, r + 1)
                dve.sem_inc(passed[3], 1)
                for i in range(2):
                    dve.wait_ge(dve_step, done[i])
                    dve.scalar_tensor_tensor(out=pm[:, i], in0=work[:, i], scalar=LOW, in1=e[:, i], op0=ALU.is_equal, op1=ALU.mult).then_inc(pm_ready, 1)

            dve.memset(v[:], 1.0).then_inc(dve_step, 1)
            step.n = 1
            dve.wait_ge(dve_step, 1)
            dve.sem_inc(scores_read, 2)
            dve.sem_inc(pm_ready, 2)
            dve.sem_inc(heads_ready, 1)
            dve.sem_inc(v_ready, 1)
            dve.sem_inc(x_added, 1)
            normalise(0, 0, first=True)
            add_v(0, 0)
            with dve.Fori(0, B) as b:
                for q in range(NP):
                    select(b * NP + q, q)
                    step.hold()
                    if q == 0:
                        with dve.If(b > 0):
                            step.restart()
                            divide(b * NG - 1, NG - 1)
                            step.restart()
                        with dve.Else():
                            step.restart()
                    elif q % GP == 0:
                        if q == GP:
                            dve.wait_ge(ao_turned, b + 1)
                            step.hold()
                        divide(b * NG + q // GP - 1, q // GP - 1)
                    if q == NORM:
                        with dve.If(b < B - 1):
                            normalise(b + 1, (b + 1) % B * T)
                        with dve.Else():
                            step.restart()
                    if q == ADD:
                        with dve.If(b > 0):
                            add(b - 1, (b + B - 1) % B * T)
                        with dve.Else():
                            step.restart()
                    if q == V + 1:
                        with dve.If(b < B - 1):
                            add_v(b + 1, (b + 1) % 2)
                        with dve.Else():
                            step.restart()
            step.restart()
            divide(B * NG - 1, NG - 1)
            add(B - 1, ROWS - T)


def argmax_rows(dve, sem, lg, best, idx, idxf, oh, count):
    for r in range(ROWS):
        dve.max(best[:, r], lg[:, r]).then_inc(sem, 1)
    dve.wait_ge(sem, ROWS)
    for r in range(ROWS):
        dve.max_index(idx[:, r], best[:, r], lg[:, r]).then_inc(sem, 1)
    dve.wait_ge(sem, 2 * ROWS)
    dve.tensor_copy(idxf[:], idx[:, :, 0]).then_inc(sem, 1)
    dve.wait_ge(sem, 2 * ROWS + 1)
    for r in range(ROWS):
        dve.tensor_scalar(oh[:, r], count[:], idxf[:, r:r + 1], None, ALU.is_equal).then_inc(sem, 1)
    dve.wait_ge(sem, 3 * ROWS + 1)


def experts(nc, a, X, ps, ident):
    ctx, sb, sem = scope(nc, "moe")
    with ctx:
        norm = Norm(sb, sem, [ps[:, 0, :], ps[:, 1, :]])
        wg = sb("wg", [P, C, EX])
        we = sb("we", [P, C, E])
        be = sb("be", [P, E])
        count = sb("count", [P, EX])
        upto = sb("upto", [P, P])
        ones = sb("ones", [P, P])
        lg = sb("lg", [P, ROWS, EX])
        best = sb("best", [P, ROWS, 8])
        idx = sb("idx", [P, ROWS, 8], U32)
        idxf = sb("idxf", [P, ROWS])
        oh = sb("oh", [P, ROWS, EX])
        nmax = sb("nmax", [P, ROWS])
        ex = sb("ex", [P, ROWS, EX])
        den = sb("den", [P, ROWS])
        gate = sb("gate", [P, ROWS])
        place = sb("place", [P, ROWS, EX])
        rank = sb("rank", [P, ROWS])
        keep = sb("keep", [P, ROWS])
        hb = sb("hb", [P, ROWS, E])

        loaded, consts, consts2 = sem("loaded"), sem("consts"), sem("consts2")
        lg_made, h_made, nmax_ready, den_ready = sem("lg_made"), sem("h_made"), sem("nmax_ready"), sem("den_ready")
        best_found, oh_ready, place_made = sem("best_found"), sem("oh_ready"), sem("place_made")
        h_ready, x_added, dve_step = sem("h_ready"), sem("x_added"), sem("dve_step")
        hp = lambda i: ps[:, 2 + i, :].rearrange("p (t n) -> p t n", t=2)
        pp = ps[:, 6, 0:ROWS * EX].rearrange("p (r e) -> p r e", r=ROWS)
        lgp = ps[:, 7, 0:ROWS * EX].rearrange("p (r e) -> p r e", r=ROWS)
        BANKS = ROWS // 2

        block = ctx.enter_context(nc.Block())

        @block.sync
        def _(sp):
            sp.dma_start(wg[:], a["wg"].rearrange("(c p) n -> p c n", p=P)).then_inc(loaded, 16)
            sp.dma_start(we[:], a["we"].rearrange("(c p) n -> p c n", p=P)).then_inc(loaded, 16)
            sp.dma_start(be[:], a["be"].partition_broadcast(P)).then_inc(loaded, 16)

        @block.gpsimd
        def _(pool):
            pool.memset(norm.mhalf[:], -0.5).then_inc(consts, 1)
            pool.memset(ones[:], 1.0).then_inc(consts, 1)
            pool.memset(upto[:], 1.0).then_inc(consts, 1)
            pool.iota(count[:], pattern=[[1, EX]], base=0, channel_multiplier=0, allow_small_or_imprecise_dtypes=True).then_inc(consts, 1)
            pool.wait_ge(consts, 4)
            norm.gpsimd(pool)
            pool.affine_select(out=upto[:], in_=upto[:], compare_op=ALU.is_ge, fill=0.0, base=0,
                               pattern=[[1, P]], channel_multiplier=-1).then_inc(consts2, 1)

        @block.scalar
        def _(act):
            norm.scalar(act)
            act.wait_ge(nmax_ready, 1)
            for r in range(ROWS):
                act.activation(ex[:, r], lg[:, r], ACT.Exp, bias=nmax[:, r:r + 1], accum_out=den[:, r:r + 1]).then_inc(den_ready, 1)

        @block.tensor
        def _(pe):
            norm.tensor(pe, ident)
            pe.wait_ge(loaded, 48)
            pe.wait_ge(norm.xnT_ready, B)
            for r in range(ROWS):
                for c in range(C):
                    mm = pe.matmul(lgp[:, r], norm.xnT[:, c, r * P:(r + 1) * P], wg[:, c, :], start=(c == 0), stop=(c == C - 1))
            mm.then_inc(lg_made, 1)
            for r in range(ROWS):
                for c in range(C):
                    mm = pe.matmul(hp(r // 2)[:, r % 2], norm.xnT[:, c, r * P:(r + 1) * P], we[:, c, :], start=(c == 0), stop=(c == C - 1))
                if r % 2:
                    mm.then_inc(h_made, 1)
            pe.wait_ge(consts2, 1)
            pe.wait_ge(oh_ready, 1)
            for r in range(ROWS):
                for before in range(r):
                    pe.matmul(pp[:, r], ones[:], oh[:, before], start=(before == 0), stop=False)
                mm = pe.matmul(pp[:, r], upto[:], oh[:, r], start=(r == 0), stop=True)
            mm.then_inc(place_made, 1)

        @block.vector
        def _(dve):
            step = Chain(dve, dve_step)
            norm.vector(dve, X)
            dve.wait_ge(loaded, 48)
            dve.wait_ge(consts, 4)
            dve.wait_ge(lg_made, 1)
            step(dve.tensor_copy(lg[:], lgp))
            argmax_rows(dve, best_found, lg, best, idx, idxf, oh, count)
            dve.sem_inc(oh_ready, 1)
            dve.tensor_scalar(nmax[:], best[:, :, 0], -1.0, None, ALU.mult).then_inc(nmax_ready, 1)
            for i in range(BANKS):
                dve.wait_ge(h_made, i + 1)
                dve.tensor_tensor(hb[:, 2 * i:2 * i + 2], hp(i), be[:].unsqueeze(1).to_broadcast([P, 2, E]), ALU.add).then_inc(h_ready, 1)
            dve.wait_ge(den_ready, ROWS)
            step(dve.reciprocal(gate[:], den[:]))
            dve.wait_ge(place_made, 1)
            step(dve.tensor_tensor(place[:], pp, oh[:], ALU.mult))
            step(dve.reduce_sum(rank[:], place[:], AX.X))
            step(dve.tensor_scalar(keep[:], rank[:], float(CAP), None, ALU.is_le))
            step(dve.tensor_tensor(keep[:], keep[:], gate[:], ALU.mult))
            dve.wait_ge(h_ready, BANKS)
            for r in range(ROWS):
                dve.scalar_tensor_tensor(out=X[:, r], in0=hb[:, r], scalar=keep[:, r:r + 1], in1=X[:, r],
                                         op0=ALU.mult, op1=ALU.add).then_inc(x_added, 1)
            dve.wait_ge(x_added, ROWS)


def context_attention(nc, a, X, ps, ident):
    ctx, sb, sem = scope(nc, "ctx")
    with ctx:
        norm = Norm(sb, sem, [ps[:, 4, :], ps[:, 5, :]])
        M, MW = 4, SK // 4
        W = 8
        wq = sb("wq", [P, C, E])
        wk = sb("wk", [P, C, E])
        wvT = sb("wvT", [P, C, E])
        G = sb("G", [P, C, E])
        qT = sb("qT", [P, C, S])
        kx = sb("kx", [P, M, C, MW])
        vx = sb("vx", [P, KT, E])
        sc = sb("sc", [P, T, SK])
        mx = sb("mx", [P, T, M])
        nmax = sb("nmax", [P, T])
        den = sb("den", [P, T, M])
        recip = sb("recip", [P, T])
        pT = sb("pT", [P, 2, 4 * P])
        o = sb("o", [P, T, E])
        oT = sb("oT", [P, C, S])

        loaded, g_made, g_copied, consts = sem("loaded"), sem("g_made"), sem("g_copied"), sem("consts")
        k_loaded = [sem(f"k_loaded{m}") for m in range(M)]
        v_loaded = [sem(f"v_loaded{m}") for m in range(M)]
        q_made, qT_ready, scores_made, scores_copied = sem("q_made"), sem("qT_ready"), sem("scores_made"), sem("scores_copied")
        mx_ready, nmax_ready, exp_ready = sem("mx_ready"), sem("nmax_ready"), sem("exp_ready")
        turned, pT_ready, pv_done, o_ready = sem("turned"), sem("pT_ready"), sem("pv_done"), sem("o_ready")
        o_turned, oT_ready, proj_ready, dve_step = sem("o_turned"), sem("oT_ready"), sem("proj_ready"), sem("dve_step")
        x_added, passed = sem("x_added"), sem("passed")
        MC, WC = T * M, T * W

        slot = lambda m: ps[:, 2 * (m % 2):2 * (m % 2) + 2, :]
        turn = lambda w: ps[:, 4 + w % 2, :]
        acc, wide = ps[:, 6, 0:E], ps[:, 7, :]

        block = ctx.enter_context(nc.Block())

        @block.sync
        def _(sp):
            for w, name in ((wq, "wq2"), (wk, "wk2"), (wvT, "wv2T")):
                sp.dma_start(w[:], a[name].rearrange("(c p) n -> p c n", p=P)).then_inc(loaded, 16)
            with sp.Fori(0, B) as b:
                for m in range(M):
                    sp.wait_ge(scores_made, MC * b + M + m + 1)
                    for c in range(C):
                        sp.dma_start(kx[:, m, c, :], a["ctxT"][bass.ds(b * C + c, 1), :, m * MW:(m + 1) * MW].rearrange("a p k -> p (a k)")).then_inc(k_loaded[m], 16)
                for m in range(M):
                    sp.wait_ge(pv_done, WC * b + W + 2 * m + 2)
                    sp.dma_start(vx[:, m * 8:(m + 1) * 8, :], a["ctx"][bass.ds(b, 1), m * MW:(m + 1) * MW, :]
                                 .rearrange("a (k p) d -> p (a k) d", p=P)).then_inc(v_loaded[m], 16)

        @block.gpsimd
        def _(pool):
            pool.memset(norm.mhalf[:], -0.5).then_inc(consts, 1)
            pool.wait_ge(consts, 1)
            norm.gpsimd(pool)

        @block.scalar
        def _(act):
            act.sem_inc(scores_copied, 2)
            norm.scalar(act)
            act.wait_ge(g_made, 1)
            act.copy(G[:].rearrange("p c n -> p (c n)"), wide).then_inc(g_copied, 1)
            with act.Fori(0, B) as b:
                act.wait_ge(q_made, b + 1)
                act.copy(qT[:].rearrange("p c s -> p (c s)"), wide).then_inc(qT_ready, 1)
                for t in range(T):
                    for m in range(M):
                        n = (b * T + t) * M + m
                        act.wait_ge(scores_made, MC + n + 1)
                        act.copy(sc[:, t, m * MW:(m + 1) * MW], slot(m).rearrange("p a k -> p (a k)")).then_inc(scores_copied, 1)
                for t in range(T):
                    act.wait_ge(nmax_ready, b * T + t + 1)
                    for m in range(M):
                        part = sc[:, t, m * MW:(m + 1) * MW]
                        act.activation(part, part, ACT.Exp, scale=1.0 / 16.0, bias=nmax[:, t:t + 1], accum_out=den[:, t, m:m + 1]).then_inc(exp_ready, 1)
                act.wait_ge(o_turned, b + 1)
                act.copy(oT[:].rearrange("p c s -> p (c s)"), wide).then_inc(oT_ready, 1)

        @block.tensor
        def _(pe):
            pe.sem_inc(scores_made, MC)
            pe.sem_inc(pv_done, WC)
            norm.tensor(pe, ident)
            pe.wait_ge(loaded, 48)
            for i in range(C):
                for c in range(C):
                    mm = pe.matmul(wide[:, i * E:(i + 1) * E], wq[:, c, i * P:(i + 1) * P], wk[:, c, :], start=(c == 0), stop=(c == C - 1))
            mm.then_inc(g_made, 1)
            pe.wait_ge(g_copied, 1)
            pe.wait_ge(norm.xnT_ready, B)
            with pe.Fori(0, B) as b:
                pe.wait_ge(x_added, (b + 1) * T)
                pe.sem_inc(passed, 1)
                for j in range(C):
                    for c in range(C):
                        mm = pe.matmul(wide[:, j * S:(j + 1) * S], G[:, c, j * P:(j + 1) * P], norm.xnT[:, c, bass.ds(b * S, S)],
                                       start=(c == 0), stop=(c == C - 1))
                mm.then_inc(q_made, 1)
                pe.wait_ge(qT_ready, b + 1)
                for t in range(T):
                    for m in range(M):
                        n = (b * T + t) * M + m
                        if t == 0:
                            pe.wait_ge(k_loaded[m], 16 * C * (b + 1))
                        pe.wait_ge(scores_copied, n + 1)
                        for w in range(2):
                            for c in range(C):
                                mm = pe.matmul(slot(m)[:, w, :], qT[:, c, t * P:(t + 1) * P], kx[:, m, c, w * 512:(w + 1) * 512], start=(c == 0), stop=(c == C - 1))
                        mm.then_inc(scores_made, 1)
                for t in range(T):
                    n = (b * T + t) * W

                    def product(w):
                        if t == 0 and w % 2 == 0:
                            pe.wait_ge(v_loaded[w // 2], 16 * (b + 1))
                        if w == 0:
                            pe.wait_ge(o_ready, b * T + t + 1)
                        pe.wait_ge(pT_ready, n + w + 3)
                        for i in range(4):
                            mm = pe.matmul(acc, pT[:, w % 2, i * P:(i + 1) * P], vx[:, 4 * w + i, :], start=(w == 0 and i == 0), stop=(w == W - 1 and i == 3))
                        mm.then_inc(pv_done, 1)

                    for w in range(W):
                        pe.wait_ge(exp_ready, (b * T + t) * M + w // 2 + 1)
                        pe.wait_ge(pT_ready, n + w + 1)
                        for i in range(4):
                            k = 4 * w + i
                            mm = pe.transpose(turn(w)[:, i * P:(i + 1) * P], sc[:, t, k * P:(k + 1) * P], ident[:])
                        mm.then_inc(turned, 1)
                        if w >= 1:
                            product(w - 1)
                    product(W - 1)
                pe.wait_ge(o_ready, b * T + T + 1)
                for c in range(C):
                    for t in range(T):
                        mm = pe.transpose(wide[:, c * S + t * P:c * S + (t + 1) * P], o[:, t, c * P:(c + 1) * P], ident[:])
                mm.then_inc(o_turned, 1)
                pe.wait_ge(oT_ready, b + 1)
                for t in range(T):
                    for c in range(C):
                        mm = pe.matmul(wide[:, t * E:(t + 1) * E], oT[:, c, t * P:(t + 1) * P], wvT[:, c, :], start=(c == 0), stop=(c == C - 1))
                mm.then_inc(proj_ready, 1)

        @block.vector
        def _(dve):
            step = Chain(dve, dve_step)
            dve.sem_inc(pT_ready, 2)
            dve.sem_inc(o_ready, 1)
            dve.sem_inc(x_added, T)
            norm.vector(dve, X)
            with dve.Fori(0, B) as b:
                step.restart()
                tile = lambda t: row_tile(X, b * T + t)
                for t in range(T):
                    for m in range(M):
                        n = (b * T + t) * M + m
                        dve.wait_ge(scores_copied, n + 3)
                        dve.reduce_max(mx[:, t, m:m + 1], sc[:, t, m * MW:(m + 1) * MW], AX.X).then_inc(mx_ready, 1)
                    dve.wait_ge(mx_ready, (b * T + t + 1) * M)
                    step(dve.reduce_max(nmax[:, t:t + 1], mx[:, t], AX.X))
                    dve.tensor_scalar(nmax[:, t:t + 1], nmax[:, t:t + 1], -1.0 / 16.0, None, ALU.mult).then_inc(nmax_ready, 1)
                for t in range(T):
                    for w in range(W):
                        n = (b * T + t) * W + w
                        dve.wait_ge(turned, n + 1)
                        dve.wait_ge(pv_done, WC + n - 1)
                        dve.tensor_copy(pT[:, w % 2], turn(w)).then_inc(pT_ready, 1)
                    dve.wait_ge(exp_ready, (b * T + t + 1) * M)
                    step(dve.reduce_sum(recip[:, t:t + 1], den[:, t], AX.X))
                    step(dve.reciprocal(recip[:, t:t + 1], recip[:, t:t + 1]))
                    dve.wait_ge(pv_done, WC + (b * T + t + 1) * W)
                    dve.tensor_scalar(o[:, t], acc, recip[:, t:t + 1], None, ALU.mult).then_inc(o_ready, 1)
                dve.wait_ge(proj_ready, b + 1)
                step.hold()
                for t in range(T):
                    dve.tensor_tensor(tile(t), tile(t), wide[:, t * E:(t + 1) * E], ALU.add).then_inc(x_added, 1)
                dve.wait_ge(x_added, T * b + 2 * T)


N_STATE = 16
TAPS = 4
RANK = 8
TIME = B * S
HALVES = TIME // 512


def state_space(nc, a, X, ps, ident):
    ctx, sb, sem = scope(nc, "ssm")
    with ctx:
        norm = Norm(sb, sem, [ps[:, 0, :], ps[:, 1, :]], turned=False)
        nw, nb = sb("nw", [P, E]), sb("nb", [P, E])
        win = sb("win", [P, 2, 4 * P])
        cw, cb = sb("cw", [P, 2, C, TAPS]), sb("cb", [P, 2, C])
        wx = sb("wx", [P, 2, C, RANK + 2 * N_STATE])
        wdt = sb("wdt", [40, 2, E])
        bdt = sb("bdt", [P, 2, C])
        alog = sb("alog", [P, 2, C, N_STATE])
        dcol = sb("dcol", [P, 2, C])
        wout = sb("wout", [P, 2, C, P])
        A = sb("A", [P, 2, C, N_STATE])
        sel = sb("sel", [96, 2 * N_STATE, P], BF16)
        diag = sb("diag", [P, C, P])
        mirror = sb("mirror", [P, P])
        xT = sb("xT", [P, 2, B, S])
        xcp = sb("xcp", [P, C, B, S + TAPS - 1])
        sz = sb("sz", [P, C, TIME])
        cv = sb("cv", [P, C, TIME])
        xc = sb("xc", [P, C, TIME])
        bc = sb("bc", [96, TIME], BF16)
        bcr = sb("bcr", [32, TIME])
        dtr = sb("dtr", [40, TIME])
        v = sb("v", [P, C, TIME])
        dt = sb("dt", [P, C, TIME])
        du = sb("du", [P, C, TIME])
        decay = [sb(f"decay{i}", [P, C, TIME]) for i in range(2)]
        brow = [sb(f"brow{i}", [P, TIME]) for i in range(2)]
        bu = [sb(f"bu{i}", [P, C, TIME]) for i in range(2)]
        h = sb("h", [P, C, TIME])
        hc = [sb(f"hc{i}", [P, C, TIME]) for i in range(2)]

        loaded, consts, zeroed = sem("loaded"), sem("consts"), sem("zeroed")
        ln_added, ln_scaled, ln_ready, ln_turned = sem("ln_added"), sem("ln_scaled"), sem("ln_ready"), sem("ln_turned")
        h_done, mirror_ready = sem("h_done"), sem("mirror_ready")
        a_exp, a_ready, sel_ready = sem("a_exp"), sem("a_ready"), sem("sel_ready")
        xT_ready, xz_made, xc_copied, sz_ready = sem("xT_ready"), sem("xz_made"), sem("xc_copied"), sem("sz_ready")
        cv_ready, xc_ready, xd_made, bc_ready, dtr_ready = sem("cv_ready"), sem("xc_ready"), sem("xd_made"), sem("bc_ready"), sem("dtr_ready")
        dt_made, v_ready, l_ready, dt_ready, diag_ready = sem("dt_made"), sem("v_ready"), sem("l_ready"), sem("dt_ready"), sem("diag_ready")
        act_step, dve_step, du_ready = sem("act_step"), sem("dve_step"), sem("du_ready")
        b_copied = sem("b_copied")
        b_made, c_made, bu_done, hc_ready, summed = sem("b_made"), sem("c_made"), sem("bu_done"), sem("hc_ready"), sem("summed")
        decay_ready, scanned, gated, out_made, x_added = sem("decay_ready"), sem("scanned"), sem("gated"), sem("out_made"), sem("x_added")

        two = lambda i: ps[:, 2 * i:2 * i + 2, :]
        flat = lambda v: v.rearrange("p a q -> p (a q)")
        spreadk = lambda i: flat(two(i)).unsqueeze(1).to_broadcast([P, C, TIME])
        PAIRS = N_STATE // 2

        def each_pair(eng, body):
            with eng.Fori(0, PAIRS - 1) as i:
                body(2 * i, False)
            body(N_STATE - 2, True)

        block = ctx.enter_context(nc.Block())

        @block.sync
        def _(sp):
            for w, name in ((nw, "nw"), (nb, "nb")):
                sp.dma_start(w[:], a[name].partition_broadcast(P)).then_inc(loaded, 16)
            for w, name in ((win, "win"), (cw, "cw"), (cb, "cb"), (wx, "wx"), (bdt, "bdt"), (alog, "alog"), (dcol, "dcol"), (wout, "wout")):
                sp.dma_start(w[:], a[name]).then_inc(loaded, 16)
            sp.dma_start(wdt[32:32 + RANK], a["wdt"]).then_inc(loaded, 16)

        LOADS = 16 * 11

        @block.gpsimd
        def _(pool):
            pool.memset(norm.mhalf[:], -0.5).then_inc(consts, 1)
            pool.memset(mirror[:], 0.0).then_inc(consts, 1)
            pool.wait_ge(consts, 2)
            pool.affine_select(out=mirror[:], in_=mirror[:], compare_op=ALU.not_equal, fill=1.0, base=1 - P,
                               pattern=[[1, P]], channel_multiplier=1).then_inc(mirror_ready, 1)
            norm.gpsimd(pool, 0)
            norm.gpsimd(pool, 1)
            pool.memset(xcp[:], 0.0).then_inc(zeroed, 1)
            pool.sem_inc(bu_done, 2)
            for d in range(2):
                pool.wait_ge(du_ready, C * d + C)

                def inputs(n, last):
                    for j in range(2):
                        N = d * N_STATE + n + j
                        pool.wait_ge(b_copied, N + 1)
                        pool.wait_ge(scanned, N + 1)
                        pool.tensor_tensor(bu[j][:], brow[j][:].unsqueeze(1).to_broadcast([P, C, TIME]), du[:], ALU.mult).then_inc(bu_done, 1)

                each_pair(pool, inputs)

        @block.scalar
        def _(act):
            act.sem_inc(decay_ready, 1)
            act.wait_ge(loaded, LOADS)
            act.activation(A[:], alog[:], ACT.Exp).then_inc(a_exp, 1)
            for b in range(B):
                act.wait_ge(ln_turned, b + 1)
                act.copy(xT[:, :, b, :], norm.banks[b % 2].rearrange("p (d s) -> p d s", d=2)).then_inc(xT_ready, 1)
            act.wait_ge(zeroed, 1)
            for d in range(2):
                act.wait_ge(xz_made, 4 * d + 2)
                if d:
                    act.wait_ge(cv_ready, C * d)
                for k in range(C):
                    act.copy(xcp[:, k, :, TAPS - 1:], flat(two(k)).rearrange("p (b s) -> p b s", b=B)).then_inc(xc_copied, 1)
                act.wait_ge(xz_made, 4 * d + 4)
                for k in range(C):
                    act.activation(sz[:, k], flat(two(2 + k)), ACT.Silu).then_inc(sz_ready, 1)
                for k in range(C):
                    act.wait_ge(cv_ready, C * d + k + 1)
                    act.activation(xc[:, k], cv[:, k], ACT.Silu).then_inc(xc_ready, 1)
                act.wait_ge(xd_made, d + 1)
                act.copy(dtr[32:32 + RANK], flat(two(0))[32:32 + RANK]).then_inc(dtr_ready, 1)
                for k in range(C):
                    n = 2 * (C * d + k)
                    act.wait_ge(dt_made, C * d + k + 1)
                    act.activation(v[:, k], flat(two(1 + k)), ACT.Identity, bias=bdt[:, d, k:k + 1]).then_inc(v_ready, 1)
                    act.wait_ge(v_ready, C * d + k + 1)
                    act.activation(dt[:, k], v[:, k], ACT.Abs).then_inc(act_step, 1)
                    act.wait_ge(act_step, n + 1)
                    act.activation(dt[:, k], dt[:, k], ACT.Exp, scale=-1.0).then_inc(act_step, 1)
                    act.wait_ge(act_step, n + 2)
                    act.activation(dt[:, k], dt[:, k], ACT.Ln, bias=1.0).then_inc(l_ready, 1)
                act.wait_ge(dt_ready, C * d + C)
                act.wait_ge(a_ready, 1)

                def decays(n, last):
                    for j in range(2):
                        N = d * N_STATE + n + j
                        act.wait_ge(b_made, N + 1)
                        act.wait_ge(bu_done, N + 1)
                        act.copy(brow[j][:], flat(two(2))).then_inc(b_copied, 1)
                        act.wait_ge(scanned, N + 1)
                        for k in range(C):
                            ins = act.activation(decay[j][:, k], dt[:, k], ACT.Exp, scale=A[:, d, k, bass.ds(n + j, 1)])
                        ins.then_inc(decay_ready, 1)

                each_pair(act, decays)

        @block.tensor
        def _(pe):
            pe.sem_inc(summed, 2)
            pe.wait_ge(mirror_ready, 1)
            for b in range(B):
                bank = norm.banks[b % 2]
                pe.wait_ge(ln_ready, (b + 1) * T)
                if b >= 2:
                    pe.wait_ge(xT_ready, b - 1)
                for t in range(T):
                    pe.transpose(bank[:, t * P:(t + 1) * P], norm.xn[:, b * T + t, 0:P], ident[:])
                    mm = pe.transpose(bank[:, S + (T - 1 - t) * P:S + (T - t) * P], norm.xn[:, b * T + t, P:2 * P], mirror[:])
                mm.then_inc(ln_turned, 1)
            pe.wait_ge(xT_ready, B)
            pe.wait_ge(loaded, LOADS)
            for d in range(2):
                if d:
                    pe.wait_ge(gated, 1)
                    pe.wait_ge(x_added, 1)
                for m in range(4):
                    for w in range(HALVES):
                        mm = pe.matmul(two(m)[:, w, :], win[:, d, m * P:(m + 1) * P], xT[:, d, 2 * w:2 * w + 2, :].rearrange("p b s -> p (b s)"),
                                       start=True, stop=True)
                    mm.then_inc(xz_made, 1)
                pe.wait_ge(xc_ready, C * d + C)
                pe.wait_ge(xc_copied, C * d + C)
                for w in range(HALVES):
                    for k in range(C):
                        mm = pe.matmul(two(0)[0:40, w, :], wx[:, d, k, :], xc[:, k, w * 512:(w + 1) * 512], start=(k == 0), stop=(k == C - 1))
                mm.then_inc(xd_made, 1)
                pe.wait_ge(dtr_ready, d + 1)
                pe.wait_ge(sz_ready, C * d + C)
                for k in range(C):
                    for w in range(HALVES):
                        mm = pe.matmul(two(1 + k)[:, w, :], wdt[32:32 + RANK, d, k * P:(k + 1) * P], dtr[32:32 + RANK, w * 512:(w + 1) * 512],
                                       start=True, stop=True)
                    mm.then_inc(dt_made, 1)
                pe.wait_ge(diag_ready, d + 1)
                pe.wait_ge(sel_ready, 1)
                pe.wait_ge(bc_ready, d + 1)
                pe.wait_ge(v_ready, C * d + C)
                for k in range(C):
                    for w in range(HALVES):
                        pe.matmul(two(k)[:, w, :], diag[:, k, :], xc[:, k, w * 512:(w + 1) * 512], start=True, stop=False, skip_group_check=True)

                def spread(i, row):
                    for w in range(HALVES):
                        mm = pe.matmul(two(i)[:, w, :], sel[:, bass.ds(row, 1), :].rearrange("p a m -> p (a m)"), bc[:, w * 512:(w + 1) * 512],
                                       start=True, stop=True)
                    return mm

                spread(2, 0).then_inc(b_made, 1)
                pe.wait_ge(b_copied, d * N_STATE + 1)
                spread(2, 1).then_inc(b_made, 1)

                def add_state(N, j, last=False):
                    pe.wait_ge(hc_ready, N + 2)
                    for k in range(C):
                        for w in range(HALVES):
                            mm = pe.matmul(two(k)[:, w, :], ident[:], hc[j][:, k, w * 512:(w + 1) * 512], start=False,
                                           stop=last, skip_group_check=True)
                    mm.then_inc(summed, 1)

                def states(n, last, first=False):
                    for j in range(2):
                        N = d * N_STATE + n + j
                        pe.wait_ge(hc_ready, N + 1)
                        spread(3, N_STATE + n + j).then_inc(c_made, 1)
                        if not (first and j == 0):
                            add_state(N - 1, 1 - j)
                        if not last:
                            pe.wait_ge(b_copied, N + 2)
                            spread(2, n + j + 2).then_inc(b_made, 1)

                states(0, False, first=True)
                with pe.Fori(1, PAIRS - 1) as i:
                    states(2 * i, False)
                states(N_STATE - 2, True)
                add_state((d + 1) * N_STATE - 1, 1, last=True)
                pe.wait_ge(gated, d + 1)
                out = flat(two(2)).rearrange("p (r n) -> p r n", n=P)
                for r in range(ROWS):
                    for k in range(C):
                        mm = pe.matmul(out[:, r], cv[:, k, r * P:(r + 1) * P], wout[:, d, k, :], start=(k == 0), stop=(k == C - 1))
                mm.then_inc(out_made, 1)

        @block.vector
        def _(dve):
            step = Chain(dve, dve_step)
            dve.sem_inc(scanned, 2)
            dve.sem_inc(hc_ready, 1)
            norm.vector(dve, X, 0)
            dve.wait_ge(norm.xn_ready, ROWS)
            for r in range(ROWS):
                dve.tensor_tensor(X[:, r], X[:, r], norm.xn[:, r], ALU.add).then_inc(ln_added, 1)
            dve.wait_ge(ln_added, ROWS)
            norm.vector(dve, norm.xn, 1)
            dve.wait_ge(loaded, LOADS)
            dve.wait_ge(norm.xn_ready, 2 * ROWS)
            for r in range(ROWS):
                dve.tensor_tensor(norm.xn[:, r], norm.xn[:, r], nw[:], ALU.mult).then_inc(ln_scaled, 1)
            for r in range(ROWS):
                dve.wait_ge(ln_scaled, r + 1)
                dve.tensor_tensor(norm.xn[:, r], norm.xn[:, r], nb[:], ALU.add).then_inc(ln_ready, 1)
            for i in range(3):
                step(dve.tensor_copy(sel[32 * i:32 * i + 32], ident[32 * i:32 * i + 32, 32 * i:32 * i + 32].unsqueeze(2).to_broadcast([32, 32, P])))
            dve.sem_inc(sel_ready, 1)
            dve.wait_ge(a_exp, 1)
            step(dve.tensor_scalar(A[:], A[:], -1.0, None, ALU.mult))
            dve.sem_inc(a_ready, 1)
            for d in range(2):
                step.restart()
                for k in range(C):
                    step(dve.tensor_scalar(diag[:, k], ident[:], dcol[:, d, k:k + 1], None, ALU.mult))
                dve.sem_inc(diag_ready, 1)
                dve.wait_ge(xc_copied, C * d + C)
                for k in range(C):
                    out = cv[:, k].rearrange("p (b s) -> p b s", b=B)
                    tap = lambda i: xcp[:, k, :, i:i + S]
                    step(dve.tensor_scalar(out, tap(TAPS - 1), cw[:, d, k, TAPS - 1:TAPS], cb[:, d, k:k + 1], ALU.mult, ALU.add))
                    for i in range(TAPS - 1):
                        step(dve.scalar_tensor_tensor(out=out, in0=tap(i), scalar=cw[:, d, k, i:i + 1], in1=out, op0=ALU.mult, op1=ALU.add))
                    dve.sem_inc(cv_ready, 1)
                dve.wait_ge(xd_made, d + 1)
                dve.wait_ge(dtr_ready, d + 1)
                xd = flat(two(0))[0:32]
                step(dve.tensor_copy(bc[0:32], xd))
                step(dve.tensor_tensor(bcr[:], xd, bc[0:32], ALU.subtract))
                step(dve.tensor_copy(bc[32:64], bcr[:]))
                step(dve.tensor_copy(hc[0][0:32, 0, 0:TIME], bc[32:64]))
                step(dve.tensor_tensor(bc[64:96], bcr[:], hc[0][0:32, 0, 0:TIME], ALU.subtract))
                dve.sem_inc(bc_ready, 1)
                for k in range(C):
                    dve.wait_ge(l_ready, C * d + k + 1)
                    step(dve.scalar_tensor_tensor(out=dt[:, k], in0=v[:, k], scalar=0.0, in1=dt[:, k], op0=ALU.max, op1=ALU.add))
                    dve.sem_inc(dt_ready, 1)
                    step(dve.tensor_tensor(du[:, k], dt[:, k], xc[:, k], ALU.mult))
                    dve.sem_inc(du_ready, 1)

                def scans(n, last):
                    for j in range(2):
                        N = d * N_STATE + n + j
                        step.restart()
                        dve.wait_ge(decay_ready, N + 2)
                        step(dve.memset(decay[j][:].rearrange("p k (b s) -> p k b s", b=B)[:, :, :, 0], 0.0))
                        dve.wait_ge(bu_done, N + 3)
                        for k in range(C):
                            dve.tensor_tensor_scan(h[:, k], decay[j][:, k], bu[j][:, k], 0.0, ALU.mult, ALU.add).then_inc(h_done, 1)
                        dve.wait_ge(h_done, C * (N + 1))
                        dve.sem_inc(scanned, 1)
                        dve.wait_ge(c_made, N + 1)
                        dve.wait_ge(summed, N + 1)
                        dve.tensor_tensor(hc[j][:], spreadk(3), h[:], ALU.mult).then_inc(hc_ready, 1)

                each_pair(dve, scans)
                step.restart()
                dve.wait_ge(summed, (d + 1) * N_STATE + 2)
                for k in range(C):
                    for b in range(B):
                        cols = slice(b * S, (b + 1) * S)
                        out = cv[:, k, cols]
                        step(dve.tensor_tensor(out if d == 0 else out[:, ::-1], flat(two(k))[:, cols], sz[:, k, cols], ALU.mult))
                dve.sem_inc(gated, 1)
                dve.wait_ge(out_made, d + 1)
                part = X[:, :, d * P:(d + 1) * P]
                dve.tensor_tensor(part, part, flat(two(2)).rearrange("p (r n) -> p r n", n=P), ALU.add).then_inc(x_added, 1)
                dve.wait_ge(x_added, d + 1)


def routed(nc, a, X, ps, ident, out):
    ctx, sb, sem = scope(nc, "ffn")
    with ctx:
        norm = Norm(sb, sem, [ps[:, 0, :], ps[:, 1, :]])
        sig = sb("sig", [P, C, EX])
        below = sb("below", [P, C, EX])
        w = sb("w", [P, C, EX, E])
        bias = sb("bias", [EX, E])
        count = sb("count", [P, EX])
        lg = sb("lg", [P, ROWS, EX])
        best = sb("best", [P, ROWS, 8])
        idx = sb("idx", [P, ROWS, 8], U32)
        idxf = sb("idxf", [P, ROWS])
        oh = sb("oh", [P, ROWS, EX])
        ohT = sb("ohT", [EX, ROWS, P])
        y = sb("y", [P, E])

        loaded, w_loaded, consts, sign_ready = sem("loaded"), sem("w_loaded"), sem("consts"), sem("sign_ready")
        lg_made, best_found, oh_ready = sem("lg_made"), sem("best_found"), sem("oh_ready")
        oh_turned, ohT_ready, bias_made, bias_used = sem("oh_turned"), sem("ohT_ready"), sem("bias_made"), sem("bias_used")
        y_made, y_used, x_added, stored, dve_step = sem("y_made"), sem("y_used"), sem("x_added"), sem("stored"), sem("dve_step")
        PAIRS = EX // 2
        pairs = lambda p: ps[:, 2 + p, :].rearrange("p (e n) -> p e n", e=2)
        lgp = ps[:, 7, 0:ROWS * EX].rearrange("p (r e) -> p r e", r=ROWS)
        ohp = lambda i: ps[0:EX, 6 + i, :]
        bp = lambda r: ps[:, r % 2, 0:E]
        PER = 512 // P

        block = ctx.enter_context(nc.Block())

        @block.sync
        def _(sp):
            sp.dma_start(sig[:], a["sigT"].rearrange("(c p) n -> p c n", p=P)).then_inc(loaded, 16)
            sp.dma_start(bias[:], a["bias3"]).then_inc(loaded, 16)
            for c in range(C):
                sp.dma_start(w[:, c], a["w3"][:, c * P:(c + 1) * P, :].rearrange("x p n -> p x n")).then_inc(w_loaded, 16)
            for b in range(B):
                sp.wait_ge(x_added, T * b + T)
                sp.dma_start(out[b].rearrange("(t p) d -> p t d", p=P), X[:, b * T:(b + 1) * T, :]).then_inc(stored, 16)
            sp.wait_ge(stored, 16 * B)

        @block.gpsimd
        def _(pool):
            pool.memset(norm.mhalf[:], -0.5).then_inc(consts, 1)
            pool.iota(count[:], pattern=[[1, EX]], base=0, channel_multiplier=0, allow_small_or_imprecise_dtypes=True).then_inc(consts, 1)
            pool.wait_ge(consts, 2)
            norm.gpsimd(pool)

        @block.scalar
        def _(act):
            norm.scalar(act)
            for i in range(ROWS // PER):
                act.wait_ge(oh_turned, i + 1)
                act.copy(ohT[:, i * PER:(i + 1) * PER].rearrange("e r q -> e (r q)"), ohp(i)).then_inc(ohT_ready, 1)

        @block.tensor
        def _(pe):
            norm.tensor(pe, ident)
            pe.wait_ge(sign_ready, 1)
            pe.wait_ge(norm.xnT_ready, B)
            for r in range(ROWS):
                for c in range(C):
                    mm = pe.matmul(lgp[:, r], norm.xnT[:, c, r * P:(r + 1) * P], sig[:, c, :], start=(c == 0), stop=(c == C - 1))
            mm.then_inc(lg_made, 1)
            pe.wait_ge(w_loaded, 32)
            for r in range(ROWS):
                for p in range(PAIRS):
                    if r:
                        pe.wait_ge(y_used, (r - 1) * PAIRS + p + 1)
                    for c in range(C):
                        mm = pe.matmul(ps[:, 2 + p, :], norm.xnT[:, c, r * P:(r + 1) * P], w[:, c, 2 * p:2 * p + 2, :].rearrange("p e n -> p (e n)"),
                                       start=(c == 0), stop=(c == C - 1))
                    mm.then_inc(y_made, 1)
                if r == 0:
                    pe.wait_ge(oh_ready, 1)
                    for i in range(ROWS // PER):
                        for s in range(PER):
                            mm = pe.transpose(ohp(i)[:, s * P:(s + 1) * P], oh[:, i * PER + s], ident[:])
                        mm.then_inc(oh_turned, 1)
                    pe.wait_ge(ohT_ready, ROWS // PER)
                for n in ([0, 1] if r == 0 else [r + 1] if r + 1 < ROWS else []):
                    if n >= 2:
                        pe.wait_ge(bias_used, n - 1)
                    pe.matmul(bp(n), ohT[:, n, :], bias[:], start=True, stop=True).then_inc(bias_made, 1)

        @block.vector
        def _(dve):
            step = Chain(dve, dve_step)
            norm.vector(dve, X)
            dve.wait_ge(loaded, 32)
            dve.wait_ge(consts, 2)
            step(dve.tensor_scalar(below[:], sig[:], 0.0, None, ALU.is_lt))
            step(dve.tensor_scalar(sig[:], sig[:], 0.0, None, ALU.is_gt))
            dve.tensor_tensor(sig[:], sig[:], below[:], ALU.subtract).then_inc(sign_ready, 1)
            dve.wait_ge(lg_made, 1)
            step(dve.tensor_copy(lg[:], lgp))
            argmax_rows(dve, best_found, lg, best, idx, idxf, oh, count)
            dve.sem_inc(oh_ready, 1)
            for r in range(ROWS):
                dve.wait_ge(bias_made, r + 1)
                step(dve.tensor_tensor(y[:], X[:, r], bp(r), ALU.add))
                dve.sem_inc(bias_used, 1)
                for x in range(EX):
                    if x % 2 == 0:
                        dve.wait_ge(y_made, r * PAIRS + x // 2 + 1)
                    ins = dve.scalar_tensor_tensor(out=X[:, r] if x == EX - 1 else y[:], in0=pairs(x // 2)[:, x % 2], scalar=oh[:, r, x:x + 1], in1=y[:],
                                                   op0=ALU.mult, op1=ALU.add)
                    if x == EX - 1:
                        ins.then_inc(x_added, 1)
                        dve.wait_ge(x_added, r + 1)
                    else:
                        step(ins)
                    if x % 2:
                        dve.sem_inc(y_used, 1)


def program(nc, a, out, qscratch):
    with ExitStack() as ctx:
        X = ctx.enter_context(nc.sbuf_tensor("X", [P, ROWS, E], F32))
        ident = ctx.enter_context(nc.sbuf_tensor("ident", [P, P], F32))
        identb = ctx.enter_context(nc.sbuf_tensor("identb", [P, P], BF16))
        W2 = ctx.enter_context(nc.sbuf_tensor("W2", [P, C, E], F32))
        qmax = ctx.enter_context(nc.sbuf_tensor("qmax", [P, 2 * C], F32))
        ps = ctx.enter_context(nc.psum_tensor("ps", [P, 8, 512], F32))
        prepare(nc, a, X, ps, ident, identb, W2, qmax, qscratch)
        cross_attention(nc, a, X, ps, ident, identb, W2, qmax, qscratch)
        self_attention(nc, a, X, ps, ident)
        experts(nc, a, X, ps, ident)
        context_attention(nc, a, X, ps, ident)
        state_space(nc, a, X, ps, ident)
        routed(nc, a, X, ps, ident, out)


def both(i, name):
    import numpy as np
    return [np.asarray(i[f"L1_attn_{d}_{name}"]) for d in ("fwd", "bwd")]


def layouts(i):
    import numpy as np
    c = lambda v: np.ascontiguousarray(v)
    ctx = np.asarray(i["ctx_1024"])
    return {
        "x": c(i["x"]),
        "mask": c(np.asarray(i["mask_Bx1xSxS2_if1"]).reshape(B, S, SK)),
        "ctxT": c(ctx.transpose(0, 2, 1).reshape(B * C, P, SK)),
        "ctxV": c(ctx.reshape(B, KT, P, H // HG, HG * D).transpose(0, 3, 2, 1, 4).reshape(B * H // HG, P, KT * HG * D)),
        "wq0": c(i["L0_xattn_Wq"]), "wk0": c(i["L0_xattn_Wk"]), "wv0": c(i["L0_xattn_Wv"]),
        "wo0T": c(np.asarray(i["L0_xattn_Wo"]).T), "bo0": c(i["L0_xattn_bo"]),
        "wq1T": c(np.asarray(i["L0_attn_Wq"]).T), "wk1T": c(np.asarray(i["L0_attn_Wk"]).T),
        "wv1T": c(np.asarray(i["L0_attn_Wv"]).T), "wo1T": c(np.asarray(i["L0_attn_Wo"]).T),
        "bq1": c(np.asarray(i["L0_attn_bq"]).reshape(H // HG, HG, D).transpose(1, 2, 0)),
        "bk1": c(np.asarray(i["L0_attn_bk"]).reshape(H // HG, HG, D).transpose(1, 2, 0)),
        "wg": c(i["L0_ffn_Wg"]), "we": c(i["L0_ffn_We"]), "be": c(i["L0_ffn_be"]), "ctx": c(ctx),
        "wq2": c(i["L1_xattn_w_q"]), "wk2": c(i["L1_xattn_w_k"]), "wv2T": c(np.asarray(i["L1_xattn_w_v"]).T),
        "nw": c(i["L1_attn_norm_w"]), "nb": c(i["L1_attn_norm_b"]),
        "win": c(np.stack([w.T for w in both(i, "in_proj_w")], 1)),
        "cw": c(np.stack([w.reshape(C, P, TAPS).transpose(1, 0, 2) for w in both(i, "conv_w")], 1)),
        "wx": c(np.stack([np.concatenate([w[RANK:], w[:RANK]]).T.reshape(C, P, -1).transpose(1, 0, 2) for w in both(i, "x_proj_w")], 1)),
        "wdt": c(np.stack([w.T for w in both(i, "dt_proj_w")], 1)),
        "cb": c(np.stack([w.reshape(C, P).T for w in both(i, "conv_b")], 1)),
        "bdt": c(np.stack([w.reshape(C, P).T for w in both(i, "dt_proj_b")], 1)),
        "dcol": c(np.stack([w.reshape(C, P).T for w in both(i, "D")], 1)),
        "alog": c(np.stack([w.reshape(C, P, N_STATE).transpose(1, 0, 2) for w in both(i, "A_log")], 1)),
        "wout": c(np.stack([w.T.reshape(C, P, P).transpose(1, 0, 2) for w in both(i, "out_proj_w")], 1)),
        "sigT": c(np.asarray(i["L1_ffn_tile_sigs"]).T), "w3": c(i["L1_ffn_W"]), "bias3": c(i["L1_ffn_b"]),
        "bv1": c(i["L0_attn_bv"]), "bo1": c(i["L0_attn_bo"]),
    }


def kernel(**inputs):
    import concourse.bacc as bacc
    from concourse.bass_utils import run_bass_kernel_spmd

    nc = bacc.Bacc("TRN2", target_bir_lowering=False, num_devices=1)
    arrays = layouts(inputs)
    a = {n: nc.dram_tensor(n, v.shape, mybir.dt.from_np(v.dtype), kind="ExternalInput").ap() for n, v in arrays.items()}
    out = nc.dram_tensor("out", (B, S, E), F32, kind="ExternalOutput").ap()
    qscratch = nc.dram_tensor("qscratch", (NB, B, C, P, S), BF16, kind="Internal").ap()
    program(nc, a, out, qscratch)
    r = run_bass_kernel_spmd(nc, [arrays], core_ids=[0])
    return r.results[0]["out"]
```
